# Optimizing a Trainium2 kernel written in Bass

```python
import numpy as np
import jax
import jax.numpy as jnp

def _softmax(x, axis=-1):
    return jax.nn.softmax(x, axis=axis)

def _gelu(x):
    return jax.nn.gelu(x, approximate=True)

def _silu(x):
    return jax.nn.silu(x)

def _sigmoid(x):
    return jax.nn.sigmoid(x)

def _layernorm(x, axis=-1, eps=1e-05):
    m = jnp.mean(x, axis=axis, keepdims=True)
    v = jnp.var(x, axis=axis, keepdims=True)
    return (x - m) / jnp.sqrt(v + eps)

def _scatter_add(tgt, idx, src, axis=0):
    return tgt.at[idx].add(src)

def _segment_sum(src, seg, n):
    return jax.ops.segment_sum(src, seg, n)
kernel_name = 'mk_gnn_ffn_d2_gnn_r32_cdf800'

def setup_inputs(seed: int=0):
    np.random.seed(seed)
    _w = jnp.asarray

    def _rec_inputs():
        import jax
        import jax.numpy as jnp
        _gk = jax.random.key(seed)
        x = -8.776e-05 + 1 * jax.random.normal(jax.random.fold_in(_gk, 1), (3125, 256), jnp.float32)
        src = jax.random.randint(jax.random.fold_in(_gk, 2), (50000,), 0, 3125, jnp.int32)
        dst = jax.random.randint(jax.random.fold_in(_gk, 3), (50000,), 0, 3125, jnp.int32)
        _o = jnp.argsort(dst, stable=True)
        src = src[_o]
        dst = dst[_o]
        edge_type_16 = jax.random.randint(jax.random.fold_in(_gk, 12), (50000,), 0, 16, jnp.int32)
        edge_type_8 = jax.random.randint(jax.random.fold_in(_gk, 13), (50000,), 0, 8, jnp.int32)
        return (x, src, dst, edge_type_16, edge_type_8)
    x, src, dst, edge_type_16, edge_type_8 = _rec_inputs()

    def _L0_gnn_setup():
        import jax, jax.numpy as jnp
        import numpy as np
        N_NODES = 625
        N_EDGES = 10000
        IN_DIM = 256
        OUT_DIM = 256
        NUM_RELS = 8
        NUM_BASES = 4
        key = jax.random.key(seed)
        k = jax.random.split(key, 7)
        return {'h': jax.random.normal(k[0], (N_NODES, IN_DIM), dtype=jnp.float32), 'basis': jax.random.normal(k[1], (NUM_BASES, IN_DIM, OUT_DIM), dtype=jnp.float32) * (6.0 / (IN_DIM + OUT_DIM)) ** 0.5, 'w_comp': jax.random.normal(k[2], (NUM_RELS, NUM_BASES), dtype=jnp.float32), 'bias': jax.random.normal(k[3], (OUT_DIM,), dtype=jnp.float32) * 0.01, 'src': jax.random.randint(k[4], (N_EDGES,), 0, N_NODES, dtype=jnp.int32), 'dst': jax.random.randint(k[5], (N_EDGES,), 0, N_NODES, dtype=jnp.int32), 'etype': jax.random.randint(k[6], (N_EDGES,), 0, NUM_RELS, dtype=jnp.int32)}
    _L0_gnn_all = _L0_gnn_setup()
    _L0_gnn_in = {k: v for k, v in _L0_gnn_all.items() if k in ('basis', 'w_comp', 'bias')}
    del _L0_gnn_all

    def _L0_ffn_setup():
        import jax, jax.numpy as jnp
        import numpy as np
        B, A = (128, 8)
        IN, OUT = (256, 256)
        SH1, SH2 = (256, 128)
        EH1, EH2 = (128, 64)
        E, TOPK = (4, 2)

        def _shared_mlp(x, W1, b1, W2, b2, W3, b3):
            h = jax.nn.relu(x @ W1 + b1)
            h = jax.nn.relu(h @ W2 + b2)
            return h @ W3 + b3

        def _experts_mlp(x, eW1, eb1, eW2, eb2, eW3, eb3):
            h = jax.nn.relu(jnp.einsum('baf,efh->ebah', x, eW1) + eb1[:, None, None, :])
            h = jax.nn.relu(jnp.einsum('ebah,ehg->ebag', h, eW2) + eb2[:, None, None, :])
            o = jnp.einsum('ebag,ego->ebao', h, eW3) + eb3[:, None, None, :]
            return jnp.moveaxis(o, 0, -1)
        key = jax.random.key(seed)
        ks = jax.random.split(key, 16)
        s = 0.05
        return {'x': jax.random.normal(ks[0], (B, A, IN), jnp.float32), 'sW1': jax.random.normal(ks[1], (IN, SH1), jnp.float32) * s, 'sb1': jnp.zeros((SH1,), jnp.float32), 'sW2': jax.random.normal(ks[2], (SH1, SH2), jnp.float32) * s, 'sb2': jnp.zeros((SH2,), jnp.float32), 'sW3': jax.random.normal(ks[3], (SH2, OUT), jnp.float32) * s, 'sb3': jnp.zeros((OUT,), jnp.float32), 'eW1': jax.random.normal(ks[4], (E, IN, EH1), jnp.float32) * s, 'eb1': jnp.zeros((E, EH1), jnp.float32), 'eW2': jax.random.normal(ks[5], (E, EH1, EH2), jnp.float32) * s, 'eb2': jnp.zeros((E, EH2), jnp.float32), 'eW3': jax.random.normal(ks[6], (E, EH2, OUT), jnp.float32) * s, 'eb3': jnp.zeros((E, OUT), jnp.float32), 'gW': jax.random.normal(ks[7], (IN, E), jnp.float32) * s, 'gb': jnp.zeros((E,), jnp.float32)}
    _L0_ffn_all = _L0_ffn_setup()
    _L0_ffn_in = {k: v for k, v in _L0_ffn_all.items() if k in ('sW1', 'sb1', 'sW2', 'sb2', 'sW3', 'sb3', 'eW1', 'eb1', 'eW2', 'eb2', 'eW3', 'eb3', 'gW', 'gb')}
    del _L0_ffn_all

    def _L1_gnn_setup():
        import jax, jax.numpy as jnp
        import numpy as np
        N_NODES = 50000
        N_EDGES = 25000
        HDIM = 256
        NUMRELS = 16

        def _gru_cell(x, h, w_ih, w_hh, b_ih, b_hh):
            gi = x @ w_ih.T + b_ih
            gh = h @ w_hh.T + b_hh
            i_r, i_z, i_n = jnp.split(gi, 3, axis=-1)
            h_r, h_z, h_n = jnp.split(gh, 3, axis=-1)
            r = jax.nn.sigmoid(i_r + h_r)
            z = jax.nn.sigmoid(i_z + h_z)
            n = jnp.tanh(i_n + r * h_n)
            return (1.0 - z) * n + z * h
        key = jax.random.key(seed)
        ks = jax.random.split(key, 9)
        h = jax.random.normal(ks[0], (N_NODES, HDIM), dtype=jnp.float32)
        relvectors = jax.random.normal(ks[1], (NUMRELS, HDIM), dtype=jnp.float32)
        s = 1.0 / np.sqrt(HDIM)
        w_ih = jax.random.uniform(ks[2], (3 * HDIM, HDIM), minval=-s, maxval=s, dtype=jnp.float32)
        w_hh = jax.random.uniform(ks[3], (3 * HDIM, HDIM), minval=-s, maxval=s, dtype=jnp.float32)
        b_ih = jax.random.uniform(ks[4], (3 * HDIM,), minval=-s, maxval=s, dtype=jnp.float32)
        b_hh = jax.random.uniform(ks[5], (3 * HDIM,), minval=-s, maxval=s, dtype=jnp.float32)
        edge_src = jax.random.randint(ks[6], (N_EDGES,), 0, N_NODES, dtype=jnp.int32)
        edge_dst = jax.random.randint(ks[7], (N_EDGES,), 0, N_NODES, dtype=jnp.int32)
        edge_rel = jax.random.randint(ks[8], (N_EDGES,), 0, NUMRELS, dtype=jnp.int32)
        return {'h': h, 'relvectors': relvectors, 'w_ih': w_ih, 'w_hh': w_hh, 'b_ih': b_ih, 'b_hh': b_hh, 'edge_src': edge_src, 'edge_dst': edge_dst, 'edge_rel': edge_rel}
    _L1_gnn_all = _L1_gnn_setup()
    _L1_gnn_in = {k: v for k, v in _L1_gnn_all.items() if k in ('relvectors', 'w_ih', 'w_hh', 'b_ih', 'b_hh')}
    del _L1_gnn_all

    def _L1_ffn_setup():
        import jax, jax.numpy as jnp
        import numpy as np
        C = 256
        HID = 1024
        E = 8
        TEMP = 1.0
        key = jax.random.key(seed)
        ks = jax.random.split(key, 7)
        x = jax.random.normal(ks[0], (8, 512, C), dtype=jnp.float32)
        W1 = jax.random.normal(ks[1], (C, HID), dtype=jnp.float32) * 0.02
        b1 = jnp.zeros((HID,), dtype=jnp.float32)
        Wg = jax.random.normal(ks[2], (HID, E), dtype=jnp.float32) * 0.02
        bg = jnp.zeros((E,), dtype=jnp.float32)
        Wd = jax.random.normal(ks[3], (E, HID, C), dtype=jnp.float32) * 0.02
        bd = jnp.zeros((E, C), dtype=jnp.float32)
        return {'x': x, 'W1': W1, 'b1': b1, 'Wg': Wg, 'bg': bg, 'Wd': Wd, 'bd': bd}
    _L1_ffn_all = _L1_ffn_setup()
    _L1_ffn_in = {k: v for k, v in _L1_ffn_all.items() if k in ('W1', 'b1', 'Wg', 'bg', 'Wd', 'bd')}
    del _L1_ffn_all
    return {'x': x, 'src': src, 'dst': dst, 'edge_type_16': edge_type_16, 'edge_type_8': edge_type_8, 'L0_gnn_basis': _L0_gnn_in['basis'], 'L0_gnn_w_comp': _L0_gnn_in['w_comp'], 'L0_gnn_bias': _L0_gnn_in['bias'], 'L0_ffn_sW1': _L0_ffn_in['sW1'], 'L0_ffn_sb1': _L0_ffn_in['sb1'], 'L0_ffn_sW2': _L0_ffn_in['sW2'], 'L0_ffn_sb2': _L0_ffn_in['sb2'], 'L0_ffn_sW3': _L0_ffn_in['sW3'], 'L0_ffn_sb3': _L0_ffn_in['sb3'], 'L0_ffn_eW1': _L0_ffn_in['eW1'], 'L0_ffn_eb1': _L0_ffn_in['eb1'], 'L0_ffn_eW2': _L0_ffn_in['eW2'], 'L0_ffn_eb2': _L0_ffn_in['eb2'], 'L0_ffn_eW3': _L0_ffn_in['eW3'], 'L0_ffn_eb3': _L0_ffn_in['eb3'], 'L0_ffn_gW': _L0_ffn_in['gW'], 'L0_ffn_gb': _L0_ffn_in['gb'], 'L1_gnn_relvectors': _L1_gnn_in['relvectors'], 'L1_gnn_w_ih': _L1_gnn_in['w_ih'], 'L1_gnn_w_hh': _L1_gnn_in['w_hh'], 'L1_gnn_b_ih': _L1_gnn_in['b_ih'], 'L1_gnn_b_hh': _L1_gnn_in['b_hh'], 'L1_ffn_W1': _L1_ffn_in['W1'], 'L1_ffn_b1': _L1_ffn_in['b1'], 'L1_ffn_Wg': _L1_ffn_in['Wg'], 'L1_ffn_bg': _L1_ffn_in['bg'], 'L1_ffn_Wd': _L1_ffn_in['Wd'], 'L1_ffn_bd': _L1_ffn_in['bd']}

def reference(x, src, dst, edge_type_16, edge_type_8, L0_gnn_basis, L0_gnn_w_comp, L0_gnn_bias, L0_ffn_sW1, L0_ffn_sb1, L0_ffn_sW2, L0_ffn_sb2, L0_ffn_sW3, L0_ffn_sb3, L0_ffn_eW1, L0_ffn_eb1, L0_ffn_eW2, L0_ffn_eb2, L0_ffn_eW3, L0_ffn_eb3, L0_ffn_gW, L0_ffn_gb, L1_gnn_relvectors, L1_gnn_w_ih, L1_gnn_w_hh, L1_gnn_b_ih, L1_gnn_b_hh, L1_ffn_W1, L1_ffn_b1, L1_ffn_Wg, L1_ffn_bg, L1_ffn_Wd, L1_ffn_bd):
    import jax
    import jax.numpy as jnp

    def _L0_gnn_ref(h, basis, w_comp, bias, src, dst, etype):
        import jax, jax.numpy as jnp
        import numpy as np
        N_NODES = 625
        N_EDGES = 10000
        IN_DIM = 256
        OUT_DIM = 256
        NUM_RELS = 8
        NUM_BASES = 4
        in_dim, out_dim = (h.shape[1], basis.shape[2])
        num_rels = w_comp.shape[0]
        wr = basis.reshape(in_dim, NUM_BASES, out_dim)
        weight = jnp.einsum('rb,ibo->iro', w_comp, wr)
        weight = weight.reshape(num_rels, in_dim, out_dim)
        t = jnp.einsum('nd,rdo->rno', h, weight)
        msg = t[etype, src]
        agg = jax.ops.segment_sum(msg, dst, num_segments=h.shape[0])
        return jax.nn.relu(agg + bias)

    def _L0_ffn_ref(x, sW1, sb1, sW2, sb2, sW3, sb3, eW1, eb1, eW2, eb2, eW3, eb3, gW, gb):
        import jax, jax.numpy as jnp
        import numpy as np
        B, A = (128, 8)
        IN, OUT = (256, 256)
        SH1, SH2 = (256, 128)
        EH1, EH2 = (128, 64)
        E, TOPK = (4, 2)

        def _shared_mlp(x, W1, b1, W2, b2, W3, b3):
            h = jax.nn.relu(x @ W1 + b1)
            h = jax.nn.relu(h @ W2 + b2)
            return h @ W3 + b3

        def _experts_mlp(x, eW1, eb1, eW2, eb2, eW3, eb3):
            h = jax.nn.relu(jnp.einsum('baf,efh->ebah', x, eW1) + eb1[:, None, None, :])
            h = jax.nn.relu(jnp.einsum('ebah,ehg->ebag', h, eW2) + eb2[:, None, None, :])
            o = jnp.einsum('ebag,ego->ebao', h, eW3) + eb3[:, None, None, :]
            return jnp.moveaxis(o, 0, -1)
        all_out = _experts_mlp(x, eW1, eb1, eW2, eb2, eW3, eb3)
        shared = _shared_mlp(x, sW1, sb1, sW2, sb2, sW3, sb3)
        gates = jax.nn.softmax(x @ gW + gb, axis=-1)
        topv, topi = jax.lax.top_k(gates, TOPK)
        topw = jax.nn.softmax(topv, axis=-1)
        sel = jnp.take_along_axis(all_out, topi[:, :, None, :], axis=-1)
        gated = jnp.sum(sel * topw[:, :, None, :], axis=-1)
        return shared + gated

    def _L1_gnn_ref(h, relvectors, w_ih, w_hh, b_ih, b_hh, edge_src, edge_dst, edge_rel):
        import jax, jax.numpy as jnp
        import numpy as np
        N_NODES = 50000
        N_EDGES = 25000
        HDIM = 256
        NUMRELS = 16

        def _gru_cell(x, h, w_ih, w_hh, b_ih, b_hh):
            gi = x @ w_ih.T + b_ih
            gh = h @ w_hh.T + b_hh
            i_r, i_z, i_n = jnp.split(gi, 3, axis=-1)
            h_r, h_z, h_n = jnp.split(gh, 3, axis=-1)
            r = jax.nn.sigmoid(i_r + h_r)
            z = jax.nn.sigmoid(i_z + h_z)
            n = jnp.tanh(i_n + r * h_n)
            return (1.0 - z) * n + z * h
        msg = h[edge_src] + relvectors[edge_rel]
        red = jax.ops.segment_sum(msg, edge_dst, num_segments=h.shape[0])
        return _gru_cell(red, h, w_ih, w_hh, b_ih, b_hh)

    def _L1_ffn_ref(x, W1, b1, Wg, bg, Wd, bd):
        import jax, jax.numpy as jnp
        import numpy as np
        C = 256
        HID = 1024
        E = 8
        TEMP = 1.0
        orig_shape = x.shape
        xf = x.reshape(-1, orig_shape[-1])
        H = jax.nn.gelu(xf @ W1 + b1, approximate=False)
        probs = jax.nn.softmax((H @ Wg + bg) / TEMP, axis=-1)
        assign = jnp.argmax(probs, axis=-1)
        out = jnp.zeros_like(xf)
        for e in range(Wd.shape[0]):
            y = H @ Wd[e] + bd[e]
            sel = (assign == e)[:, None]
            out = out + jnp.where(sel, probs[:, e:e + 1] * y, 0.0)
        return out.reshape(orig_shape)
    x = x + _L0_gnn_ref(_layernorm(x, axis=-1), L0_gnn_basis, L0_gnn_w_comp, L0_gnn_bias, src, dst, edge_type_8)
    x = x + _L0_ffn_ref(_layernorm(x, axis=-1)[None], L0_ffn_sW1, L0_ffn_sb1, L0_ffn_sW2, L0_ffn_sb2, L0_ffn_sW3, L0_ffn_sb3, L0_ffn_eW1, L0_ffn_eb1, L0_ffn_eW2, L0_ffn_eb2, L0_ffn_eW3, L0_ffn_eb3, L0_ffn_gW, L0_ffn_gb)[0]
    x = x + _L1_gnn_ref(_layernorm(x, axis=-1), L1_gnn_relvectors, L1_gnn_w_ih, L1_gnn_w_hh, L1_gnn_b_ih, L1_gnn_b_hh, src, dst, edge_type_16)
    x = x + _L1_ffn_ref(_layernorm(x, axis=-1)[None], L1_ffn_W1, L1_ffn_b1, L1_ffn_Wg, L1_ffn_bg, L1_ffn_Wd, L1_ffn_bd)[0]
    return x

_drawn_inputs = setup_inputs


def setup_inputs(seed=0):
    import zlib

    import numpy as np

    out = dict(_drawn_inputs(seed))
    spreads = {'L0_ffn_sb1': (0.0, 0.8),
     'L0_ffn_sb2': (0.0, 0.8),
     'L0_ffn_sb3': (0.0, 0.764),
     'L0_ffn_eb1': (0.0, 0.8),
     'L0_ffn_eb2': (0.0, 0.8),
     'L0_ffn_eb3': (0.0, 2.0),
     'L0_ffn_gb': (0.0, 0.8),
     'L1_ffn_b1': (0.0, 0.8),
     'L1_ffn_bg': (0.0, 0.8),
     'L1_ffn_bd': (0.0, 2.0)}
    factors = {'L0_gnn_bias': 8.0,
     'L0_ffn_sW1': 4.273,
     'L0_ffn_sW2': 3.832,
     'L0_ffn_sW3': 3.068,
     'L0_ffn_eW1': 8.0,
     'L0_ffn_eW2': 8.0,
     'L0_ffn_eW3': 8.0,
     'L0_ffn_gW': 8.0,
     'L1_gnn_w_hh': 13.86,
     'L1_gnn_b_ih': 200.0,
     'L1_gnn_b_hh': 200.0,
     'L1_ffn_W1': 8.0,
     'L1_ffn_Wg': 8.0,
     'L1_ffn_Wd': 8.0,
     'L1_gnn_relvectors': 2.736}
    for name, (base, spread) in spreads.items():
        noise = np.random.default_rng([zlib.crc32(name.encode()), seed]).standard_normal(out[name].shape)
        drawn = base * np.exp(spread * noise) if base else spread * noise
        out[name] = jnp.asarray(drawn.astype(out[name].dtype))
    for name, factor in factors.items():
        out[name] = (out[name] * factor).astype(out[name].dtype)
    return out
```

```python
from contextlib import ExitStack

import concourse.bass as bass
from concourse import mybir

F32 = mybir.dt.float32
I32 = mybir.dt.int32
U32 = mybir.dt.uint32
ALU = mybir.AluOpType
ACT = mybir.ActivationFunctionType
AX = mybir.AxisListType

P = 128
N, D, E = 3125, 256, 50000
NB = -(-N // P)
NTAIL = N - (NB - 1) * P
NP = NB * P
GB = 5
NG = NB // GB
GN = GB * P
HALF = GN // 2
ET = -(-E // P)
ETAIL = E - (ET - 1) * P
UNR = 17
NIT = ET // UNR
CUT = 8
PARTS = ((0, CUT), (CUT, UNR))
BANKS = ((0, 2), (2, 4), (4, 6), (6, 8), (8, 10), (10, 12), (12, 14), (14, UNR))
WIN = 16
NWIN = -(-N // WIN)
ACCW = NP + WIN
NONE = 1.0e6
R8, R16, NBASE = 8, 16, 4
NE0, NE1 = 4, 8
HID = 1024
MH = HID // P
TILES = (N + NE1 * (P - 1)) // P
SLOTS = TILES * P
EPS = 1e-5
assert UNR * NIT == ET and GB * NG == NB and TILES % 8 == 0


class Level:

    def __init__(self, eng, name, start=0):
        self.eng, self.reg = eng, eng.alloc_register(name)
        eng.reg_mov(self.reg, start)

    def up(self, n=1):
        self.eng.reg_add(self.reg, self.reg, n)
        return self.reg


def one(b):
    return bass.ds(b, 1)


def allocate(nc, ctx):
    def sb(name, shape, dt=F32):
        return ctx.enter_context(nc.sbuf_tensor(name, shape, dt))

    class M:
        pass

    m = M()
    m.x = sb("x", [P, NB, D])
    m.hT = sb("hT", [P, 2, NP])
    m.h = sb("h", [P, NB, D])
    m.region = sb("region", [P, R8 * ACCW])
    m.hn = sb("hn", [P, GB, D])
    m.tT = sb("tT", [P, GB, 2, P])
    m.ident = sb("ident", [P, P])
    m.iota = sb("iota", [P, P])
    m.ones = sb("ones", [P, P])
    m.mv = sb("mv", [P, NB, 2])
    m.stats = sb("stats", [P, NB, 6])
    m.std = sb("std", [P, NB])
    m.rstd = sb("rstd", [P, NB])
    m.src = sb("src", [P, ET], I32)
    m.src_now = sb("src_now", [P, UNR], I32)
    m.dst0 = sb("dst0", [P, ET])
    m.dst = sb("dst", [P, ET])
    m.type8 = sb("type8", [P, ET])
    m.type16 = sb("type16", [P, ET])
    m.base0 = sb("base0", [P, ET])
    m.base = sb("base", [P, ET])
    m.base_row = sb("base_row", [1, ET], I32)
    m.key = sb("key", [P, ET])
    m.valid = sb("valid", [P, ET])
    m.wincol = sb("wincol", [P, 1])
    m.hrow = sb("hrow", [P, D])[:, :]
    m.rounds = sb("rounds", [1, 1], I32)
    m.ps = ctx.enter_context(nc.psum_tensor("ps", [P, 8, 512], F32))

    def carve(whole, start, *shape):
        n = 1
        for s in shape:
            n *= s
        v = whole[:, start:start + n]
        names = "abcd"[:len(shape)]
        if len(shape) > 1:
            v = v.rearrange("p (" + " ".join(names) + ") -> p " + " ".join(names), **dict(zip(names, shape)))
        return v, start + n

    hflat = m.h[:, :, :].rearrange("p b d -> p (b d)")
    reg = m.region[:, :]
    m.acc0, _ = carve(reg, 0, R8, ACCW)
    m.ring0, at = carve(hflat, 0, UNR, P)
    m.hot0, at = carve(hflat, at, UNR, P)
    m.sring, _ = carve(hflat, 0, GB, R8, P)
    m.gbuf = m.h[:, :, 0:P]
    m.basis, _ = carve(m.hT[:, :, :].rearrange("p a n -> p (a n)"), 0, R8, D)
    m.sW1, at = carve(reg, 0, 2, 256)
    m.sW2, at = carve(reg, at, 2, 128)
    m.sW3, at = carve(reg, at, 256)
    m.eW1, at = carve(reg, at, NE0, 2, 128)
    m.eW2, at = carve(reg, at, NE0, 64)
    m.eW3, at = carve(reg, at, 2, 256)
    m.gW, at = carve(reg, at, 2, NE0)
    m.gb, at = carve(reg, at, NE0)
    m.b1, at = carve(reg, at, 6)
    m.b2, at = carve(reg, at, 3)
    m.b3, at = carve(reg, at, 256)
    m.logit0, at = carve(reg, at, NB, NE0)
    m.gate0, at = carve(reg, at, 12, NB * NE0)
    m.w0, at = carve(reg, at, NB, NE0)
    m.wst, at = carve(reg, at, GB, NE0)
    m.wT, at = carve(reg, at, GN)
    m.sel, at = carve(reg, at, 2, P)
    m.a1, at = carve(reg, at, 6, GN)
    m.a2, at = carve(reg, at, 3, GN)
    m.bias0, at = carve(reg, at, 256)
    assert at <= R8 * ACCW
    m.acc1, at = carve(reg, 0, 3, ACCW)
    m.ring1, at = carve(reg, at, UNR, D)
    m.hot_type, at = carve(reg, at, UNR, P)
    m.hot1, at = carve(reg, at, UNR, WIN)
    m.wih, at = carve(reg, at, 2, 768)
    m.whh, at = carve(reg, at, 2, 768)
    m.rel, at = carve(reg, at, D)
    m.bih, at = carve(reg, at, 6)
    m.bhh, at = carve(reg, at, 6)
    m.brz, at = carve(reg, at, 4)
    assert at <= R8 * ACCW
    m.gr, at2 = carve(reg, 3 * ACCW, 2, GN)
    m.gz, at2 = carve(reg, at2, 2, GN)
    m.gn, at2 = carve(reg, at2, 2, GN)
    m.gt, at2 = carve(reg, at2, 2, GN)
    assert at2 <= 3 * ACCW + UNR * (D + P)
    m.Wd, at = carve(reg, 0, NE1, MH, D)
    m.W1, at = carve(reg, at, 2, HID)
    m.Wg, at = carve(reg, at, MH, NE1)
    m.bg, at = carve(reg, at, NE1)
    m.bf1, at = carve(reg, at, MH)
    m.bd, at = carve(reg, at, NE1, D)
    assert at <= R8 * ACCW
    m.H0, end = carve(reg, at, MH, GN)
    assert end <= R8 * ACCW
    m.HQ = [carve(reg, at, MH, 4 * P)[0], carve(m.hT[:, :, :].rearrange("p a n -> p (a n)"), 0, MH, 4 * P)[0]]
    m.hTQ = carve(m.hT[:, :, :].rearrange("p a n -> p (a n)"), MH * 4 * P, 2, 4 * P)[0]
    m.slots = [carve(hflat, i * 4 * D, 4, D)[0] for i in range(2)]
    m.results = [carve(hflat, (2 + i) * 4 * D, 4, D)[0] for i in range(2)]
    small = m.hn[:, :, :].rearrange("p b d -> p (b d)")
    m.logit1, at = carve(small, 0, NB, NE1)
    m.prob1, at = carve(small, at, NB, NE1)
    m.pick, at = carve(small, at, NB, NE1)
    m.before, at = carve(small, at, NB, NE1)
    m.cum, at = carve(small, at, NE1, NB)
    m.tmp1, at = carve(small, at, NB, NE1)
    small = m.tT[:, :, :, :].rearrange("p b c d -> p (b c d)")
    m.tri, at = carve(small, 0, P)
    m.tmp2, at = carve(small, at, TILES, NE1)
    m.tot, at = carve(small, at, NE1, NB)
    m.best, at = carve(small, at, NB)
    m.col1, at = carve(small, at, NB)
    m.posf, at = carve(small, at, NB)
    m.slot_of, at = carve(small, at, NB)
    m.slot_of = m.slot_of.bitcast(I32)
    m.steps, at = carve(small, at, NB)
    m.ntiles, at = carve(small, at, NE1)
    m.ends, at = carve(small, at, NE1)
    m.starts, at = carve(small, at, NE1)
    m.padmask, at = carve(small, at, NE1)
    m.ofTf, at = carve(small, at, TILES)
    m.ofT, at = carve(small, at, TILES)
    m.ofT = m.ofT.bitcast(I32)
    assert at <= GB * 2 * P
    return m


def prepare(nc, ctx, m, io):
    def sem(name):
        return ctx.enter_context(nc.semaphore(name))

    in_x, in_src, in_edges, in_dstrow, in_comp = (sem("in_" + s) for s in ("x", "src", "edges", "dstrow", "comp"))
    pads, zeroed, z_out, pool_step, v_step, bc_ready, fl_ready = (
        sem(s) for s in ("pads", "zeroed", "z_out", "pool_step", "v_step", "bc_ready", "fl_ready"))
    hflat = m.h[:, :, :].rearrange("p b d -> p (b d)")
    hTflat = m.hT[:, :, :].rearrange("p a n -> p (a n)")
    stage = hflat[:, 0:4 * ET].rearrange("p (a t) -> p a t", a=4).bitcast(I32)
    rows = hTflat[:, 0:4 * P].rearrange("p (c e) -> p c e", c=4).bitcast(I32)
    rows_f = hTflat[:, 512:1024].rearrange("p (c e) -> p c e", c=4)
    lows = hTflat[:, 1024:1028]
    diag = hTflat[:, 1100:1612].rearrange("p (c t) -> p c t", c=4)
    over = hTflat[:, 1700:1701]
    over_t = hTflat[:, 1800:1800 + ET]
    flag = hTflat[0:1, 2300:2301]
    flagr = hTflat[0:1, 2302:2303]
    m.comp_rep = hTflat[:, 2400:2404]
    FULL = (ET - 1) // P
    REST = ET - 1 - FULL * P
    with nc.Block() as block:
        @block.sync
        def _(sp):
            sp.wait_ge(pads, 3)
            sp.dma_start(stage[:, 0, 0:ET - 1], io["dst_main"]).then_inc(in_edges, 16)
            sp.dma_start(rows[:, 0:FULL, :], io["dst"][0:FULL * P * P].rearrange("(c p e) -> p c e", c=FULL, p=P)
                         ).then_inc(in_dstrow, 16)
            sp.dma_start(rows[0:REST, FULL, :], io["dst"][FULL * P * P:(ET - 1) * P].rearrange("(p e) -> p e", e=P)
                         ).then_inc(in_dstrow, 16)
            sp.dma_start(rows[REST:REST + 1, FULL, 0:ETAIL],
                         io["dst"][(ET - 1) * P:E].rearrange("(p e) -> p e", p=1)).then_inc(in_dstrow, 16)
            for k, name in ((0, "dst"), (1, "t8"), (2, "t16")):
                sp.dma_start(stage[0:ETAIL, k, ET - 1:ET], io[name][(ET - 1) * P:E].rearrange("(p e) -> p e", e=1)
                             ).then_inc(in_edges, 16)
            sp.dma_start(m.src[0:ETAIL, ET - 1:ET], io["src"][(ET - 1) * P:E].rearrange("(p e) -> p e", e=1)
                         ).then_inc(in_edges, 16)
            sp.dma_start(stage[:, 1, 0:ET - 1], io["t8_main"]).then_inc(in_edges, 16)
            sp.dma_start(stage[:, 2, 0:ET - 1], io["t16_main"]).then_inc(in_edges, 16)
            sp.dma_start(m.src[:, 0:ET - 1], io["src_main"]).then_inc(in_src, 16)
            sp.wait_ge(zeroed, 1)
            sp.dma_start(io["slots_in"].rearrange("(p r) c -> p (r c)", p=P), m.region[:, 0:TILES * D]
                         ).then_inc(z_out, 16)
            sp.wait_ge(z_out, 16)
            sp.wait_ge(in_x, 32)
            sp.wait_ge(in_src, 16)

        @block.scalar
        def _(act):
            act.wait_ge(pads, 4)
            act.dma_start(m.x[:, 0:NB - 1, :], io["x"][0:(NB - 1) * P, :].rearrange("(b p) d -> p b d", p=P)
                          ).then_inc(in_x, 16)
            act.dma_start(m.x[0:NTAIL, NB - 1, :], io["x"][(NB - 1) * P:N, :]).then_inc(in_x, 16)
            act.dma_start(m.comp_rep, io["w_comp"].rearrange("(o r) b -> o r b", o=1).broadcast_to(
                [P // R8, R8, NBASE])).then_inc(in_comp, 16)

        @block.gpsimd
        def _(g):
            g.memset(stage[:, 0:3, ET - 1:ET], int(NONE)).then_inc(pads, 1)
            g.memset(rows[:, FULL, :], int(NONE)).then_inc(pads, 1)
            g.memset(m.src[:, ET - 1:ET], 0).then_inc(pads, 1)
            g.memset(m.x[:, NB - 1, :], 0.0).then_inc(pads, 1)
            g.memset(m.ident[:, :], 0.0).then_inc(pool_step, 1)
            g.memset(m.ones[:, :], 1.0).then_inc(pool_step, 1)
            g.iota(m.iota[:, :], pattern=[[1, P]], base=0, channel_multiplier=0,
                   allow_small_or_imprecise_dtypes=True).then_inc(pool_step, 1)
            g.wait_ge(pool_step, 3)
            g.affine_select(out=m.ident[:, :], in_=m.ident[:, :], compare_op=ALU.not_equal, fill=1.0, base=0,
                            pattern=[[-1, P]], channel_multiplier=1).then_inc(pool_step, 1)
            g.memset(m.region[:, :], 0.0).then_inc(zeroed, 1)

        @block.vector
        def _(v):
            v.wait_ge(in_dstrow, 48)
            v.tensor_copy(rows_f, rows).then_inc(v_step, 1)
            v.wait_ge(v_step, 1)
            v.tensor_reduce(lows, rows_f, AX.X, ALU.min).then_inc(v_step, 1)
            v.wait_ge(v_step, 2)
            v.wait_ge(pool_step, 4)
            for c in range(4):
                v.tensor_scalar(diag[:, c, :], m.ident[:, :], lows[:, c:c + 1], None, ALU.mult).then_inc(v_step, 1)
            v.wait_ge(in_edges, 16 * 7)
            v.tensor_copy(m.dst0[:, :], stage[:, 0, :]).then_inc(v_step, 1)
            v.tensor_copy(m.type8[:, :], stage[:, 1, :]).then_inc(v_step, 1)
            v.tensor_copy(m.type16[:, :], stage[:, 2, :]).then_inc(v_step, 1)
            v.wait_ge(bc_ready, 1)
            v.tensor_copy(m.base0[:, :], m.ps[:, 0, 0:ET]).then_inc(v_step, 1)
            v.wait_ge(v_step, 10)
            v.tensor_tensor(over_t, m.dst0[:, :], m.base0[:, :], ALU.subtract).then_inc(v_step, 1)
            v.wait_ge(v_step, 11)
            v.tensor_scalar(over_t, over_t, float(WIN), None, ALU.is_ge).then_inc(v_step, 1)
            v.tensor_scalar(m.valid[:, :], m.dst0[:, :], NONE / 2, None, ALU.is_lt).then_inc(v_step, 1)
            v.wait_ge(v_step, 13)
            v.tensor_tensor(over_t, over_t, m.valid[:, :], ALU.mult).then_inc(v_step, 1)
            v.wait_ge(v_step, 14)
            v.tensor_reduce(over, over_t, AX.X, ALU.max).then_inc(v_step, 1)
            v.wait_ge(fl_ready, 1)
            v.tensor_reduce(flag, m.ps[0:1, 1, 0:P], AX.X, ALU.max).then_inc(v_step, 1)
            v.wait_ge(v_step, 16)
            v.tensor_scalar(flagr, flag, float(NWIN), 1.0, ALU.mult, ALU.add).then_inc(v_step, 1)
            v.wait_ge(v_step, 17)
            v.tensor_copy(m.rounds[:, :], flagr).then_inc(v_step, 1)
            v.wait_ge(in_comp, 16)

        @block.tensor
        def _(pe):
            pe.wait_ge(v_step, 6)
            for c in range(4):
                mm = pe.matmul(m.ps[:, 0, c * P:(c + 1) * P], m.ones[:, :], diag[:, c, :], start=True, stop=True)
            mm.then_inc(bc_ready, 1)
            pe.wait_ge(v_step, 15)
            pe.transpose(m.ps[0:1, 1, 0:P], over, m.ident[:, :]).then_inc(fl_ready, 1)


def statistics(v, m, stat):
    with v.Fori(0, NB) as b:
        v.bn_stats(m.stats[:, one(b), :], m.x[:, one(b), :]).then_inc(stat, 1)
    v.wait_ge(stat, NB)
    mean, half_gap, dev = m.mv[:, :, 0], m.mv[:, :, 1], m.rstd[:, :]
    v.tensor_tensor(mean, m.stats[:, :, 1], m.stats[:, :, 4], ALU.add).then_inc(stat, 1)
    v.tensor_tensor(half_gap, m.stats[:, :, 1], m.stats[:, :, 4], ALU.subtract).then_inc(stat, 1)
    v.tensor_tensor(dev, m.stats[:, :, 2], m.stats[:, :, 5], ALU.add).then_inc(stat, 1)
    v.wait_ge(stat, NB + 3)
    v.tensor_scalar(mean, mean, 0.5, None, ALU.mult).then_inc(stat, 1)
    v.scalar_tensor_tensor(out=half_gap, in0=half_gap, scalar=0.25, in1=half_gap, op0=ALU.mult, op1=ALU.mult
                           ).then_inc(stat, 1)
    v.wait_ge(stat, NB + 5)
    v.scalar_tensor_tensor(out=dev, in0=dev, scalar=1.0 / D, in1=half_gap, op0=ALU.mult, op1=ALU.add
                           ).then_inc(stat, 1)
    v.wait_ge(stat, STATS - 1)
    v.tensor_scalar(m.std[:, :], dev, EPS, None, ALU.add).then_inc(stat, 1)


STATS = NB + 7


def layernorm(nc, ctx, m, io, tag, use=None, keep=False, full=True, loads=(), table=None):
    def sem(name):
        return ctx.enter_context(nc.semaphore(tag + name))

    stat, root, normed, turned, evacuated = (sem(s) for s in ("stat", "root", "normed", "turned", "evacuated"))
    used, made = (sem("used"), sem("made")) if use else (None, None)
    copied = sem("copied") if keep or full else None
    kept = sem("kept") if keep else None
    stored = sem("stored") if table is not None else None
    cmat = sem("cmat") if use == "G" else None
    loaded = sem("loaded") if loads else None
    cd = m.dst[:, 0:64]
    copies = keep or full
    out, width, prod = {"G": (m.gbuf, P, None), "gates": (m.logit0, NE0, None), None: (None, 0, None)}[use]
    first_waits = {"G": (cmat, 3), "gates": (loaded, 16 * len(loads))}.get(use)
    with nc.Block() as block:
        @block.vector
        def _(v):
            if use == "G":
                v.tensor_copy(cd.rearrange("p (k b) -> p k b", b=NBASE),
                              m.comp_rep.rearrange("p (o b) -> p o b", o=1).broadcast_to([P, 16, NBASE])
                              ).then_inc(cmat, 1)
            statistics(v, m, stat)
            v.wait_ge(root, 1)
            v.reciprocal(m.rstd[:, :], m.std[:, :]).then_inc(stat, 1)
            v.wait_ge(stat, STATS + 1)
            slot_turned, slot_copied = Level(v, tag + "slot_turned"), Level(v, tag + "slot_copied")

            def group(g, first):
                for j in range(GB):
                    if not first:
                        v.wait_ge(turned, slot_turned.up())
                    if not first and copies:
                        v.wait_ge(copied, slot_copied.up())
                    v.tensor_scalar(m.hn[:, j, :], m.x[:, one(g * GB + j), :], m.mv[:, one(g * GB + j), 0],
                                    m.rstd[:, one(g * GB + j)], ALU.subtract, ALU.mult).then_inc(normed, 1)
            group(0, True)
            with v.Fori(1, NG) as g:
                group(g, False)

        @block.tensor
        def _(pe):
            if first_waits:
                pe.wait_ge(*first_waits)
            in_hn, bank_free, in_tT, out_free = (Level(pe, tag + s) for s in ("in_hn", "bank_free", "in_tT", "out_free"))

            def group(first):
                for j in range(GB):
                    pe.wait_ge(normed, in_hn.up())
                    if not (first and j < 2):
                        pe.wait_ge(evacuated, bank_free.up())
                    for c in range(2):
                        t = pe.transpose(m.ps[:, (0, 1, 0, 1, 7)[j], c * P:(c + 1) * P], m.hn[:, j, c * P:(c + 1) * P],
                                         m.ident[:, :])
                    t.then_inc(turned, 1)
                for j in range(GB if use else 0):
                    pe.wait_ge(evacuated, in_tT.up())
                    if not first:
                        pe.wait_ge(made, out_free.up())
                    for c in range(2):
                        if use == "G":
                            q = pe.matmul(m.ps[:, 2 + j, c * 64:(c + 1) * 64], m.tT[:, j, c, :], cd,
                                          start=True, stop=True)
                        else:
                            q = pe.matmul(m.ps[:, 2 + j, 0:NE0], m.tT[:, j, c, :], m.gW[:, c, :],
                                          start=(c == 0), stop=(c == 1))
                    q.then_inc(used, 1)
            group(True)
            with pe.Fori(1, NG):
                group(False)

        @block.scalar
        def _(act):
            act.wait_ge(stat, STATS)
            act.activation(m.std[:, :], m.std[:, :], ACT.Sqrt).then_inc(root, 1)
            in_bank, slot_used, slot_copied, product = (
                Level(act, tag + s) for s in ("in_bank", "slot_used", "aslot_copied", "product"))

            def group(g, first):
                for j in range(GB):
                    act.wait_ge(turned, in_bank.up())
                    if not first and use:
                        act.wait_ge(used, slot_used.up())
                    if not first and copies:
                        act.wait_ge(copied, slot_copied.up())
                    act.activation(m.tT[:, j, :, :], m.ps[:, (0, 1, 0, 1, 7)[j], 0:2 * P].rearrange(
                        "p (c n) -> p c n", c=2), ACT.Copy).then_inc(evacuated, 1)
                for j in range(GB if use else 0):
                    act.wait_ge(used, product.up())
                    act.activation(out[:, one(g * GB + j), :], m.ps[:, 2 + j, 0:width].rearrange(
                        "p (o n) -> p o n", o=1), ACT.Copy).then_inc(made, 1)
            group(0, True)
            with act.Fori(1, NG) as g:
                group(g, False)

        @block.gpsimd
        def _(gp):
            if use == "G":
                gp.wait_ge(cmat, 1)
                gp.affine_select(out=cd, in_=cd, compare_op=ALU.is_ge, fill=0.0, base=0,
                                 pattern=[[-R8, 16], [0, NBASE]], channel_multiplier=1).then_inc(cmat, 1)
                gp.wait_ge(cmat, 2)
                gp.affine_select(out=cd, in_=cd, compare_op=ALU.is_ge, fill=0.0, base=R8 - 1,
                                 pattern=[[R8, 16], [0, NBASE]], channel_multiplier=-1).then_inc(cmat, 1)
            if copies:
                ready = Level(gp, tag + "ready")
                with gp.Fori(0, NG) as g:
                    for j in range(GB):
                        gp.wait_ge(evacuated, ready.up())
                        if keep:
                            gp.tensor_copy(m.h[:, one(g * GB + j), :], m.hn[:, j, :].rearrange("p (o d) -> p o d", o=1)
                                           ).then_inc(kept, 1)
                        gp.tensor_copy(m.hT[:, :, bass.ds((g * GB + j) * P, P)], m.tT[:, j, :, :]).then_inc(copied, 1)

        @block.sync
        def _(sp):
            for dst, src in loads:
                sp.dma_start(dst, src).then_inc(loaded, 16)
            sp.wait_ge(loaded, 16 * len(loads)) if loads else None
            if table is not None:
                src = m.gbuf if use == "G" else m.h
                done = made if use == "G" else copied
                for g in range(NG):
                    sp.wait_ge(done, GB * (g + 1))
                    sp.dma_start(table[g * GN:(g + 1) * GN, :].rearrange("(b p) q -> p b q", p=P),
                                 src[:, g * GB:(g + 1) * GB, :]).then_inc(stored, 16)
                sp.wait_ge(stored, 16 * NG)


def sweep(nc, ctx, m, io, layer):
    def sem(name):
        return ctx.enter_context(nc.semaphore(f"l{layer}_{name}"))

    tag = f"l{layer}_"
    acc, ring, table = ((m.acc0, m.ring0, io["g_table"]), (m.acc1, m.ring1, io["h_table"]))[layer]
    key_step, keys_ready, src_ready, hot, summed, added = (
        sem(s) for s in ("key_step", "keys_ready", "src_ready", "hot", "summed", "added"))
    gathered = [sem(f"gathered{j}") for j in range(UNR)]
    loaded = sem("loaded")
    filled = sem("filled") if layer == 1 else None
    slots = [m.ps[:, k, (j - a) * P:(j - a + 1) * P] for k, (a, b) in enumerate(BANKS) for j in range(a, b)]
    with nc.Block() as block:
        @block.sync
        def _(sp):
            loads = [(m.basis, io["basis"].rearrange("(r p) d -> p r d", p=P))] if layer == 0 else [
                (m.wih, io["w_ihT"].rearrange("(c p) g -> p c g", p=P)),
                (m.whh, io["w_hhT"].rearrange("(c p) g -> p c g", p=P)),
                (m.rel[0:R16, :], io["rel"]),
                (m.bih, io["b_ihT"]), (m.bhh, io["b_hhT"])]
            for dst, src in loads:
                sp.dma_start(dst, src).then_inc(loaded, 16)
            sp.wait_ge(loaded, 16 * len(loads))

        @block.gpsimd
        def _(g):
            if layer == 1:
                g.memset(m.hot_type, 0.0).then_inc(filled, 1)
                g.memset(m.acc1, 0.0).then_inc(filled, 1)
            rounds = g.value_load(m.rounds[:, :], min_val=1, max_val=1 + NWIN)
            want = g.alloc_register(tag + "want")
            g.reg_mov(want, 1)
            with g.Fori(0, rounds):
                with g.Fori(0, NIT):
                    for a, b in PARTS:
                        g.wait_ge(src_ready, want)
                        g.reg_add(want, want, 1)
                        for j in range(a, b):
                            g.indirect_dma_start(ring[:, j, :], None, table,
                                                 bass.IndirectOffsetOnAxis(ap=m.src_now[:, j:j + 1], axis=0)
                                                 ).then_inc(gathered[j], 16)

        @block.scalar
        def _(act):
            rounds = act.value_load(m.rounds[:, :], min_val=1, max_val=1 + NWIN)
            keys, consumed = Level(act, tag + "keys"), Level(act, tag + "consumed")

            def indices(it, first):
                for a, b in PARTS:
                    if not first:
                        act.wait_ge(summed, consumed.up(b - a))
                    act.activation(m.src_now[:, a:b], m.src[:, bass.ds(it * UNR + a, b - a)], ACT.Copy
                                   ).then_inc(src_ready, 1)
            with act.Fori(0, rounds):
                act.wait_ge(keys_ready, keys.up())
                indices(0, True)
                with act.Fori(1, NIT) as it:
                    indices(it, False)
                consumed.up(UNR)

        @block.tensor
        def _(pe):
            rounds = pe.value_load(m.rounds[:, :], min_val=1, max_val=1 + NWIN)
            hots, landed, free = Level(pe, tag + "hots"), Level(pe, tag + "landed"), Level(pe, tag + "free")

            def products(first):
                landed.up(16)
                for a, b in PARTS:
                    if not first:
                        pe.wait_ge(added, free.up(b - a))
                    pe.wait_ge(hot, hots.up(1 + layer))
                    for j in range(a, b):
                        pe.wait_ge(gathered[j], landed.reg)
                        if layer == 0:
                            mm = pe.matmul(slots[j], ring[:, j, :], m.hot0[:, j, :], start=True, stop=True)
                        else:
                            for c in range(2):
                                pe.matmul(slots[j][:, c * WIN:(c + 1) * WIN], ring[:, j, c * P:(c + 1) * P],
                                          m.hot1[:, j, :], start=True, stop=True)
                            mm = pe.matmul(slots[j][:, 2 * WIN:3 * WIN], m.hot_type[:, j, :], m.hot1[:, j, :],
                                           start=True, stop=True)
                        mm.then_inc(summed, 1)
            with pe.Fori(0, rounds):
                products(True)
                with pe.Fori(1, NIT):
                    products(False)
                free.up(UNR)

        @block.vector
        def _(v):
            rounds = v.value_load(m.rounds[:, :], min_val=1, max_val=1 + NWIN)
            step, sums, adds = Level(v, tag + "step", 3), Level(v, tag + "sums"), Level(v, tag + "adds")
            v.tensor_copy(m.dst[:, :], m.dst0[:, :]).then_inc(key_step, 1)
            v.tensor_copy(m.base[:, :], m.base0[:, :]).then_inc(key_step, 1)
            v.memset(m.wincol[:, :], 0.0).then_inc(key_step, 1)
            v.wait_ge(key_step, 3)
            if layer == 1:
                v.wait_ge(filled, 2)

            def link(ins):
                ins.then_inc(key_step, 1)
                v.wait_ge(key_step, step.up())

            def keys():
                link(v.tensor_tensor(m.key[:, :], m.dst[:, :], m.base[:, :], ALU.subtract))
                link(v.tensor_scalar(m.valid[:, :], m.key[:, :], 0.0, None, ALU.is_ge))
                link(v.scalar_tensor_tensor(out=m.valid[:, :], in0=m.key[:, :], scalar=float(WIN), in1=m.valid[:, :],
                                            op0=ALU.is_lt, op1=ALU.mult))
                if layer == 0:
                    link(v.scalar_tensor_tensor(out=m.key[:, :], in0=m.type8[:, :], scalar=float(WIN), in1=m.key[:, :],
                                                op0=ALU.mult, op1=ALU.add))
                link(v.scalar_tensor_tensor(out=m.key[:, :], in0=m.key[:, :], scalar=1.0, in1=m.valid[:, :],
                                            op0=ALU.add, op1=ALU.mult))
                link(v.tensor_scalar(m.key[:, :], m.key[:, :], -1.0, None, ALU.add))
                link(v.scalar_tensor_tensor(out=m.dst[:, :], in0=m.valid[:, :], scalar=NONE, in1=m.dst[:, :],
                                            op0=ALU.mult, op1=ALU.add))
                link(v.tensor_copy(m.base_row[:, :], m.base[0:1, :]))
                link(v.tensor_scalar(m.base[:, :], m.base[:, :], 0.0, m.wincol[:, :], ALU.mult, ALU.add))
                v.tensor_scalar(m.wincol[:, :], m.wincol[:, :], float(WIN), None, ALU.add).then_inc(keys_ready, 1)

            def one_hots(it, part):
                a, b = PARTS[part]
                n = b - a

                def column(t):
                    return t[:, bass.ds(it * UNR + a, n)].rearrange("p (t o) -> p t o", o=1)

                def row(w):
                    return m.iota[:, 0:w].rearrange("p (o w) -> p o w", o=1).broadcast_to([P, n, w])
                if layer == 0:
                    v.tensor_tensor(m.hot0[:, a:b, :], row(P), column(m.key).broadcast_to([P, n, P]), ALU.is_equal
                                    ).then_inc(hot, 1)
                else:
                    v.tensor_tensor(m.hot1[:, a:b, :], row(WIN), column(m.key).broadcast_to([P, n, WIN]), ALU.is_equal
                                    ).then_inc(hot, 1)
                    v.tensor_tensor(m.hot_type[:, a:b, 0:R16], row(R16), column(m.type16).broadcast_to([P, n, R16]),
                                    ALU.is_equal).then_inc(hot, 1)

            def windows(it, part):
                k = R8 if layer == 0 else 3
                opens = {a: b - a for a, b in BANKS}
                for j in range(*PARTS[part]):
                    at = v.value_load(m.base_row[0:1, bass.ds(it * UNR + j, 1)], min_val=0, max_val=N)
                    if j in opens:
                        v.wait_ge(summed, sums.up(opens[j]))
                    v.wait_ge(added, adds.reg)
                    adds.up()
                    win = acc[:, 0:k, bass.ds(at, WIN)]
                    v.tensor_tensor(win, win, slots[j][:, 0:k * WIN].rearrange("p (k w) -> p k w", k=k), ALU.add
                                    ).then_inc(added, 1)

            with v.Fori(0, rounds):
                keys()
                one_hots(0, 0)
                one_hots(0, 1)
                windows(0, 0)
                with v.Fori(1, NIT) as it:
                    one_hots(it, 0)
                    windows(it - 1, 1)
                    one_hots(it, 1)
                    windows(it, 0)
                windows(NIT - 1, 1)


def aggregate(nc, ctx, m, io):
    def sem(name):
        return ctx.enter_context(nc.semaphore("agg_" + name))

    loaded, copied, multiplied, read, biased, summed = (
        sem(s) for s in ("loaded", "copied", "multiplied", "read", "biased", "summed"))
    with nc.Block() as block:
        @block.sync
        def _(sp):
            sp.dma_start(m.hrow, io["gnn_bias"].rearrange("(o d) -> o d", o=1).broadcast_to([P, D])
                         ).then_inc(loaded, 16)
            sp.wait_ge(loaded, 16)

        @block.scalar
        def _(act):
            free = Level(act, "agg_free")

            def group(g, first):
                for j in range(GB):
                    if not first:
                        act.wait_ge(multiplied, free.up())
                    act.activation(m.sring[:, j, :, :], m.acc0[:, :, bass.ds((g * GB + j) * P, P)], ACT.Copy
                                   ).then_inc(copied, 1)
            group(0, True)
            with act.Fori(1, NG) as g:
                group(g, False)

        @block.tensor
        def _(pe):
            ready, free = Level(pe, "agg_ready"), Level(pe, "agg_bank_free")

            def group(first):
                for j in range(GB):
                    pe.wait_ge(copied, ready.up())
                    if not first:
                        pe.wait_ge(read, free.up())
                    for r in range(R8):
                        mm = pe.matmul(m.ps[:, j, 0:D], m.sring[:, j, r, :], m.basis[:, r, :],
                                       start=(r == 0), stop=(r == R8 - 1))
                    mm.then_inc(multiplied, 1)
            group(True)
            with pe.Fori(1, NG):
                group(False)

        @block.vector
        def _(v):
            v.wait_ge(loaded, 16)
            ready, own = Level(v, "agg_product"), Level(v, "agg_biased")
            with v.Fori(0, NG) as g:
                for j in range(GB):
                    v.wait_ge(multiplied, ready.up())
                    v.tensor_tensor(m.hn[:, j, :], m.ps[:, j, 0:D], m.hrow, ALU.add).then_inc(read, 1)
                    v.wait_ge(read, own.up())
                    xb = m.x[:, one(g * GB + j), :]
                    v.scalar_tensor_tensor(out=xb, in0=m.hn[:, j, :].rearrange("p (o d) -> p o d", o=1), scalar=0.0,
                                           in1=xb, op0=ALU.max, op1=ALU.add).then_inc(summed, 1)


def top_two(nc, ctx, m, io):
    def sem(name):
        return ctx.enter_context(nc.semaphore("top_" + name))

    v_step, a_step = sem("v_step"), sem("a_step")
    n = NB * NE0
    logit, w = m.logit0, m.w0
    scr = [m.gate0[:, i, :] for i in range(12)]

    def be(t):
        return t.rearrange("p (b e) -> p b e", e=NE0)
    prob, comp, rank = be(scr[0]), m.gate0[:, 1:5, :], m.gate0[:, 5, :]
    col, shifted, chosen, exps = m.gate0[:, 6, 0:NB], be(scr[7]), be(scr[8]), be(scr[9])

    def spread(c):
        return c.rearrange("p (b o) -> p b o", o=1).broadcast_to([P, NB, NE0])
    with nc.Block() as block:
        @block.vector
        def _(v):
            count = [0]

            def link(ins):
                count[0] += 1
                ins.then_inc(v_step, 1)
                v.wait_ge(v_step, count[0])

            def softmax_head(src):
                link(v.tensor_reduce(col, src, AX.X, ALU.max))
                link(v.tensor_tensor(shifted, src, spread(col), ALU.subtract))

            def softmax_tail(dst, src):
                link(v.tensor_reduce(col, src, AX.X, ALU.add))
                link(v.reciprocal(col, col))
                link(v.tensor_tensor(dst, src, spread(col), ALU.mult))

            link(v.tensor_tensor(logit, logit, m.gb.rearrange("p (o e) -> p o e", o=1).broadcast_to([P, NB, NE0]),
                                 ALU.add))
            softmax_head(logit)
            v.wait_ge(a_step, 1)
            softmax_tail(prob, exps)
            link(v.memset(comp, 0.0))
            for e in range(NE0):
                ce = be(comp[:, e, :])
                for lo, hi, op in ((0, e, ALU.is_ge), (e + 1, NE0, ALU.is_gt)):
                    if hi > lo:
                        link(v.tensor_tensor(ce[:, :, lo:hi], prob[:, :, lo:hi],
                                             prob[:, :, e:e + 1].broadcast_to([P, NB, hi - lo]), op))
            link(v.tensor_reduce(rank, comp.rearrange("p e (b f) -> p (e b) f", f=NE0), AX.X, ALU.add))
            link(v.tensor_scalar(chosen.rearrange("p b e -> p e b"), rank.rearrange("p (e b) -> p e b", e=NE0),
                                 2.0, None, ALU.is_lt))
            softmax_head(prob)
            v.wait_ge(a_step, 2)
            link(v.tensor_tensor(exps, exps, chosen, ALU.mult))
            softmax_tail(w, exps)
            top_two.steps = count[0]

        @block.scalar
        def _(act):
            act.wait_ge(v_step, 3)
            act.activation(exps, shifted, ACT.Exp).then_inc(a_step, 1)
            act.wait_ge(v_step, 3 + 3 + 1 + 2 * (NE0 - 1) + 2 + 2)
            act.activation(exps, shifted, ACT.Exp).then_inc(a_step, 1)


def ffn0(nc, ctx, m, io):
    def sem(name):
        return ctx.enter_context(nc.semaphore("f0_" + name))

    staged, task, a_read, wb_task, weighted, out_task, o_read, setup = (
        sem(s) for s in ("staged", "task", "a_read", "wb_task", "weighted", "out_task",
                         "o_read", "setup"))
    NA = 3 + 12 + 6
    TURNS = ((0, 2), (2, 4), (4, 5))

    def half(h):
        return slice(h * HALF, (h + 1) * HALF)
    with nc.Block() as block:
        @block.gpsimd
        def _(g):
            g.memset(m.sel[0:NE0, :, :], 1.0).then_inc(setup, 1)
            g.memset(m.wT[0:NE0 + 1, :], 1.0).then_inc(setup, 1)
            sel = m.sel[0:NE0, :, :].rearrange("e q c -> e (q c)")
            g.wait_ge(setup, 2)
            g.affine_select(out=sel, in_=sel, compare_op=ALU.is_ge, fill=0.0, base=0, pattern=[[1, 2 * P]],
                            channel_multiplier=-64).then_inc(setup, 1)
            g.wait_ge(setup, 3)
            g.affine_select(out=sel, in_=sel, compare_op=ALU.is_ge, fill=0.0, base=63, pattern=[[-1, 2 * P]],
                            channel_multiplier=64).then_inc(setup, 1)
            turned = Level(g, "f0_turned", 3)
            g.tensor_copy(m.wst, m.w0[:, 0:GB, :]).then_inc(staged, 1)
            with g.Fori(1, NG) as i:
                g.wait_ge(a_read, turned.reg)
                turned.up(NA)
                g.tensor_copy(m.wst, m.w0[:, bass.ds(i * GB, GB), :]).then_inc(staged, 1)

        @block.tensor
        def _(pe):
            pe.wait_ge(setup, 4)
            stage, banks, evac, wfree, wted, ofree = (
                Level(pe, "f0_" + s) for s in ("stage", "banks", "evac", "wfree", "wted", "ofree"))

            def group(g, first):
                k = 0

                def bank():
                    nonlocal k
                    if not (first and k < 3):
                        pe.wait_ge(a_read, banks.up())
                    k += 1
                    return (k - 1) % 3

                pe.wait_ge(staged, stage.up())
                for a, b in TURNS:
                    t = bank()
                    for j in range(a, b):
                        mm = pe.transpose(m.ps[0:NE0, t, (j - a) * P:(j - a + 1) * P], m.wst[:, j, :], m.ident[:, :])
                    mm.then_inc(task, 1)
                for i in range(6):
                    for h in range(2):
                        t = bank()
                        for c in range(2):
                            w = m.sW1[:, c, i * P:(i + 1) * P] if i < 2 else m.eW1[:, i - 2, c, :]
                            mm = pe.matmul(m.ps[:, t, 0:HALF], w, m.hT[:, c, bass.ds(g * GN + h * HALF, HALF)],
                                           start=(c == 0), stop=(c == 1))
                        mm.then_inc(task, 1)
                pe.wait_ge(a_read, evac.up(3))

                def spread(q):
                    for h in range(2):
                        if not (first and q == 0):
                            pe.wait_ge(weighted, wfree.up())
                        pe.matmul(m.ps[:, 3 + h, 0:HALF], m.sel[0:NE0, q, :], m.wT[0:NE0, half(h)],
                                  start=True, stop=True).then_inc(wb_task, 1)
                spread(0)
                pe.wait_ge(a_read, evac.up(12))
                for i in (1, 2, 0):
                    if i == 2:
                        spread(1)
                    for h in range(2):
                        t = bank()
                        if i == 0:
                            for c in range(2):
                                mm = pe.matmul(m.ps[:, t, 0:HALF], m.sW2[:, c, :], m.a1[:, c, half(h)],
                                               start=(c == 0), stop=(c == 1))
                        else:
                            for e in range(2):
                                x = 2 * (i - 1) + e
                                mm = pe.matmul(m.ps[64 * e:64 * e + 64, t, 0:HALF], m.eW2[:, x, :],
                                               m.a1[:, 2 + x, half(h)], start=True, stop=True)
                        mm.then_inc(task, 1)
                pe.wait_ge(a_read, evac.up(6))
                pe.wait_ge(weighted, wted.up(4))
                for j in range(GB):
                    if not (first and j < 2):
                        pe.wait_ge(o_read, ofree.up())
                    o = m.ps[:, (5, 6, 7, 5, 6)[j], 0:D]
                    s = slice(j * P, (j + 1) * P)
                    pe.matmul(o, m.a2[:, 0, s], m.sW3, start=True, stop=False)
                    for q in range(2):
                        pe.matmul(o, m.a2[:, 1 + q, s], m.eW3[:, q, :], start=False, stop=False)
                    pe.matmul(o, m.wT[0:NE0 + 1, s], m.b3[0:NE0 + 1, :], start=False, stop=True
                              ).then_inc(out_task, 1)
            group(0, True)
            with pe.Fori(1, NG) as g:
                group(g, False)

        @block.scalar
        def _(act):
            act.wait_ge(setup, 2)
            ready, outs = Level(act, "f0_ready"), Level(act, "f0_outs")

            def group(first):
                k = 0

                def tile():
                    nonlocal k
                    act.wait_ge(task, ready.up())
                    k += 1
                    return (k - 1) % 3

                if not first:
                    act.wait_ge(out_task, outs.up(GB))
                for a, b in TURNS:
                    t = tile()
                    act.activation(m.wT[0:NE0, a * P:b * P], m.ps[0:NE0, t, 0:(b - a) * P], ACT.Copy
                                   ).then_inc(a_read, 1)
                for i in range(6):
                    for h in range(2):
                        t = tile()
                        act.activation(m.a1[:, i, half(h)], m.ps[:, t, 0:HALF], ACT.Relu, bias=m.b1[:, i:i + 1]
                                       ).then_inc(a_read, 1)
                for i in (1, 2, 0):
                    for h in range(2):
                        t = tile()
                        act.activation(m.a2[:, i, half(h)], m.ps[:, t, 0:HALF], ACT.Relu, bias=m.b2[:, i:i + 1]
                                       ).then_inc(a_read, 1)
            group(True)
            with act.Fori(1, NG):
                group(False)

        @block.vector
        def _(v):
            spread, evac, outs = Level(v, "f0_spread"), Level(v, "f0_vevac", 15), Level(v, "f0_vouts")
            with v.Fori(0, NG) as g:
                for n in range(4):
                    q, h = n // 2, n % 2
                    v.wait_ge(wb_task, spread.up())
                    v.wait_ge(a_read, evac.up())
                    a = m.a2[:, 1 + q, half(h)]
                    v.tensor_tensor(a, a, m.ps[:, 3 + n % 2, 0:HALF], ALU.mult).then_inc(weighted, 1)
                evac.up(NA - 4)
                for j in range(GB):
                    v.wait_ge(out_task, outs.up())
                    xb = m.x[:, one(g * GB + j), :]
                    v.tensor_tensor(xb, xb, m.ps[:, (5, 6, 7, 5, 6)[j], 0:D].rearrange("p (o d) -> p o d", o=1),
                                    ALU.add).then_inc(o_read, 1)


def gru(nc, ctx, m, io):
    def sem(name):
        return ctx.enter_context(nc.semaphore("gru_" + name))

    rel_task, rel_read, rz_task, rz_read, n_task, n_read, tanhed, mixed, turned, summed, bias = (
        sem(s) for s in ("rel_task", "rel_read", "rz_task", "rz_read", "n_task", "n_read", "tanhed", "mixed",
                         "turned", "summed", "bias"))
    TB = (6, 7, 1, 6, 7)

    def half(h):
        return slice(h * HALF, (h + 1) * HALF)
    with nc.Block() as block:
        @block.tensor
        def _(pe):
            names = ("rel_free", "rel_done", "rz_free", "n_free", "mix", "x_free")
            rel_free, rel_done, rz_free, n_free, mix, x_free = (Level(pe, "gru_" + s, int(s == "rel_free")) for s in names)

            def group(g, first):
                def nodes(h):
                    return bass.ds(g * GN + h * HALF, HALF)
                for n in range(4):
                    h, c = n // 2, n % 2
                    if not (first and n < 1):
                        pe.wait_ge(rel_read, rel_free.reg)
                        rel_free.up()
                    pe.matmul(m.ps[:, 0, 0:HALF], m.rel[0:R16, c * P:(c + 1) * P], m.acc1[0:R16, 2, nodes(h)],
                              start=True, stop=True).then_inc(rel_task, 1)
                pe.wait_ge(rel_read, rel_done.up(4))
                k = 0
                for h in range(2):
                    for c in range(2):
                        for gate in range(2):
                            if not (first and k < 2):
                                pe.wait_ge(rz_read, rz_free.up())
                            k += 1
                            col = slice((2 * gate + c) * P, (2 * gate + c + 1) * P)
                            o = m.ps[:, 2 + gate, 0:HALF]
                            for f in range(2):
                                pe.matmul(o, m.wih[:, f, col], m.acc1[:, f, nodes(h)], start=(f == 0), stop=False)
                            for f in range(2):
                                mm = pe.matmul(o, m.whh[:, f, col], m.hT[:, f, nodes(h)], start=False, stop=(f == 1))
                            mm.then_inc(rz_task, 1)
                        for part, (w, src) in enumerate(((m.whh, m.hT), (m.wih, m.acc1))):
                            if not (first and k <= 2):
                                pe.wait_ge(n_read, n_free.up())
                            col = slice((4 + c) * P, (5 + c) * P)
                            for f in range(2):
                                mm = pe.matmul(m.ps[:, 4 + part, 0:HALF], w[:, f, col], src[:, f, nodes(h)],
                                               start=(f == 0), stop=(f == 1))
                            mm.then_inc(n_task, 1)
                pe.wait_ge(mixed, mix.up(12))
                for j in range(GB):
                    if not (first and j < 2):
                        pe.wait_ge(summed, x_free.up())
                    for c in range(2):
                        t = pe.transpose(m.ps[:, TB[j], c * P:(c + 1) * P], m.gn[:, c, j * P:(j + 1) * P],
                                         m.ident[:, :])
                    t.then_inc(turned, 1)
            group(0, True)
            with pe.Fori(1, NG) as g:
                group(g, False)

        @block.scalar
        def _(act):
            ready, free, pre = Level(act, "gru_ready"), Level(act, "gru_gfree"), Level(act, "gru_pre")
            act.wait_ge(bias, 1)

            def group(first):
                if not first:
                    act.wait_ge(turned, free.up(GB))

                def tanh(n):
                    h, c = n // 2, n % 2
                    act.wait_ge(n_read, pre.up(2))
                    act.activation(m.gn[:, c, half(h)], m.gt[:, c, half(h)], ACT.Tanh, bias=m.bih[:, 4 + c:5 + c]
                                   ).then_inc(tanhed, 1)
                for n in range(4):
                    h, c = n // 2, n % 2
                    for gate, dst in enumerate((m.gr, m.gz)):
                        act.wait_ge(rz_task, ready.up())
                        act.activation(dst[:, c, half(h)], m.ps[:, 2 + gate, 0:HALF], ACT.Sigmoid,
                                       bias=m.brz[:, 2 * gate + c:2 * gate + c + 1]).then_inc(rz_read, 1)
                    if n:
                        tanh(n - 1)
                tanh(3)
            group(True)
            with act.Fori(1, NG):
                group(False)

        @block.vector
        def _(v):
            v.tensor_tensor(m.brz, m.bih[:, 0:4], m.bhh[:, 0:4], ALU.add).then_inc(bias, 1)
            names = ("rel", "r", "ntask", "own", "z", "tan", "mown", "back")
            rel, r, ntask, own, z, tan, mown, back = (Level(v, "gru_v" + s) for s in names)
            with v.Fori(0, NG) as g:
                for n in range(4):
                    h, c = n // 2, n % 2
                    v.wait_ge(rel_task, rel.up())
                    a = m.acc1[:, c, bass.ds(g * GN + h * HALF, HALF)]
                    v.tensor_tensor(a, a, m.ps[:, 0, 0:HALF], ALU.add).then_inc(rel_read, 1)

                def new(n):
                    h, c = n // 2, n % 2
                    t = m.gt[:, c, half(h)]
                    v.wait_ge(n_task, ntask.up())
                    v.wait_ge(rz_read, r.up())
                    r.up()
                    v.scalar_tensor_tensor(out=t, in0=m.ps[:, 4, 0:HALF], scalar=m.bhh[:, 4 + c:5 + c],
                                           in1=m.gr[:, c, half(h)], op0=ALU.add, op1=ALU.mult).then_inc(n_read, 1)
                    v.wait_ge(n_task, ntask.up())
                    v.wait_ge(n_read, own.up())
                    own.up()
                    v.tensor_tensor(t, t, m.ps[:, 5, 0:HALF], ALU.add).then_inc(n_read, 1)

                def mix(n):
                    h, c = n // 2, n % 2
                    t, new_h = m.gt[:, c, half(h)], m.gn[:, c, half(h)]
                    v.wait_ge(tanhed, tan.up())
                    v.tensor_tensor(t, m.hT[:, c, bass.ds(g * GN + h * HALF, HALF)], new_h, ALU.subtract
                                    ).then_inc(mixed, 1)
                    v.wait_ge(rz_read, z.up(2))
                    v.wait_ge(mixed, mown.up())
                    v.tensor_tensor(t, t, m.gz[:, c, half(h)], ALU.mult).then_inc(mixed, 1)
                    v.wait_ge(mixed, mown.up())
                    v.tensor_tensor(new_h, new_h, t, ALU.add).then_inc(mixed, 1)
                    mown.up()
                for n in range(4):
                    new(n)
                    if n:
                        mix(n - 1)
                mix(3)
                for j in range(GB):
                    v.wait_ge(turned, back.up())
                    xb = m.x[:, one(g * GB + j), :]
                    v.tensor_tensor(xb, xb, m.ps[:, TB[j], 0:D].rearrange("p (o d) -> p o d", o=1), ALU.add
                                    ).then_inc(summed, 1)


def hidden(nc, ctx, m, io):
    def sem(name):
        return ctx.enter_context(nc.semaphore("hid_" + name))

    task, gelued, logits, read = (sem(s) for s in ("task", "gelued", "logits", "read"))

    def half(h):
        return slice(h * HALF, (h + 1) * HALF)
    with nc.Block() as block:
        @block.tensor
        def _(pe):
            free, done, lfree = Level(pe, "hid_free"), Level(pe, "hid_done"), Level(pe, "hid_lfree")

            def group(g, first):
                for k in range(2 * MH):
                    i, h = k // 2, k % 2
                    if not (first and k < 4):
                        pe.wait_ge(gelued, free.up())
                    for c in range(2):
                        mm = pe.matmul(m.ps[:, k % 4, 0:HALF], m.W1[:, c, i * P:(i + 1) * P],
                                       m.hT[:, c, bass.ds(g * GN + h * HALF, HALF)], start=(c == 0), stop=(c == 1))
                    mm.then_inc(task, 1)
                pe.wait_ge(gelued, done.up(2 * MH))
                if not first:
                    pe.wait_ge(read, lfree.up())
                for j in range(GB):
                    for i in range(MH):
                        mm = pe.matmul(m.ps[:, 4, j * NE1:(j + 1) * NE1], m.H0[:, i, j * P:(j + 1) * P], m.Wg[:, i, :],
                                       start=(i == 0), stop=(i == MH - 1))
                mm.then_inc(logits, 1)
            group(0, True)
            with pe.Fori(1, NG) as g:
                group(g, False)

        @block.scalar
        def _(act):
            ready, free = Level(act, "hid_ready"), Level(act, "hid_hfree")

            def group(first):
                if not first:
                    act.wait_ge(logits, free.up())
                for k in range(2 * MH):
                    act.wait_ge(task, ready.up())
                    act.activation(m.H0[:, k // 2, half(k % 2)], m.ps[:, k % 4, 0:HALF], ACT.Gelu,
                                   bias=m.bf1[:, k // 2:k // 2 + 1]).then_inc(gelued, 1)
            group(True)
            with act.Fori(1, NG):
                group(False)

        @block.vector
        def _(v):
            ready = Level(v, "hid_vready")
            with v.Fori(0, NG) as g:
                v.wait_ge(logits, ready.up())
                v.tensor_tensor(m.logit1[:, bass.ds(g * GB, GB), :],
                                m.ps[:, 4, 0:GB * NE1].rearrange("p (b e) -> p b e", e=NE1),
                                m.bg.rearrange("p (o e) -> p o e", o=1).broadcast_to([P, GB, NE1]), ALU.add
                                ).then_inc(read, 1)


def route(nc, ctx, m, io):
    def sem(name):
        return ctx.enter_context(nc.semaphore("rt_" + name))

    v_step, a_step, p_step, counted, placed, sent = (
        sem(s) for s in ("v_step", "a_step", "p_step", "counted", "placed", "sent"))

    def per_block(c, e=NE1):
        return c.rearrange("p (b o) -> p b o", o=1).broadcast_to([P, NB, e])

    def per_expert(r, n):
        return r.rearrange("p (o e) -> p o e", o=1).broadcast_to([P, n, NE1])
    with nc.Block() as block:
        @block.vector
        def _(v):
            count = [0]

            def link(ins):
                count[0] += 1
                ins.then_inc(v_step, 1)
                v.wait_ge(v_step, count[0])

            link(v.tensor_reduce(m.col1, m.logit1, AX.X, ALU.max))
            link(v.tensor_tensor(m.tmp1, m.logit1, per_block(m.col1), ALU.subtract))
            v.wait_ge(a_step, 1)
            link(v.tensor_reduce(m.col1, m.prob1, AX.X, ALU.add))
            link(v.reciprocal(m.col1, m.col1))
            link(v.tensor_tensor(m.prob1, m.prob1, per_block(m.col1), ALU.mult))
            link(v.tensor_reduce(m.best, m.prob1, AX.X, ALU.max))
            link(v.tensor_tensor(m.tmp1, m.prob1, per_block(m.best), ALU.is_lt))
            link(v.scalar_tensor_tensor(out=m.tmp1, in0=m.tmp1, scalar=float(4 * NE1),
                                        in1=per_expert(m.iota[:, 0:NE1], NB), op0=ALU.mult, op1=ALU.add))
            link(v.tensor_reduce(m.col1, m.tmp1, AX.X, ALU.min))
            link(v.tensor_tensor(m.pick, per_expert(m.iota[:, 0:NE1], NB), per_block(m.col1), ALU.is_equal))
            v.wait_ge(p_step, 4)
            last = m.pick[:, NB - 1, :]
            link(v.tensor_tensor(last, last, m.padmask, ALU.mult))
            v.wait_ge(counted, 1)
            link(v.tensor_copy(m.tot, m.ps[:, 1, 0:NB * NE1].rearrange("p (b e) -> p e b", e=NE1)))
            for e in range(NE1):
                link(v.tensor_tensor_scan(out=m.cum[:, e, :], data0=m.ones[:, 0:NB], data1=m.tot[:, e, :],
                                          initial=0.0, op0=ALU.mult, op1=ALU.add))
            steps = m.steps.rearrange("p (o k) -> p o k", o=1).broadcast_to([P, NE1, NB])
            link(v.tensor_scalar(m.steps, m.iota[:, 0:NB], float(P), None, ALU.mult))
            t = m.tmp1.rearrange("p b e -> p (b e)").rearrange("p (e k) -> p e k", k=NB)
            link(v.tensor_tensor(t, m.cum[:, :, NB - 1:NB].broadcast_to([P, NE1, NB]), steps, ALU.is_gt))
            link(v.tensor_reduce(m.ntiles, t, AX.X, ALU.add))
            link(v.tensor_tensor_scan(out=m.ends, data0=m.ones[:, 0:NE1], data1=m.ntiles, initial=0.0,
                                      op0=ALU.mult, op1=ALU.add))
            link(v.tensor_tensor(m.starts, m.ends, m.ntiles, ALU.subtract))
            link(v.tensor_tensor(m.tmp2, m.iota[:, 0:TILES].rearrange("p (t o) -> p t o", o=1
                                                                      ).broadcast_to([P, TILES, NE1]),
                                 per_expert(m.ends, TILES), ALU.is_ge))
            link(v.tensor_reduce(m.ofTf, m.tmp2, AX.X, ALU.add))
            link(v.tensor_scalar(m.ofTf, m.ofTf, float(NE1 - 1), None, ALU.min))
            link(v.tensor_copy(m.ofT, m.ofTf))
            link(v.tensor_scalar(m.starts, m.starts, float(P), None, ALU.mult))
            link(v.tensor_tensor(m.cum, m.cum, m.tot, ALU.subtract))
            link(v.tensor_tensor(m.before, m.ps[:, 0, 0:NB * NE1].rearrange("p (b e) -> p b e", e=NE1),
                                 m.cum.rearrange("p e b -> p b e"), ALU.add))
            link(v.tensor_tensor(m.before, m.before, per_expert(m.starts, NB), ALU.add))
            link(v.tensor_tensor(m.before, m.before, m.pick, ALU.mult))
            link(v.tensor_reduce(m.posf, m.before, AX.X, ALU.add))
            v.tensor_copy(m.slot_of, m.posf).then_inc(placed, 1)

        @block.scalar
        def _(act):
            act.wait_ge(v_step, 2)
            act.activation(m.prob1, m.tmp1, ACT.Exp).then_inc(a_step, 1)

        @block.tensor
        def _(pe):
            pe.wait_ge(v_step, 11)
            pick = m.pick.rearrange("p b e -> p (b e)")
            pe.matmul(m.ps[:, 0, 0:NB * NE1], m.tri, pick, start=True, stop=True)
            pe.matmul(m.ps[:, 1, 0:NB * NE1], m.ones[:, :], pick, start=True, stop=True).then_inc(counted, 1)

        @block.gpsimd
        def _(g):
            g.memset(m.tri, 1.0).then_inc(p_step, 1)
            g.memset(m.padmask, 1.0).then_inc(p_step, 1)
            g.wait_ge(p_step, 2)
            g.affine_select(out=m.tri, in_=m.tri, compare_op=ALU.is_gt, fill=0.0, base=0, pattern=[[1, P]],
                            channel_multiplier=-1).then_inc(p_step, 1)
            g.affine_select(out=m.padmask, in_=m.padmask, compare_op=ALU.is_ge, fill=0.0, base=NTAIL - 1,
                            pattern=[[0, NE1]], channel_multiplier=-1).then_inc(p_step, 1)
            g.wait_ge(placed, 1)
            for b in range(NB):
                n = P if b < NB - 1 else NTAIL
                g.indirect_dma_start(io["slots_in"], bass.IndirectOffsetOnAxis(ap=m.slot_of[0:n, b:b + 1], axis=0),
                                     m.h[0:n, b, :], None).then_inc(sent, 16)
            g.wait_ge(sent, 16 * NB)


def experts(nc, ctx, m, io):
    def sem(name):
        return ctx.enter_context(nc.semaphore("ex_" + name))

    loaded = [sem("loaded0"), sem("loaded1")]
    stored = [sem("stored0"), sem("stored1")]
    turned, evacuated, task, gelued, product, read = (
        sem(s) for s in ("turned", "evacuated", "task", "gelued", "product", "read"))
    Q = TILES // 4
    with nc.Block() as block:
        @block.sync
        def _(sp):
            def rows(t, q):
                return t[bass.ds(q * 4 * P, 4 * P), :].rearrange("(i p) d -> p i d", p=P)
            for i in range(2):
                sp.dma_start(m.slots[i], rows(io["slots_in"], i)).then_inc(loaded[i], 16)
            for q in range(Q):
                i = q % 2
                sp.wait_ge(read, 4 * (q + 1))
                sp.dma_start(rows(io["slots_out"], q), m.results[i]).then_inc(stored[i], 16)
                if q + 2 < Q:
                    sp.wait_ge(turned, q + 1)
                    sp.dma_start(m.slots[i], rows(io["slots_in"], q + 2)).then_inc(loaded[i], 16)
            for i in range(2):
                sp.wait_ge(stored[i], 16 * Q // 2)

        @block.tensor
        def _(pe):
            landed, hts, free, hid, ofree = (Level(pe, "ex_" + s) for s in ("landed", "hts", "free", "hid", "ofree"))

            def quad(q, i, first):
                e = [pe.value_load(m.ofT[0:1, bass.ds(q * 4 + t, 1)], min_val=0, max_val=NE1 - 1) for t in range(4)]
                if i == 0:
                    landed.up(16)
                pe.wait_ge(loaded[i], landed.reg)
                for c in range(2):
                    for t in range(4):
                        mm = pe.transpose(m.ps[:, c, t * P:(t + 1) * P], m.slots[i][:, t, c * P:(c + 1) * P],
                                          m.ident[:, :])
                mm.then_inc(turned, 1)
                pe.wait_ge(evacuated, hts.up())
                for k in range(MH):
                    if not (first and k < 4):
                        pe.wait_ge(gelued, free.up())
                    for c in range(2):
                        mm = pe.matmul(m.ps[:, 2 + k % 4, :], m.W1[:, c, k * P:(k + 1) * P], m.hTQ[:, c, :],
                                       start=(c == 0), stop=(c == 1))
                    mm.then_inc(task, 1)
                pe.wait_ge(gelued, hid.up(MH))
                for t in range(4):
                    if not (first and t < 2):
                        pe.wait_ge(read, ofree.up())
                    for k in range(MH):
                        mm = pe.matmul(m.ps[:, 6 + t % 2, 0:D], m.HQ[i][:, k, t * P:(t + 1) * P],
                                       m.Wd[:, one(e[t]), k, :], start=(k == 0), stop=(k == MH - 1))
                    mm.then_inc(product, 1)
            quad(0, 0, True)
            quad(1, 1, False)
            with pe.Fori(1, Q // 2) as q2:
                for i in range(2):
                    quad(q2 * 2 + i, i, False)

        @block.scalar
        def _(act):
            ready, free = Level(act, "ex_ready"), Level(act, "ex_hfree")

            def quad(i, first):
                if not first:
                    act.wait_ge(product, free.up(4))
                for k in range(MH):
                    act.wait_ge(task, ready.up())
                    act.activation(m.HQ[i][:, k, :], m.ps[:, 2 + k % 4, :], ACT.Gelu, bias=m.bf1[:, k:k + 1]
                                   ).then_inc(gelued, 1)
            for i in range(2):
                quad(i, True)
            with act.Fori(1, Q // 2):
                for i in range(2):
                    quad(i, False)

        @block.vector
        def _(v):
            turn, prod, store = Level(v, "ex_turn"), Level(v, "ex_prod"), Level(v, "ex_store")

            def quad(q, i, first):
                v.wait_ge(turned, turn.up())
                for c in range(2):
                    ins = v.tensor_copy(m.hTQ[:, c, :], m.ps[:, c, :])
                ins.then_inc(evacuated, 1)
                if not first:
                    if i == 0:
                        store.up(16)
                    v.wait_ge(stored[i], store.reg)
                for t in range(4):
                    e = v.value_load(m.ofT[0:1, bass.ds(q * 4 + t, 1)], min_val=0, max_val=NE1 - 1)
                    v.wait_ge(product, prod.up())
                    v.tensor_tensor(m.results[i][:, t, :].rearrange("p (o d) -> p o d", o=1),
                                    m.ps[:, 6 + t % 2, 0:D].rearrange("p (o d) -> p o d", o=1),
                                    m.bd[:, one(e), :], ALU.add).then_inc(read, 1)
            for i in range(2):
                quad(i, i, True)
            with v.Fori(1, Q // 2) as q2:
                for i in range(2):
                    quad(q2 * 2 + i, i, False)


def finish(nc, ctx, m, io):
    def sem(name):
        return ctx.enter_context(nc.semaphore("fin_" + name))

    fetched = [sem(f"fetched{g}") for g in range(NG)]
    done, stored = sem("done"), sem("stored")

    def size(b):
        return P if b < NB - 1 else NTAIL
    with nc.Block() as block:
        @block.gpsimd
        def _(g):
            for b in range(NB):
                n = size(b)
                g.indirect_dma_start(m.h[0:n, b, :], None, io["slots_out"],
                                     bass.IndirectOffsetOnAxis(ap=m.slot_of[0:n, b:b + 1], axis=0)
                                     ).then_inc(fetched[b // GB], 16)

        @block.vector
        def _(v):
            for g in range(NG):
                v.wait_ge(fetched[g], 16 * GB)
                for b in range(g * GB, (g + 1) * GB):
                    n = size(b)
                    v.scalar_tensor_tensor(out=m.x[0:n, b, :], in0=m.h[0:n, b, :], scalar=m.best[0:n, b:b + 1],
                                           in1=m.x[0:n, b, :], op0=ALU.mult, op1=ALU.add).then_inc(done, 1)

        @block.sync
        def _(sp):
            for g in range(NG):
                sp.wait_ge(done, GB * (g + 1))
                lo, hi = g * GB, min((g + 1) * GB, NB - 1)
                sp.dma_start(io["out"][lo * P:hi * P, :].rearrange("(b p) d -> p b d", p=P), m.x[:, lo:hi, :]
                             ).then_inc(stored, 16)
            sp.dma_start(io["out"][(NB - 1) * P:N, :], m.x[0:NTAIL, NB - 1, :]).then_inc(stored, 16)
            sp.wait_ge(stored, 16 * (NG + 1))


def program(nc, io):
    with ExitStack() as ctx:
        m = allocate(nc, ctx)

        def bcast(t):
            n = t.shape[0]
            return t.rearrange("(o d) -> o d", o=1).broadcast_to([P, n])

        def phase(build, *args, **named):
            build(nc, ctx, m, io, *args, **named)
        phase(prepare)
        phase(layernorm, "n0_", use="G", full=False, table=io["g_table"])
        phase(sweep, 0)
        phase(aggregate)
        phase(layernorm, "n1_", use="gates", loads=[
            (m.gW, io["gW"].rearrange("(c p) e -> p c e", p=P)), (m.gb, bcast(io["gb"])),
            (m.sW1, io["sW1"].rearrange("(c p) h -> p c h", p=P)), (m.sW2, io["sW2"].rearrange("(c p) h -> p c h", p=P)),
            (m.sW3, io["sW3"]), (m.eW2, io["eW2"].rearrange("e p h -> p e h")),
            (m.eW3, io["eW3q"].rearrange("q p d -> p q d")),
            (m.b1, io["b1T"]), (m.b2, io["b2T"]),
            (m.b3[0:NE0, :], io["eb3"]), (m.b3[NE0:NE0 + 1, :], io["sb3"].rearrange("(o d) -> o d", o=1)),
        ] + [(m.eW1[:, e, :, :], io["eW1"][e].rearrange("(c p) h -> p c h", p=P)) for e in range(NE0)])
        phase(top_two)
        phase(ffn0)
        phase(layernorm, "n2_", keep=True, table=io["h_table"])
        phase(sweep, 1)
        phase(gru)
        phase(layernorm, "n3_", keep=True, loads=[
            (m.W1, io["W1"].rearrange("(c p) h -> p c h", p=P)), (m.Wg, io["Wg"].rearrange("(c p) e -> p c e", p=P)),
            (m.bg, bcast(io["bg"])), (m.bf1, io["bf1T"]),
            (m.bd, io["bd"].rearrange("(o e) d -> o e d", o=1).broadcast_to([P, NE1, D])),
        ] + [(m.Wd[:, e, :, :], io["Wd"][e].rearrange("(c p) d -> p c d", p=P)) for e in range(NE1)])
        phase(hidden)
        phase(route)
        phase(experts)
        phase(finish)


def kernel(**inputs):
    import numpy as np
    import concourse.bacc as bacc
    from concourse.bass_utils import run_bass_kernel_spmd as run

    a = {k: np.asarray(v) for k, v in inputs.items()}
    full = (ET - 1) * P

    def tiles(e):
        return e[:full].reshape(ET - 1, P).T

    def columns(b):
        return b.reshape(-1, P).T
    host = {
        "x": a["x"], "src": a["src"], "dst": a["dst"], "t8": a["edge_type_8"], "t16": a["edge_type_16"],
        "src_main": tiles(a["src"]), "dst_main": tiles(a["dst"]), "t8_main": tiles(a["edge_type_8"]),
        "t16_main": tiles(a["edge_type_16"]),
        "basis": a["L0_gnn_basis"].reshape(R8 * P, D), "w_comp": a["L0_gnn_w_comp"], "gnn_bias": a["L0_gnn_bias"],
        "sW1": a["L0_ffn_sW1"], "sW2": a["L0_ffn_sW2"], "sW3": a["L0_ffn_sW3"], "sb3": a["L0_ffn_sb3"],
        "eW1": a["L0_ffn_eW1"], "eW2": a["L0_ffn_eW2"], "eW3q": a["L0_ffn_eW3"].reshape(2, P, D), "eb3": a["L0_ffn_eb3"],
        "b1T": np.concatenate([columns(a["L0_ffn_sb1"]), columns(a["L0_ffn_eb1"])], 1),
        "b2T": np.concatenate([columns(a["L0_ffn_sb2"]), columns(a["L0_ffn_eb2"])], 1),
        "gW": a["L0_ffn_gW"], "gb": a["L0_ffn_gb"],
        "rel": a["L1_gnn_relvectors"], "w_ihT": a["L1_gnn_w_ih"].T, "w_hhT": a["L1_gnn_w_hh"].T,
        "b_ihT": columns(a["L1_gnn_b_ih"]), "b_hhT": columns(a["L1_gnn_b_hh"]),
        "W1": a["L1_ffn_W1"], "bf1T": columns(a["L1_ffn_b1"]), "Wg": a["L1_ffn_Wg"], "bg": a["L1_ffn_bg"],
        "Wd": a["L1_ffn_Wd"], "bd": a["L1_ffn_bd"],
    }
    host = {k: np.ascontiguousarray(v) for k, v in host.items()}
    nc = bacc.Bacc("TRN2", target_bir_lowering=False, num_devices=1)
    io = {k: nc.dram_tensor("in_" + k, v.shape, mybir.dt.from_np(v.dtype), kind="ExternalInput").ap()
          for k, v in host.items()}
    io["out"] = nc.dram_tensor("out_x", (N, D), F32, kind="ExternalOutput").ap()
    for name, shape in (("g_table", (NP, P)), ("h_table", (NP, D)), ("slots_in", (SLOTS, D)),
                        ("slots_out", (SLOTS, D))):
        io[name] = nc.dram_tensor(name, shape, F32).ap()
    program(nc, io)
    r = run(nc, [{"in_" + k: v for k, v in host.items()}], core_ids=[0])
    return r.results[0]["out_x"]
```

```python
from contextlib import ExitStack

import concourse.bass as bass
from concourse import mybir

F32 = mybir.dt.float32
I32 = mybir.dt.int32
U32 = mybir.dt.uint32
ALU = mybir.AluOpType
ACT = mybir.ActivationFunctionType
AX = mybir.AxisListType

P = 128
N, D, E = 3125, 256, 50000
NB = -(-N // P)
NTAIL = N - (NB - 1) * P
NP = NB * P
GB = 5
NG = NB // GB
GN = GB * P
HALF = GN // 2
EP = 125
ET = E // EP
UNR = 16
NIT = ET // UNR
SG = 4
NSG = ET // SG
PG = UNR // SG
PART = UNR // 2
WIN = 16
GWIN = 48
ACCW0, ACCW1 = NP + WIN, NP + GWIN
REGION = 8 * ACCW0
NONE = 1.0e6
R8, R16, NBASE = 8, 16, 4
NE0, NE1 = 4, 8
HID = 1024
MH = HID // P
TILES = (N + NE1 * (P - 1)) // P
SLOTS = TILES * P
EPS = 1e-5
assert EP * ET == E and UNR * NIT == ET and NIT == NB and GB * NG == NB and TILES % 8 == 0


class Level:

    def __init__(self, eng, name, start=0):
        self.eng, self.reg = eng, eng.alloc_register(name)
        eng.reg_mov(self.reg, start)

    def up(self, n=1):
        self.eng.reg_add(self.reg, self.reg, n)
        return self.reg


def one(b):
    return bass.ds(b, 1)


def allocate(nc, ctx):
    def sb(name, shape, dt=F32):
        return ctx.enter_context(nc.sbuf_tensor(name, shape, dt))

    class M:
        pass

    m = M()
    m.x = sb("x", [P, NB, D])
    m.hT = sb("hT", [P, 2, NP])
    m.h = sb("h", [P, NB, D])
    m.region = sb("region", [P, REGION])
    m.hn = sb("hn", [P, GB, D])
    m.tT = sb("tT", [P, GB, 2, P])
    m.ident = sb("ident", [P, P])
    m.iota = sb("iota", [P, P])
    m.ones = sb("ones", [P, P])
    m.mv = sb("mv", [P, NB, 2])
    m.stats = sb("stats", [P, NB, 6])
    m.std = sb("std", [P, NB])
    m.rstd = sb("rstd", [P, NB])
    m.src = sb("src", [EP, ET], I32)
    m.src_now = sb("src_now", [EP, UNR], I32)
    m.dst0 = sb("dst0", [EP, ET])
    m.dst = sb("dst", [EP, ET])
    m.type8 = sb("type8", [EP, ET])
    m.type16 = sb("type16", [EP, ET])
    m.base = sb("base", [P, ET + NSG])
    m.first_row = sb("first_row", [1, ET + NSG], I32)
    m.base_row = sb("base_row", [1, ET], I32)
    m.key = sb("key", [EP, ET])
    m.valid = sb("valid", [EP, ET])
    m.cmat = sb("cmat", [P, 64])
    m.wincol = sb("wincol", [EP, 1])
    m.hrow = sb("hrow", [P, D])[:, :]
    m.rounds = sb("rounds", [1, 2], I32)
    m.ps = ctx.enter_context(nc.psum_tensor("ps", [P, 8, 512], F32))

    def carve(whole, start, *shape):
        n = 1
        for s in shape:
            n *= s
        v = whole[:, start:start + n]
        names = "abcd"[:len(shape)]
        if len(shape) > 1:
            v = v.rearrange("p (" + " ".join(names) + ") -> p " + " ".join(names), **dict(zip(names, shape)))
        return v, start + n

    hflat = m.h[:, :, :].rearrange("p b d -> p (b d)")
    reg = m.region[:, :]
    m.acc0, _ = carve(reg, 0, R8, ACCW0)
    m.ring0, at = carve(hflat[0:EP], 0, UNR, P)
    m.hot0, at = carve(hflat[0:EP], at, UNR, P)
    m.sring, _ = carve(hflat, 0, GB, R8, P)
    m.gbuf = m.h[:, :, 0:P]
    m.basis, _ = carve(m.hT[:, :, :].rearrange("p a n -> p (a n)"), 0, R8, D)
    m.sW1, at = carve(reg, 0, 2, 256)
    m.sW2, at = carve(reg, at, 2, 128)
    m.sW3, at = carve(reg, at, 256)
    m.eW1, at = carve(reg, at, NE0, 2, 128)
    m.eW2, at = carve(reg, at, NE0, 64)
    m.eW3, at = carve(reg, at, 2, 256)
    m.gW, at = carve(reg, at, 2, NE0)
    m.gb, at = carve(reg, at, NE0)
    m.b1, at = carve(reg, at, 6)
    m.b2, at = carve(reg, at, 3)
    m.b3, at = carve(reg, at, 256)
    m.logit0, at = carve(reg, at, NB, NE0)
    m.gate0, at = carve(reg, at, 12, NB * NE0)
    m.w0, at = carve(reg, at, NB, NE0)
    m.wst, at = carve(reg, at, GB, NE0)
    m.wT, at = carve(reg, at, GN)
    m.sel, at = carve(reg, at, 2, P)
    m.a1, at = carve(reg, at, 6, GN)
    m.a2, at = carve(reg, at, 3, GN)
    m.bias0, at = carve(reg, at, 256)
    assert at <= REGION
    m.acc1, at = carve(reg, 0, 3, ACCW1)
    m.ring1, at = carve(reg[0:EP], at, UNR, D)
    m.hot_type, at = carve(reg[0:EP], at, UNR, R16)
    m.hot1, at = carve(reg[0:EP], at, UNR, GWIN)
    m.wih, at = carve(reg, at, 2, 768)
    m.whh, at = carve(reg, at, 2, 768)
    m.rel, at = carve(reg, at, D)
    m.bih, at = carve(reg, at, 6)
    m.bhh, at = carve(reg, at, 6)
    m.brz, third = carve(reg, at, 4)
    m.Wd, at = carve(reg, 0, NE1, MH, D)
    m.bd, at = carve(reg, at, NE1, D)
    assert third <= at
    m.W1, at = carve(reg, at, 2, HID)
    m.Wg, at = carve(reg, at, MH, NE1)
    m.bg, at = carve(reg, at, NE1)
    m.bf1, at = carve(reg, at, MH)
    m.rz, at2 = carve(reg, at, 2, 2, P)
    m.gt, at2 = carve(reg, at2, 2, P)
    m.gn, at2 = carve(reg, at2, 2, P)
    m.H0, at2 = carve(reg, at2, MH, P)
    assert at2 <= REGION and at + MH * 4 * P <= REGION
    m.HQ = [carve(reg, at, MH, 4 * P)[0], carve(m.hT[:, :, :].rearrange("p a n -> p (a n)"), 0, MH, 4 * P)[0]]
    m.hTQ = carve(m.hT[:, :, :].rearrange("p a n -> p (a n)"), MH * 4 * P, 2, 4 * P)[0]
    m.slots = [carve(hflat, i * 4 * D, 4, D)[0] for i in range(2)]
    m.results = [carve(hflat, (2 + i) * 4 * D, 4, D)[0] for i in range(2)]
    small = m.hn[:, :, :].rearrange("p b d -> p (b d)")
    m.logit1, at = carve(small, 0, NB, NE1)
    m.prob1, at = carve(small, at, NB, NE1)
    m.pick, at = carve(small, at, NB, NE1)
    m.before, at = carve(small, at, NB, NE1)
    m.cum, at = carve(small, at, NE1, NB)
    m.tmp1, at = carve(small, at, NB, NE1)
    small = m.tT[:, :, :, :].rearrange("p b c d -> p (b c d)")
    m.tri, at = carve(small, 0, P)
    m.tmp2, at = carve(small, at, TILES, NE1)
    m.tot, at = carve(small, at, NE1, NB)
    m.best, at = carve(small, at, NB)
    m.col1, at = carve(small, at, NB)
    m.posf, at = carve(small, at, NB)
    m.slot_of, at = carve(small, at, NB)
    m.slot_of = m.slot_of.bitcast(I32)
    m.steps, at = carve(small, at, NB)
    m.ntiles, at = carve(small, at, NE1)
    m.ends, at = carve(small, at, NE1)
    m.starts, at = carve(small, at, NE1)
    m.padmask, at = carve(small, at, NE1)
    m.ofTf, at = carve(small, at, TILES)
    m.ofT, at = carve(small, at, TILES)
    m.ofT = m.ofT.bitcast(I32)
    assert at <= GB * 2 * P
    return m


def prepare(nc, ctx, m, io):
    def sem(name):
        return ctx.enter_context(nc.semaphore(name))

    in_x, in_src, in_edges, in_dstrow, in_comp = (sem("in_" + s) for s in ("x", "src", "edges", "dstrow", "comp"))
    zeroed, z_out, pads, pool_step, v_step, bc_ready, fl_ready = (
        sem(s) for s in ("zeroed", "z_out", "pads", "pool_step", "v_step", "bc_ready", "fl_ready"))
    hflat = m.h[:, :, :].rearrange("p b d -> p (b d)")
    hTflat = m.hT[:, :, :].rearrange("p a n -> p (a n)")
    stage = hflat[0:EP, 0:3 * ET].rearrange("p (a t) -> p a t", a=3).bitcast(I32)
    rows = hTflat[0:NSG, 0:SG * EP].bitcast(I32)
    rows_f = hTflat[0:NSG, 500:500 + SG * EP].rearrange("p (k e) -> p k e", k=SG)
    lows = hTflat[0:NSG, 1024:1024 + SG + 1]
    diag = hTflat[0:NSG, 1100:1100 + (SG + 1) * NSG].rearrange("p (k g) -> p k g", k=SG + 1)
    over = hTflat[0:EP, 1700:1701]
    over_t = hTflat[0:EP, 1800:1800 + 2 * ET + NSG]
    limit = hTflat[0:EP, 2800:2800 + ET]
    flag = hTflat[0:1, 3300:3301]
    spare = hTflat[0:1, 3302:3302 + ET + NSG]
    flagr = hTflat[0:1, 3301:3302]
    m.comp_rep = hTflat[:, 4000:4004]
    with nc.Block() as block:
        @block.sync
        def _(sp):
            sp.dma_start(rows, io["dst_groups"]).then_inc(in_dstrow, 16)
            for k, name in enumerate(("dst", "t8", "t16")):
                sp.dma_start(stage[:, k, :], io[name]).then_inc(in_edges, 16)
            sp.dma_start(m.src[:, :], io["src"]).then_inc(in_src, 16)
            sp.wait_ge(zeroed, 1)
            sp.dma_start(io["slots_in"].rearrange("(p r) c -> p (r c)", p=P), m.region[:, 0:TILES * D]
                         ).then_inc(z_out, 16)
            sp.wait_ge(z_out, 16)
            sp.wait_ge(in_x, 32)
            sp.wait_ge(in_src, 16)

        @block.scalar
        def _(act):
            act.dma_start(m.x[:, 0:NB - 1, :], io["x"][0:(NB - 1) * P, :].rearrange("(b p) d -> p b d", p=P)
                          ).then_inc(in_x, 16)
            act.wait_ge(pads, 1)
            act.dma_start(m.x[0:NTAIL, NB - 1, :], io["x"][(NB - 1) * P:N, :]).then_inc(in_x, 16)
            act.dma_start(m.comp_rep, io["w_comp"].rearrange("(o r) b -> o r b", o=1).broadcast_to(
                [P // R8, R8, NBASE])).then_inc(in_comp, 16)

        @block.gpsimd
        def _(g):
            g.memset(m.ident[:, :], 0.0).then_inc(pool_step, 1)
            g.memset(m.ones[:, :], 1.0).then_inc(pool_step, 1)
            g.memset(m.x[:, NB - 1, :], 0.0).then_inc(pads, 1)
            g.iota(m.iota[:, :], pattern=[[1, P]], base=0, channel_multiplier=0,
                   allow_small_or_imprecise_dtypes=True).then_inc(pool_step, 1)
            g.wait_ge(pool_step, 3)
            g.affine_select(out=m.ident[:, :], in_=m.ident[:, :], compare_op=ALU.not_equal, fill=1.0, base=0,
                            pattern=[[-1, P]], channel_multiplier=1).then_inc(pool_step, 1)
            g.iota(limit.rearrange("p (i t) -> p i t", t=UNR), pattern=[[P, NIT], [0, UNR]], base=-P,
                   channel_multiplier=0, allow_small_or_imprecise_dtypes=True).then_inc(pool_step, 1)
            g.memset(m.region[:, :], 0.0).then_inc(zeroed, 1)

        @block.vector
        def _(v):
            v.memset(m.wincol[:, :], 0.0).then_inc(v_step, 1)
            v.wait_ge(in_dstrow, 16)
            v.tensor_copy(rows_f, rows.rearrange("p (k e) -> p k e", k=SG)).then_inc(v_step, 1)
            v.wait_ge(v_step, 2)
            v.tensor_reduce(lows[:, 0:SG], rows_f, AX.X, ALU.min).then_inc(v_step, 1)
            v.wait_ge(v_step, 3)
            v.tensor_reduce(lows[:, SG:SG + 1], lows[:, 0:SG], AX.X, ALU.min).then_inc(v_step, 1)
            v.wait_ge(v_step, 4)
            v.wait_ge(pool_step, 5)
            for k in range(SG + 1):
                v.tensor_scalar(diag[:, k, :], m.ident[0:NSG, 0:NSG], lows[:, k:k + 1], None, ALU.mult
                                ).then_inc(v_step, 1)
            v.wait_ge(in_edges, 16 * 3)
            v.tensor_copy(m.dst0[:, :], stage[:, 0, :]).then_inc(v_step, 1)
            v.tensor_copy(m.type8[:, :], stage[:, 1, :]).then_inc(v_step, 1)
            v.tensor_copy(m.type16[:, :], stage[:, 2, :]).then_inc(v_step, 1)
            v.wait_ge(bc_ready, 1)
            v.tensor_copy(m.base[:, 0:ET].rearrange("p (g k) -> p k g", k=SG),
                          m.ps[:, 0, 0:ET].rearrange("p (k g) -> p k g", k=SG)).then_inc(v_step, 1)
            v.tensor_copy(m.base[:, ET:ET + NSG], m.ps[:, 0, ET:ET + NSG]).then_inc(v_step, 1)
            v.wait_ge(v_step, 14)
            v.tensor_tensor(over_t[:, 0:ET], m.dst0[:, :], m.base[0:EP, 0:ET], ALU.subtract).then_inc(v_step, 1)
            v.tensor_tensor(over_t[:, ET:2 * ET].rearrange("p (g k) -> p g k", k=SG),
                            m.dst0[:, :].rearrange("p (g k) -> p g k", k=SG),
                            m.base[0:EP, ET:ET + NSG].rearrange("p (g o) -> p g o", o=1).broadcast_to([EP, NSG, SG]),
                            ALU.subtract).then_inc(v_step, 1)
            v.tensor_tensor(limit, m.base[0:EP, 0:ET], limit, ALU.is_lt).then_inc(v_step, 1)
            v.wait_ge(v_step, 17)
            v.tensor_scalar(over_t[:, 0:ET], over_t[:, 0:ET], float(WIN), None, ALU.is_ge).then_inc(v_step, 1)
            v.tensor_scalar(over_t[:, ET:2 * ET], over_t[:, ET:2 * ET], float(GWIN), None, ALU.is_ge).then_inc(v_step, 1)
            v.wait_ge(v_step, 19)
            v.tensor_tensor(over_t[:, 0:ET], over_t[:, 0:ET], limit, ALU.max).then_inc(v_step, 1)
            v.wait_ge(v_step, 20)
            v.tensor_reduce(over, over_t[:, 0:2 * ET], AX.X, ALU.max).then_inc(v_step, 1)
            v.wait_ge(fl_ready, 1)
            v.tensor_reduce(flag, m.ps[0:1, 1, 0:EP], AX.X, ALU.max).then_inc(v_step, 1)
            v.wait_ge(v_step, 22)
            for layer, width in enumerate((WIN, GWIN)):
                v.tensor_scalar(m.rounds[:, layer:layer + 1], flag, float(-(-N // width)), None, ALU.mult
                                ).then_inc(v_step, 1)
            v.tensor_scalar(flagr, flag, -1.0, 1.0, ALU.mult, ALU.add).then_inc(v_step, 1)
            v.tensor_scalar(flag, flag, float(NP), None, ALU.mult).then_inc(v_step, 1)
            v.wait_ge(v_step, 26)
            v.tensor_scalar(spare, m.base[0:1, :], flagr, flag, ALU.mult, ALU.add).then_inc(v_step, 1)
            v.wait_ge(v_step, 27)
            v.tensor_copy(m.first_row[:, :], spare).then_inc(v_step, 1)
            v.wait_ge(in_comp, 16)

        @block.tensor
        def _(pe):
            pe.wait_ge(v_step, 9)
            for k in range(SG + 1):
                mm = pe.matmul(m.ps[:, 0, k * NSG:(k + 1) * NSG], m.ones[0:NSG, :], diag[:, k, :], start=True, stop=True)
            mm.then_inc(bc_ready, 1)
            pe.wait_ge(v_step, 21)
            pe.transpose(m.ps[0:1, 1, 0:EP], over, m.ident[0:EP, 0:EP]).then_inc(fl_ready, 1)


def statistics(v, m, stat):
    with v.Fori(0, NB) as b:
        v.bn_stats(m.stats[:, one(b), :], m.x[:, one(b), :]).then_inc(stat, 1)
    v.wait_ge(stat, NB)
    mean, half_gap, dev = m.mv[:, :, 0], m.mv[:, :, 1], m.rstd[:, :]
    v.tensor_tensor(mean, m.stats[:, :, 1], m.stats[:, :, 4], ALU.add).then_inc(stat, 1)
    v.tensor_tensor(half_gap, m.stats[:, :, 1], m.stats[:, :, 4], ALU.subtract).then_inc(stat, 1)
    v.tensor_tensor(dev, m.stats[:, :, 2], m.stats[:, :, 5], ALU.add).then_inc(stat, 1)
    v.wait_ge(stat, NB + 3)
    v.tensor_scalar(mean, mean, 0.5, None, ALU.mult).then_inc(stat, 1)
    v.scalar_tensor_tensor(out=half_gap, in0=half_gap, scalar=0.25, in1=half_gap, op0=ALU.mult, op1=ALU.mult
                           ).then_inc(stat, 1)
    v.wait_ge(stat, NB + 5)
    v.scalar_tensor_tensor(out=dev, in0=dev, scalar=1.0 / D, in1=half_gap, op0=ALU.mult, op1=ALU.add
                           ).then_inc(stat, 1)
    v.wait_ge(stat, STATS - 1)
    v.tensor_scalar(m.std[:, :], dev, EPS, None, ALU.add).then_inc(stat, 1)


STATS = NB + 7


def layernorm(nc, ctx, m, io, tag, use=None, keep=False, full=True, loads=(), table=None):
    def sem(name):
        return ctx.enter_context(nc.semaphore(tag + name))

    stat, root, normed, turned, evacuated = (sem(s) for s in ("stat", "root", "normed", "turned", "evacuated"))
    used, made = (sem("used"), sem("made")) if use else (None, None)
    copied = sem("copied") if keep or full else None
    kept = sem("kept") if keep else None
    stored = sem("stored") if table is not None else None
    cmat = sem("cmat") if use == "G" else None
    loaded = sem("loaded") if loads else None
    cd = m.cmat[:, :]
    copies = keep or full
    out, width, prod = {"G": (m.gbuf, P, None), "gates": (m.logit0, NE0, None), None: (None, 0, None)}[use]
    first_waits = {"G": (cmat, 3), "gates": (loaded, 16 * len(loads))}.get(use)
    with nc.Block() as block:
        @block.vector
        def _(v):
            if use == "G":
                v.tensor_copy(cd.rearrange("p (k b) -> p k b", b=NBASE),
                              m.comp_rep.rearrange("p (o b) -> p o b", o=1).broadcast_to([P, 16, NBASE])
                              ).then_inc(cmat, 1)
            statistics(v, m, stat)
            v.wait_ge(root, 1)
            v.reciprocal(m.rstd[:, :], m.std[:, :]).then_inc(stat, 1)
            v.wait_ge(stat, STATS + 1)
            slot_turned, slot_copied = Level(v, tag + "slot_turned"), Level(v, tag + "slot_copied")

            def group(g, first):
                for j in range(GB):
                    if not first:
                        v.wait_ge(turned, slot_turned.up())
                    if not first and copies:
                        v.wait_ge(copied, slot_copied.up())
                    v.tensor_scalar(m.hn[:, j, :], m.x[:, one(g * GB + j), :], m.mv[:, one(g * GB + j), 0],
                                    m.rstd[:, one(g * GB + j)], ALU.subtract, ALU.mult).then_inc(normed, 1)
            group(0, True)
            with v.Fori(1, NG) as g:
                group(g, False)

        @block.tensor
        def _(pe):
            if first_waits:
                pe.wait_ge(*first_waits)
            in_hn, bank_free, in_tT, out_free = (Level(pe, tag + s) for s in ("in_hn", "bank_free", "in_tT", "out_free"))

            def group(first):
                for j in range(GB):
                    pe.wait_ge(normed, in_hn.up())
                    if not (first and j < 2):
                        pe.wait_ge(evacuated, bank_free.up())
                    for c in range(2):
                        t = pe.transpose(m.ps[:, (0, 1, 0, 1, 7)[j], c * P:(c + 1) * P], m.hn[:, j, c * P:(c + 1) * P],
                                         m.ident[:, :])
                    t.then_inc(turned, 1)
                for j in range(GB if use else 0):
                    pe.wait_ge(evacuated, in_tT.up())
                    if not first:
                        pe.wait_ge(made, out_free.up())
                    for c in range(2):
                        if use == "G":
                            q = pe.matmul(m.ps[:, 2 + j, c * 64:(c + 1) * 64], m.tT[:, j, c, :], cd,
                                          start=True, stop=True)
                        else:
                            q = pe.matmul(m.ps[:, 2 + j, 0:NE0], m.tT[:, j, c, :], m.gW[:, c, :],
                                          start=(c == 0), stop=(c == 1))
                    q.then_inc(used, 1)
            group(True)
            with pe.Fori(1, NG):
                group(False)

        @block.scalar
        def _(act):
            act.wait_ge(stat, STATS)
            act.activation(m.std[:, :], m.std[:, :], ACT.Sqrt).then_inc(root, 1)
            in_bank, slot_used, slot_copied, product = (
                Level(act, tag + s) for s in ("in_bank", "slot_used", "aslot_copied", "product"))

            def group(g, first):
                for j in range(GB):
                    act.wait_ge(turned, in_bank.up())
                    if not first and use:
                        act.wait_ge(used, slot_used.up())
                    if not first and copies:
                        act.wait_ge(copied, slot_copied.up())
                    act.activation(m.tT[:, j, :, :], m.ps[:, (0, 1, 0, 1, 7)[j], 0:2 * P].rearrange(
                        "p (c n) -> p c n", c=2), ACT.Copy).then_inc(evacuated, 1)
                for j in range(GB if use else 0):
                    act.wait_ge(used, product.up())
                    act.activation(out[:, one(g * GB + j), :], m.ps[:, 2 + j, 0:width].rearrange(
                        "p (o n) -> p o n", o=1), ACT.Copy).then_inc(made, 1)
            group(0, True)
            with act.Fori(1, NG) as g:
                group(g, False)

        @block.gpsimd
        def _(gp):
            if use == "G":
                gp.wait_ge(cmat, 1)
                gp.affine_select(out=cd, in_=cd, compare_op=ALU.is_ge, fill=0.0, base=0,
                                 pattern=[[-R8, 16], [0, NBASE]], channel_multiplier=1).then_inc(cmat, 1)
                gp.wait_ge(cmat, 2)
                gp.affine_select(out=cd, in_=cd, compare_op=ALU.is_ge, fill=0.0, base=R8 - 1,
                                 pattern=[[R8, 16], [0, NBASE]], channel_multiplier=-1).then_inc(cmat, 1)
            if copies:
                ready = Level(gp, tag + "ready")
                with gp.Fori(0, NG) as g:
                    for j in range(GB):
                        gp.wait_ge(evacuated, ready.up())
                        if keep:
                            gp.tensor_copy(m.h[:, one(g * GB + j), :], m.hn[:, j, :].rearrange("p (o d) -> p o d", o=1)
                                           ).then_inc(kept, 1)
                        gp.tensor_copy(m.hT[:, :, bass.ds((g * GB + j) * P, P)], m.tT[:, j, :, :]).then_inc(copied, 1)

        @block.sync
        def _(sp):
            for dst, src in loads:
                sp.dma_start(dst, src).then_inc(loaded, 16)
            sp.wait_ge(loaded, 16 * len(loads)) if loads else None
            if table is not None:
                src = m.gbuf if use == "G" else m.h
                done = made if use == "G" else copied
                for g in range(NG):
                    sp.wait_ge(done, GB * (g + 1))
                    sp.dma_start(table[g * GN:(g + 1) * GN, :].rearrange("(b p) q -> p b q", p=P),
                                 src[:, g * GB:(g + 1) * GB, :]).then_inc(stored, 16)
                sp.wait_ge(stored, 16 * NG)


class Sweep:

    def __init__(self, nc, ctx, m, io, layer):
        def sem(name):
            return ctx.enter_context(nc.semaphore(f"l{layer}_{name}"))

        self.nc, self.m, self.io, self.layer, self.tag = nc, m, io, layer, f"l{layer}_"
        self.ring, self.table = ((m.ring0, io["g_table"]), (m.ring1, io["h_table"]))[layer]
        self.width = (WIN, GWIN)[layer]
        self.adds = (SG, 2)[layer]
        self.key_step, self.hot, self.summed, self.added, self.cleared = (
            sem(s) for s in ("key_step", "hot", "summed", "added", "cleared"))
        self.src_ready = [sem(f"src_ready{p}") for p in range(2)]
        self.gathered = [sem(f"gathered{j}") for j in range(UNR)]

    def rounds(self, eng):
        return eng.value_load(self.m.rounds[:, self.layer:self.layer + 1], min_val=0, max_val=-(-N // WIN))

    def start_sync(self, sp):
        self.taken = Level(sp, self.tag + "taken", 16)
        for p in range(2):
            self.load_indices(sp, 0, p)

    def load_indices(self, sp, it, p):
        sp.dma_start(self.m.src_now[:, p * PART:(p + 1) * PART], self.m.src[:, bass.ds(it * UNR + p * PART, PART)]
                     ).then_inc(self.src_ready[p], 16)

    def indices(self, sp, it):
        for p in range(2):
            for j in range(p * PART, (p + 1) * PART):
                sp.wait_ge(self.gathered[j], self.taken.reg)
            self.load_indices(sp, it, p)
        self.taken.up(16)

    def start_gather(self, g):
        self.indexed = [Level(g, f"{self.tag}indexed{p}", 16) for p in range(2)]
        self.ring_free = Level(g, self.tag + "ring_free", PG // 2)

    def gather(self, g, p):
        g.wait_ge(self.src_ready[p], self.indexed[p].reg)
        self.indexed[p].up(16)
        g.wait_ge(self.summed, self.ring_free.reg)
        self.ring_free.up(PG // 2)
        for j in range(p * PART, (p + 1) * PART):
            g.indirect_dma_start(self.ring[:, j, :], None, self.table,
                                 bass.IndirectOffsetOnAxis(ap=self.m.src_now[:, j:j + 1], axis=0)
                                 ).then_inc(self.gathered[j], 16)

    def start_sums(self, pe):
        pe.sem_inc(self.summed, PG)
        names = ("hots", "landed", "bank_free")
        self.hots, self.landed, self.bank_free = (Level(pe, self.tag + s, n) for s, n in zip(names, (0, 0, self.adds)))

    def sums(self, pe, k):
        m, tiles = self.m, range(k * SG, (k + 1) * SG)
        if k == 0:
            self.landed.up(16)
        pe.wait_ge(self.added, self.bank_free.reg)
        self.bank_free.up(self.adds)
        if k % 2 == 0:
            pe.wait_ge(self.hot, self.hots.up(1 + self.layer))
        if self.layer == 0:
            for j in tiles:
                pe.wait_ge(self.gathered[j], self.landed.reg)
                mm = pe.matmul(m.ps[:, k % 2, (j % SG) * P:(j % SG + 1) * P], self.ring[:, j, :], m.hot0[:, j, :],
                               start=True, stop=True)
        else:
            for c in range(2):
                for j in tiles:
                    if c == 0:
                        pe.wait_ge(self.gathered[j], self.landed.reg)
                    pe.matmul(m.ps[:, k % 2, c * GWIN:(c + 1) * GWIN], self.ring[:, j, c * P:(c + 1) * P],
                              m.hot1[:, j, :], start=(j % SG == 0), stop=(j % SG == SG - 1))
            for j in tiles:
                mm = pe.matmul(m.ps[0:R16, k % 2, 2 * GWIN:3 * GWIN], m.hot_type[:, j, :], m.hot1[:, j, :],
                               start=(j % SG == 0), stop=(j % SG == SG - 1))
        mm.then_inc(self.summed, 1)

    def start_windows(self, v):
        m = self.m
        self.step, self.ready = Level(v, self.tag + "step", 1), Level(v, self.tag + "ready", PG + 1)
        self.own = Level(v, self.tag + "own", 2 * self.adds)
        v.memset(m.wincol[:, :], 0.0).then_inc(self.cleared, 1)
        v.tensor_copy(m.dst[:, :], m.dst0[:, :]).then_inc(self.added, 2 * self.adds)
        v.wait_ge(self.cleared, 1)
        v.wait_ge(self.added, 2 * self.adds)

    def keys(self, v, walk):
        m, width = self.m, self.width

        def link(ins):
            ins.then_inc(self.key_step, 1)
            v.wait_ge(self.key_step, self.step.reg)
            self.step.up()

        def by_group(t):
            return t.rearrange("p (g k) -> p g k", k=SG)
        key, valid, dst = m.key[:, :], m.valid[:, :], m.dst[:, :]
        if walk:
            link(v.tensor_scalar(key, dst, m.wincol[:, :], None, ALU.subtract))
            link(v.tensor_scalar(m.base_row[:, :], m.base[0:1, 0:ET], 0.0, m.wincol[0:1, :], ALU.mult, ALU.add))
        elif self.layer == 0:
            link(v.tensor_tensor(key, dst, m.base[0:EP, 0:ET], ALU.subtract))
            link(v.tensor_copy(m.base_row[:, :], m.first_row[:, 0:ET]))
        else:
            link(v.tensor_tensor(by_group(key), by_group(dst), m.base[0:EP, ET:].rearrange(
                "p (g o) -> p g o", o=1).broadcast_to([EP, NSG, SG]), ALU.subtract))
            link(v.tensor_copy(m.base_row[:, 0:NSG], m.first_row[:, ET:]))
        link(v.tensor_scalar(valid, key, 0.0, None, ALU.is_ge))
        link(v.scalar_tensor_tensor(out=valid, in0=key, scalar=float(width), in1=valid, op0=ALU.is_lt, op1=ALU.mult))
        if self.layer == 0:
            link(v.scalar_tensor_tensor(out=key, in0=m.type8[:, :], scalar=float(WIN), in1=key,
                                        op0=ALU.mult, op1=ALU.add))
        link(v.scalar_tensor_tensor(out=key, in0=key, scalar=1.0, in1=valid, op0=ALU.add, op1=ALU.mult))
        link(v.tensor_scalar(key, key, -1.0, None, ALU.add))
        if walk:
            link(v.scalar_tensor_tensor(out=dst, in0=valid, scalar=NONE, in1=dst, op0=ALU.mult, op1=ALU.add))
            link(v.tensor_scalar(m.wincol[:, :], m.wincol[:, :], float(width), None, ALU.add))

    def one_hots(self, v, it, p):
        m, a, b = self.m, p * PART, (p + 1) * PART

        def column(t):
            return t[:, bass.ds(it * UNR + a, PART)].rearrange("p (t o) -> p t o", o=1)

        def row(w):
            return m.iota[0:EP, 0:w].rearrange("p (o w) -> p o w", o=1).broadcast_to([EP, PART, w])
        if self.layer == 0:
            v.tensor_tensor(m.hot0[:, a:b, :], row(P), column(m.key).broadcast_to([EP, PART, P]), ALU.is_equal
                            ).then_inc(self.hot, 1)
        else:
            v.tensor_tensor(m.hot1[:, a:b, :], row(GWIN), column(m.key).broadcast_to([EP, PART, GWIN]), ALU.is_equal
                            ).then_inc(self.hot, 1)
            v.tensor_tensor(m.hot_type[:, a:b, :], row(R16), column(m.type16).broadcast_to([EP, PART, R16]),
                            ALU.is_equal).then_inc(self.hot, 1)

    def windows(self, v, it, p):
        m = self.m
        per = SG if self.layer == 0 else 1
        n = per * PG // 2
        _, at = self.nc.values_load_multi_w_load_instructions(
            m.base_row[0:1, bass.ds(it * 2 * n + p * n, n)], engines=[mybir.EngineType.DVE], min_val=0, max_val=NP,
            skip_runtime_bounds_check_because="a window starts at a node or at the padding")
        for i in range(n):
            bank = i // per
            if i % per == 0:
                v.wait_ge(self.summed, self.ready.reg)
                self.ready.up()
            v.wait_ge(self.added, self.own.reg)
            if self.layer == 0:
                self.own.up()
                win = m.acc0[:, :, bass.ds(at[i], WIN)]
                v.tensor_tensor(win, win, m.ps[:, bank, (i % SG) * P:(i % SG + 1) * P].rearrange(
                    "p (k w) -> p k w", k=R8), ALU.add).then_inc(self.added, 1)
            else:
                self.own.up(2)
                win = m.acc1[:, 0:2, bass.ds(at[i], GWIN)]
                v.tensor_tensor(win, win, m.ps[:, bank, 0:2 * GWIN].rearrange("p (k w) -> p k w", k=2), ALU.add
                                ).then_inc(self.added, 1)
                win = m.acc1[0:R16, 2, bass.ds(at[i], GWIN)]
                v.tensor_tensor(win, win, m.ps[0:R16, bank, 2 * GWIN:3 * GWIN], ALU.add).then_inc(self.added, 1)

    def walk_sync(self, sp):
        rounds = self.rounds(sp)
        with sp.If(rounds > 0):
            with sp.Fori(0, rounds):
                with sp.Fori(1, NIT) as it:
                    self.indices(sp, it)
                self.indices(sp, 0)

    def walk_gather(self, g):
        rounds = self.rounds(g)
        with g.If(rounds > 0):
            with g.Fori(0, rounds):
                with g.Fori(0, NIT):
                    for p in range(2):
                        self.gather(g, p)

    def walk_sums(self, pe):
        rounds = self.rounds(pe)
        with pe.If(rounds > 0):
            with pe.Fori(0, rounds):
                with pe.Fori(0, NIT):
                    for k in range(PG):
                        self.sums(pe, k)

    def walk_windows(self, v):
        rounds = self.rounds(v)
        with v.If(rounds > 0):
            with v.Fori(0, rounds):
                self.keys(v, walk=True)
                with v.Fori(0, NIT) as it:
                    for p in range(2):
                        self.one_hots(v, it, p)
                    for p in range(2):
                        self.windows(v, it, p)


def messages0(nc, ctx, m, io):
    loaded = ctx.enter_context(nc.semaphore("basis_in"))
    s = Sweep(nc, ctx, m, io, 0)
    with nc.Block() as block:
        @block.sync
        def _(sp):
            sp.dma_start(m.basis, io["basis"].rearrange("(r p) d -> p r d", p=P)).then_inc(loaded, 16)
            s.start_sync(sp)
            s.walk_sync(sp)
            with sp.Fori(1, NIT) as it:
                s.indices(sp, it)
            sp.wait_ge(loaded, 16)

        @block.gpsimd
        def _(g):
            s.start_gather(g)
            s.walk_gather(g)
            with g.Fori(0, NIT):
                for p in range(2):
                    s.gather(g, p)

        @block.tensor
        def _(pe):
            s.start_sums(pe)
            s.walk_sums(pe)
            with pe.Fori(0, NIT):
                for k in range(PG):
                    s.sums(pe, k)

        @block.vector
        def _(v):
            s.start_windows(v)
            s.walk_windows(v)
            s.keys(v, walk=False)
            for p in range(2):
                s.one_hots(v, 0, p)
            s.windows(v, 0, 0)
            with v.Fori(1, NIT) as it:
                s.one_hots(v, it, 0)
                s.windows(v, it - 1, 1)
                s.one_hots(v, it, 1)
                s.windows(v, it, 0)
            s.windows(v, NIT - 1, 1)


def aggregate(nc, ctx, m, io):
    def sem(name):
        return ctx.enter_context(nc.semaphore("agg_" + name))

    loaded, copied, multiplied, read, biased, summed = (
        sem(s) for s in ("loaded", "copied", "multiplied", "read", "biased", "summed"))
    with nc.Block() as block:
        @block.sync
        def _(sp):
            sp.dma_start(m.hrow, io["gnn_bias"].rearrange("(o d) -> o d", o=1).broadcast_to([P, D])
                         ).then_inc(loaded, 16)
            sp.wait_ge(loaded, 16)

        @block.scalar
        def _(act):
            free = Level(act, "agg_free")

            def group(g, first):
                for j in range(GB):
                    if not first:
                        act.wait_ge(multiplied, free.up())
                    act.activation(m.sring[:, j, :, :], m.acc0[:, :, bass.ds((g * GB + j) * P, P)], ACT.Copy
                                   ).then_inc(copied, 1)
            group(0, True)
            with act.Fori(1, NG) as g:
                group(g, False)

        @block.tensor
        def _(pe):
            ready, free = Level(pe, "agg_ready"), Level(pe, "agg_bank_free")

            def group(first):
                for j in range(GB):
                    pe.wait_ge(copied, ready.up())
                    if not first:
                        pe.wait_ge(read, free.up())
                    for r in range(R8):
                        mm = pe.matmul(m.ps[:, j, 0:D], m.sring[:, j, r, :], m.basis[:, r, :],
                                       start=(r == 0), stop=(r == R8 - 1))
                    mm.then_inc(multiplied, 1)
            group(True)
            with pe.Fori(1, NG):
                group(False)

        @block.vector
        def _(v):
            v.wait_ge(loaded, 16)
            ready, own = Level(v, "agg_product"), Level(v, "agg_biased")
            with v.Fori(0, NG) as g:
                for j in range(GB):
                    v.wait_ge(multiplied, ready.up())
                    v.tensor_tensor(m.hn[:, j, :], m.ps[:, j, 0:D], m.hrow, ALU.add).then_inc(read, 1)
                    v.wait_ge(read, own.up())
                    xb = m.x[:, one(g * GB + j), :]
                    v.scalar_tensor_tensor(out=xb, in0=m.hn[:, j, :].rearrange("p (o d) -> p o d", o=1), scalar=0.0,
                                           in1=xb, op0=ALU.max, op1=ALU.add).then_inc(summed, 1)


def top_two(nc, ctx, m, io):
    def sem(name):
        return ctx.enter_context(nc.semaphore("top_" + name))

    v_step, a_step = sem("v_step"), sem("a_step")
    n = NB * NE0
    logit, w = m.logit0, m.w0
    scr = [m.gate0[:, i, :] for i in range(12)]

    def be(t):
        return t.rearrange("p (b e) -> p b e", e=NE0)
    prob, comp, rank = be(scr[0]), m.gate0[:, 1:5, :], m.gate0[:, 5, :]
    col, shifted, chosen, exps = m.gate0[:, 6, 0:NB], be(scr[7]), be(scr[8]), be(scr[9])

    def spread(c):
        return c.rearrange("p (b o) -> p b o", o=1).broadcast_to([P, NB, NE0])
    with nc.Block() as block:
        @block.vector
        def _(v):
            count = [0]

            def link(ins):
                count[0] += 1
                ins.then_inc(v_step, 1)
                v.wait_ge(v_step, count[0])

            def softmax_head(src):
                link(v.tensor_reduce(col, src, AX.X, ALU.max))
                link(v.tensor_tensor(shifted, src, spread(col), ALU.subtract))

            def softmax_tail(dst, src):
                link(v.tensor_reduce(col, src, AX.X, ALU.add))
                link(v.reciprocal(col, col))
                link(v.tensor_tensor(dst, src, spread(col), ALU.mult))

            link(v.tensor_tensor(logit, logit, m.gb.rearrange("p (o e) -> p o e", o=1).broadcast_to([P, NB, NE0]),
                                 ALU.add))
            softmax_head(logit)
            v.wait_ge(a_step, 1)
            softmax_tail(prob, exps)
            link(v.memset(comp, 0.0))
            for e in range(NE0):
                ce = be(comp[:, e, :])
                for lo, hi, op in ((0, e, ALU.is_ge), (e + 1, NE0, ALU.is_gt)):
                    if hi > lo:
                        link(v.tensor_tensor(ce[:, :, lo:hi], prob[:, :, lo:hi],
                                             prob[:, :, e:e + 1].broadcast_to([P, NB, hi - lo]), op))
            link(v.tensor_reduce(rank, comp.rearrange("p e (b f) -> p (e b) f", f=NE0), AX.X, ALU.add))
            link(v.tensor_scalar(chosen.rearrange("p b e -> p e b"), rank.rearrange("p (e b) -> p e b", e=NE0),
                                 2.0, None, ALU.is_lt))
            softmax_head(prob)
            v.wait_ge(a_step, 2)
            link(v.tensor_tensor(exps, exps, chosen, ALU.mult))
            softmax_tail(w, exps)
            top_two.steps = count[0]

        @block.scalar
        def _(act):
            act.wait_ge(v_step, 3)
            act.activation(exps, shifted, ACT.Exp).then_inc(a_step, 1)
            act.wait_ge(v_step, 3 + 3 + 1 + 2 * (NE0 - 1) + 2 + 2)
            act.activation(exps, shifted, ACT.Exp).then_inc(a_step, 1)


def ffn0(nc, ctx, m, io):
    def sem(name):
        return ctx.enter_context(nc.semaphore("f0_" + name))

    staged, task, a_read, wb_task, weighted, out_task, o_read, setup = (
        sem(s) for s in ("staged", "task", "a_read", "wb_task", "weighted", "out_task",
                         "o_read", "setup"))
    NA = 3 + 12 + 6
    TURNS = ((0, 2), (2, 4), (4, 5))

    def half(h):
        return slice(h * HALF, (h + 1) * HALF)
    with nc.Block() as block:
        @block.gpsimd
        def _(g):
            g.memset(m.sel[0:NE0, :, :], 1.0).then_inc(setup, 1)
            g.memset(m.wT[0:NE0 + 1, :], 1.0).then_inc(setup, 1)
            sel = m.sel[0:NE0, :, :].rearrange("e q c -> e (q c)")
            g.wait_ge(setup, 2)
            g.affine_select(out=sel, in_=sel, compare_op=ALU.is_ge, fill=0.0, base=0, pattern=[[1, 2 * P]],
                            channel_multiplier=-64).then_inc(setup, 1)
            g.wait_ge(setup, 3)
            g.affine_select(out=sel, in_=sel, compare_op=ALU.is_ge, fill=0.0, base=63, pattern=[[-1, 2 * P]],
                            channel_multiplier=64).then_inc(setup, 1)
            turned = Level(g, "f0_turned", 3)
            g.tensor_copy(m.wst, m.w0[:, 0:GB, :]).then_inc(staged, 1)
            with g.Fori(1, NG) as i:
                g.wait_ge(a_read, turned.reg)
                turned.up(NA)
                g.tensor_copy(m.wst, m.w0[:, bass.ds(i * GB, GB), :]).then_inc(staged, 1)

        @block.tensor
        def _(pe):
            pe.wait_ge(setup, 4)
            stage, banks, evac, wfree, wted, ofree = (
                Level(pe, "f0_" + s) for s in ("stage", "banks", "evac", "wfree", "wted", "ofree"))

            def group(g, first):
                k = 0

                def bank():
                    nonlocal k
                    if not (first and k < 3):
                        pe.wait_ge(a_read, banks.up())
                    k += 1
                    return (k - 1) % 3

                pe.wait_ge(staged, stage.up())
                for a, b in TURNS:
                    t = bank()
                    for j in range(a, b):
                        mm = pe.transpose(m.ps[0:NE0, t, (j - a) * P:(j - a + 1) * P], m.wst[:, j, :], m.ident[:, :])
                    mm.then_inc(task, 1)
                for i in range(6):
                    for h in range(2):
                        t = bank()
                        for c in range(2):
                            w = m.sW1[:, c, i * P:(i + 1) * P] if i < 2 else m.eW1[:, i - 2, c, :]
                            mm = pe.matmul(m.ps[:, t, 0:HALF], w, m.hT[:, c, bass.ds(g * GN + h * HALF, HALF)],
                                           start=(c == 0), stop=(c == 1))
                        mm.then_inc(task, 1)
                pe.wait_ge(a_read, evac.up(3))

                def spread(q):
                    for h in range(2):
                        if not (first and q == 0):
                            pe.wait_ge(weighted, wfree.up())
                        pe.matmul(m.ps[:, 3 + h, 0:HALF], m.sel[0:NE0, q, :], m.wT[0:NE0, half(h)],
                                  start=True, stop=True).then_inc(wb_task, 1)
                spread(0)
                pe.wait_ge(a_read, evac.up(12))
                for i in (1, 2, 0):
                    if i == 2:
                        spread(1)
                    for h in range(2):
                        t = bank()
                        if i == 0:
                            for c in range(2):
                                mm = pe.matmul(m.ps[:, t, 0:HALF], m.sW2[:, c, :], m.a1[:, c, half(h)],
                                               start=(c == 0), stop=(c == 1))
                        else:
                            for e in range(2):
                                x = 2 * (i - 1) + e
                                mm = pe.matmul(m.ps[64 * e:64 * e + 64, t, 0:HALF], m.eW2[:, x, :],
                                               m.a1[:, 2 + x, half(h)], start=True, stop=True)
                        mm.then_inc(task, 1)
                pe.wait_ge(a_read, evac.up(6))
                pe.wait_ge(weighted, wted.up(4))
                for j in range(GB):
                    if not (first and j < 2):
                        pe.wait_ge(o_read, ofree.up())
                    o = m.ps[:, (5, 6, 7, 5, 6)[j], 0:D]
                    s = slice(j * P, (j + 1) * P)
                    pe.matmul(o, m.a2[:, 0, s], m.sW3, start=True, stop=False)
                    for q in range(2):
                        pe.matmul(o, m.a2[:, 1 + q, s], m.eW3[:, q, :], start=False, stop=False)
                    pe.matmul(o, m.wT[0:NE0 + 1, s], m.b3[0:NE0 + 1, :], start=False, stop=True
                              ).then_inc(out_task, 1)
            group(0, True)
            with pe.Fori(1, NG) as g:
                group(g, False)

        @block.scalar
        def _(act):
            act.wait_ge(setup, 2)
            ready, outs = Level(act, "f0_ready"), Level(act, "f0_outs")

            def group(first):
                k = 0

                def tile():
                    nonlocal k
                    act.wait_ge(task, ready.up())
                    k += 1
                    return (k - 1) % 3

                if not first:
                    act.wait_ge(out_task, outs.up(GB))
                for a, b in TURNS:
                    t = tile()
                    act.activation(m.wT[0:NE0, a * P:b * P], m.ps[0:NE0, t, 0:(b - a) * P], ACT.Copy
                                   ).then_inc(a_read, 1)
                for i in range(6):
                    for h in range(2):
                        t = tile()
                        act.activation(m.a1[:, i, half(h)], m.ps[:, t, 0:HALF], ACT.Relu, bias=m.b1[:, i:i + 1]
                                       ).then_inc(a_read, 1)
                for i in (1, 2, 0):
                    for h in range(2):
                        t = tile()
                        act.activation(m.a2[:, i, half(h)], m.ps[:, t, 0:HALF], ACT.Relu, bias=m.b2[:, i:i + 1]
                                       ).then_inc(a_read, 1)
            group(True)
            with act.Fori(1, NG):
                group(False)

        @block.vector
        def _(v):
            spread, evac, outs = Level(v, "f0_spread"), Level(v, "f0_vevac", 15), Level(v, "f0_vouts")
            with v.Fori(0, NG) as g:
                for n in range(4):
                    q, h = n // 2, n % 2
                    v.wait_ge(wb_task, spread.up())
                    v.wait_ge(a_read, evac.up())
                    a = m.a2[:, 1 + q, half(h)]
                    v.tensor_tensor(a, a, m.ps[:, 3 + n % 2, 0:HALF], ALU.mult).then_inc(weighted, 1)
                evac.up(NA - 4)
                for j in range(GB):
                    v.wait_ge(out_task, outs.up())
                    xb = m.x[:, one(g * GB + j), :]
                    v.tensor_tensor(xb, xb, m.ps[:, (5, 6, 7, 5, 6)[j], 0:D].rearrange("p (o d) -> p o d", o=1),
                                    ALU.add).then_inc(o_read, 1)


def turns(eng, turn, last):
    def stages(i):
        return [i < NIT] + [0 <= i - 1 - k < NB for k in range(1, last + 1)]
    for i in range(last + 2):
        turn(i, stages(i))
    with eng.Fori(last + 2, NIT) as i:
        turn(i, [True] * (last + 1))
    for i in range(NIT, NIT + last + 1):
        turn(i, stages(i))


def first(i, n):
    return isinstance(i, int) and i < n


def layer1(nc, ctx, m, io):
    def sem(name):
        return ctx.enter_context(nc.semaphore("c_" + name))

    (loaded, setup, rel_task, red, rz_task, n_task, rz_read, gate_step, pre, tanhed, mix_step, x_turned, x_step, varied,
     rooted, normed, h_turned, evacuated, kept, hid_task, gelued, logit_task, logit_read) = (sem(s) for s in (
         "loaded", "setup", "rel_task", "red", "rz_task", "n_task", "rz_read", "gate_step", "pre", "tanhed", "mix_step",
         "x_turned", "x_step", "varied", "rooted", "normed", "h_turned", "evacuated", "kept", "hid_task", "gelued",
         "logit_task", "logit_read"))
    s = Sweep(nc, ctx, m, io, 1)
    RZ, NN, HIDA, REL, TURN = 2, 3, 4, 6, 7
    hn, tT = m.hn[:, GB - 1, :], m.tT[:, 0, :, :]
    stats, mv, rstd, half_neg = m.stats[:, 0, :], m.mv[:, 0, :], m.rstd[:, 0:1], m.std[:, 0:1]
    loads = [(m.wih, io["w_ihT"].rearrange("(c p) g -> p c g", p=P)),
             (m.whh, io["w_hhT"].rearrange("(c p) g -> p c g", p=P)),
             (m.rel[0:R16, :], io["rel"]), (m.bih, io["b_ihT"]), (m.bhh, io["b_hhT"]),
             (m.W1, io["W1"].rearrange("(c p) h -> p c h", p=P)), (m.Wg, io["Wg"].rearrange("(c p) e -> p c e", p=P)),
             (m.bg, io["bg"].rearrange("(o d) -> o d", o=1).broadcast_to([P, NE1])), (m.bf1, io["bf1T"])]

    def at(b):
        return bass.ds(b * P, P)
    with nc.Block() as block:
        @block.sync
        def _(sp):
            s.start_sync(sp)
            for dst, src in loads:
                sp.dma_start(dst, src).then_inc(loaded, 16)
            s.walk_sync(sp)
            with sp.Fori(1, NIT) as it:
                s.indices(sp, it)

        @block.gpsimd
        def _(g):
            g.memset(m.acc1, 0.0).then_inc(setup, 1)
            g.memset(half_neg, -0.5).then_inc(setup, 1)
            s.start_gather(g)
            s.walk_gather(g)
            has_var = Level(g, "c_has_var", 1)
            g.wait_ge(setup, 2)

            def turn(i, stages):
                sweep, root = stages[0], stages[-1]
                for p in range(2):
                    if sweep:
                        s.gather(g, p)
                    if p == 0 and root:
                        g.wait_ge(varied, has_var.reg)
                        has_var.up()
                        g.tensor_tensor(rstd, mv[:, 1:2], half_neg, ALU.pow).then_inc(rooted, 1)
            turns(g, turn, 3)

        @block.tensor
        def _(pe):
            s.start_sums(pe)
            s.walk_sums(pe)
            pe.wait_ge(loaded, 16 * len(loads))
            (covered, lread, red_in, rz_free, n_free, mixed, xread, hready, tready, hfree, gdone) = (
                Level(pe, "c_" + n, k) for n, k in (
                    ("covered", 0), ("lread", 1), ("red_in", 1), ("rz_free", 1), ("n_free", 1), ("mixed", 3),
                    ("xread", 1), ("hready", 1), ("tready", 1), ("hfree", 1), ("gdone", 2)))
            covered.up(s.adds * (2 + PG * 2))

            def turn(i, stages):
                sweep, cell, rest, logit = stages
                if rest:
                    pe.wait_ge(mix_step, mixed.reg)
                    mixed.up(3)
                    for c in range(2):
                        t = pe.transpose(m.ps[:, TURN, c * P:(c + 1) * P], m.gn[:, c, :], m.ident[:, :])
                    t.then_inc(x_turned, 1)
                if sweep:
                    s.sums(pe, 0)
                if cell:
                    if not first(i, 5):
                        pe.wait_ge(logit_read, lread.reg)
                        lread.up()
                    if sweep or i == NIT:
                        pe.wait_ge(s.added, covered.reg)
                        covered.up(s.adds * PG)
                    for c in range(2):
                        mm = pe.matmul(m.ps[:, REL, c * P:(c + 1) * P], m.rel[0:R16, c * P:(c + 1) * P],
                                       m.acc1[0:R16, 2, at(i - 2)], start=True, stop=True)
                    mm.then_inc(rel_task, 1)
                if sweep:
                    s.sums(pe, 1)
                if cell:
                    pe.wait_ge(red, red_in.reg)
                    red_in.up()
                if logit:
                    pe.wait_ge(gelued, gdone.reg)
                    gdone.up(2)
                    for k in range(MH):
                        mm = pe.matmul(m.ps[:, REL, 2 * P:2 * P + NE1], m.H0[:, k, :], m.Wg[:, k, :],
                                       start=(k == 0), stop=(k == MH - 1))
                    mm.then_inc(logit_task, 1)
                if cell:
                    if not first(i, 3):
                        pe.wait_ge(rz_read, rz_free.reg)
                        rz_free.up()
                    for gate in range(2):
                        for c in range(2):
                            col = slice((2 * gate + c) * P, (2 * gate + c + 1) * P)
                            for f in range(2):
                                pe.matmul(m.ps[:, RZ, col], m.whh[:, f, col], m.hT[:, f, at(i - 2)],
                                          start=(f == 0), stop=False)
                            for f in range(2):
                                mm = pe.matmul(m.ps[:, RZ, col], m.wih[:, f, col], m.acc1[:, f, at(i - 2)],
                                               start=False, stop=(f == 1))
                    mm.then_inc(rz_task, 1)
                    if not first(i, 3):
                        pe.wait_ge(pre, n_free.reg)
                        n_free.up()
                    for part, (w, src) in enumerate(((m.whh, m.hT), (m.wih, m.acc1))):
                        for c in range(2):
                            col = slice((4 + c) * P, (5 + c) * P)
                            for f in range(2):
                                mm = pe.matmul(m.ps[:, NN, (2 * part + c) * P:(2 * part + c + 1) * P], w[:, f, col],
                                               src[:, f, at(i - 2)], start=(f == 0), stop=(f == 1))
                    mm.then_inc(n_task, 1)
                if sweep:
                    s.sums(pe, 2)
                    s.sums(pe, 3)
                if rest:
                    pe.wait_ge(normed, hready.reg)
                    hready.up()
                    for c in range(2):
                        t = pe.transpose(m.ps[:, TURN, c * P:(c + 1) * P], hn[:, c * P:(c + 1) * P], m.ident[:, :])
                    t.then_inc(h_turned, 1)
                    pe.wait_ge(evacuated, tready.reg)
                    tready.up()
                    for half in range(2):
                        if not first(i, 4):
                            pe.wait_ge(gelued, hfree.reg)
                            hfree.up()
                        for k in range(4 * half, 4 * half + 4):
                            for c in range(2):
                                mm = pe.matmul(m.ps[:, HIDA + half, (k % 4) * P:(k % 4 + 1) * P],
                                               m.W1[:, c, k * P:(k + 1) * P], tT[:, c, :], start=(c == 0), stop=(c == 1))
                        mm.then_inc(hid_task, 1)
            turns(pe, turn, 3)

        @block.scalar
        def _(act):
            rz, ht, nt, pr, hid, hfree, gfree = (Level(act, "c_a" + n, k) for n, k in (
                ("rz", 1), ("ht", 1), ("nt", 0), ("pr", 1), ("hid", 1), ("hfree", 1), ("gfree", 3)))
            act.wait_ge(setup, 3)

            def turn(i, stages):
                sweep, cell, rest, logit = stages
                if cell:
                    if not first(i, 3):
                        act.wait_ge(mix_step, gfree.reg)
                        gfree.up(3)
                    act.wait_ge(rz_task, rz.reg)
                    rz.up()
                    for gate in range(2):
                        for c in range(2):
                            k = 2 * gate + c
                            ins = act.activation(m.rz[:, gate, c, :], m.ps[:, RZ, k * P:(k + 1) * P], ACT.Tanh,
                                                 bias=m.brz[:, k:k + 1], scale=0.5)
                    ins.then_inc(rz_read, 1)
                if rest:
                    act.wait_ge(h_turned, ht.reg)
                    ht.up()
                    act.activation(tT, m.ps[:, TURN, 0:D].rearrange("p (c n) -> p c n", c=2), ACT.Copy
                                   ).then_inc(evacuated, 1)
                    act.activation(m.h[:, one(i - 3), :], hn.rearrange("p (o d) -> p o d", o=1), ACT.Copy
                                   ).then_inc(kept, 1)
                if cell:
                    act.wait_ge(pre, pr.reg)
                    pr.up()
                    for c in range(2):
                        ins = act.activation(m.gn[:, c, :], m.gt[:, c, :], ACT.Tanh, bias=m.bih[:, 4 + c:5 + c])
                    ins.then_inc(tanhed, 1)
                if rest:
                    if not first(i, 4):
                        act.wait_ge(logit_task, hfree.reg)
                        hfree.up()
                    for half in range(2):
                        act.wait_ge(hid_task, hid.reg)
                        hid.up()
                        for k in range(4 * half, 4 * half + 4):
                            ins = act.activation(m.H0[:, k, :], m.ps[:, HIDA + half, (k % 4) * P:(k % 4 + 1) * P],
                                                 ACT.Gelu, bias=m.bf1[:, k:k + 1])
                        ins.then_inc(gelued, 1)
            turns(act, turn, 3)

        @block.vector
        def _(v):
            s.start_windows(v)
            v.wait_ge(setup, 2)
            s.walk_windows(v)
            s.keys(v, walk=False)
            v.wait_ge(loaded, 16 * len(loads))
            v.tensor_tensor(m.brz, m.bih[:, 0:4], m.bhh[:, 0:4], ALU.add).then_inc(gate_step, 1)
            v.wait_ge(gate_step, 1)
            v.tensor_scalar(m.brz, m.brz, 0.5, None, ALU.mult).then_inc(setup, 1)
            (xt, xs, rt, lg, rl, rzr, nt, gs, th, ms, root, kp) = (Level(v, "c_v" + n, k) for n, k in (
                ("xt", 1), ("xs", 1), ("rt", 1), ("lg", 1), ("rl", 1), ("rzr", 1), ("nt", 1), ("gs", 2), ("th", 1),
                ("ms", 1), ("root", 1), ("kp", 1)))

            def turn(i, stages):
                sweep, cell, rest, logit = stages
                if sweep:
                    s.one_hots(v, i, 0)
                if (sweep and not first(i, 1)) or first(i, NIT + 1) and not sweep:
                    s.windows(v, i - 1, 1)
                if sweep:
                    s.one_hots(v, i, 1)
                if rest:
                    xb = m.x[:, one(i - 3), :]
                    v.wait_ge(x_turned, xt.reg)
                    xt.up()
                    v.tensor_tensor(xb, xb, m.ps[:, TURN, 0:D].rearrange("p (o d) -> p o d", o=1), ALU.add
                                    ).then_inc(x_step, 1)
                if cell:
                    acc = m.acc1[:, 0:2, at(i - 2)]
                    v.wait_ge(rel_task, rl.reg)
                    rl.up()
                    v.tensor_tensor(acc, acc, m.ps[:, REL, 0:D].rearrange("p (c n) -> p c n", c=2), ALU.add
                                    ).then_inc(red, 1)
                if rest:
                    v.wait_ge(x_step, xs.reg)
                    xs.up()
                    v.bn_stats(stats, xb.rearrange("p o d -> p (o d)")).then_inc(x_step, 1)
                    v.wait_ge(x_step, xs.reg)
                    xs.up()
                    v.bn_aggr(mv, stats).then_inc(x_step, 1)
                    v.wait_ge(x_step, xs.reg)
                    xs.up()
                    v.tensor_scalar(mv[:, 1:2], mv[:, 1:2], EPS, None, ALU.add).then_inc(varied, 1)
                if logit:
                    v.wait_ge(logit_task, lg.reg)
                    lg.up()
                    v.tensor_tensor(m.logit1[:, one(i - 4), :], m.ps[:, REL, 2 * P:2 * P + NE1].rearrange(
                        "p (o e) -> p o e", o=1), m.bg.rearrange("p (o e) -> p o e", o=1), ALU.add
                        ).then_inc(logit_read, 1)
                if sweep:
                    s.windows(v, i, 0)
                if rest:
                    if not first(i, 4):
                        v.wait_ge(kept, kp.reg)
                        kp.up()
                    v.wait_ge(rooted, root.reg)
                    root.up()
                    v.tensor_scalar(hn.rearrange("p (o d) -> p o d", o=1), xb, mv[:, 0:1], rstd,
                                    ALU.subtract, ALU.mult).then_inc(normed, 1)
                if cell:
                    v.wait_ge(rz_read, rzr.reg)
                    rzr.up()
                    v.tensor_scalar(m.rz, m.rz, 0.5, 0.5, ALU.mult, ALU.add).then_inc(gate_step, 1)
                    v.wait_ge(n_task, nt.reg)
                    nt.up()
                    for c in range(2):
                        v.wait_ge(gate_step, gs.reg)
                        gs.up()
                        v.scalar_tensor_tensor(out=m.gt[:, c, :], in0=m.ps[:, NN, c * P:(c + 1) * P],
                                               scalar=m.bhh[:, 4 + c:5 + c], in1=m.rz[:, 0, c, :], op0=ALU.add,
                                               op1=ALU.mult).then_inc(gate_step, 1)
                    v.wait_ge(gate_step, gs.reg)
                    gs.up()
                    v.tensor_tensor(m.gt, m.gt, m.ps[:, NN, 2 * P:4 * P].rearrange("p (c n) -> p c n", c=2), ALU.add
                                    ).then_inc(pre, 1)
                    v.wait_ge(tanhed, th.reg)
                    th.up()
                    v.tensor_tensor(m.gt, m.hT[:, :, at(i - 2)], m.gn, ALU.subtract).then_inc(mix_step, 1)
                    v.wait_ge(mix_step, ms.reg)
                    ms.up()
                    v.tensor_tensor(m.gt, m.gt, m.rz[:, 1, :, :], ALU.mult).then_inc(mix_step, 1)
                    v.wait_ge(mix_step, ms.reg)
                    ms.up()
                    v.tensor_tensor(m.gn, m.gn, m.gt, ALU.add).then_inc(mix_step, 1)
                    ms.up()
            turns(v, turn, 3)


def route(nc, ctx, m, io):
    def sem(name):
        return ctx.enter_context(nc.semaphore("rt_" + name))

    v_step, a_step, p_step, counted, placed, sent, wd_in = (
        sem(s) for s in ("v_step", "a_step", "p_step", "counted", "placed", "sent", "wd_in"))

    def per_block(c, e=NE1):
        return c.rearrange("p (b o) -> p b o", o=1).broadcast_to([P, NB, e])

    def per_expert(r, n):
        return r.rearrange("p (o e) -> p o e", o=1).broadcast_to([P, n, NE1])
    with nc.Block() as block:
        @block.vector
        def _(v):
            count = [0]

            def link(ins):
                count[0] += 1
                ins.then_inc(v_step, 1)
                v.wait_ge(v_step, count[0])

            link(v.tensor_reduce(m.col1, m.logit1, AX.X, ALU.max))
            link(v.tensor_tensor(m.tmp1, m.logit1, per_block(m.col1), ALU.subtract))
            v.wait_ge(a_step, 1)
            link(v.tensor_reduce(m.col1, m.prob1, AX.X, ALU.add))
            link(v.reciprocal(m.col1, m.col1))
            link(v.tensor_tensor(m.prob1, m.prob1, per_block(m.col1), ALU.mult))
            link(v.tensor_reduce(m.best, m.prob1, AX.X, ALU.max))
            link(v.tensor_tensor(m.tmp1, m.prob1, per_block(m.best), ALU.is_lt))
            link(v.scalar_tensor_tensor(out=m.tmp1, in0=m.tmp1, scalar=float(4 * NE1),
                                        in1=per_expert(m.iota[:, 0:NE1], NB), op0=ALU.mult, op1=ALU.add))
            link(v.tensor_reduce(m.col1, m.tmp1, AX.X, ALU.min))
            link(v.tensor_tensor(m.pick, per_expert(m.iota[:, 0:NE1], NB), per_block(m.col1), ALU.is_equal))
            v.wait_ge(p_step, 4)
            last = m.pick[:, NB - 1, :]
            link(v.tensor_tensor(last, last, m.padmask, ALU.mult))
            v.wait_ge(counted, 1)
            link(v.tensor_copy(m.tot, m.ps[:, 1, 0:NB * NE1].rearrange("p (b e) -> p e b", e=NE1)))
            for e in range(NE1):
                link(v.tensor_tensor_scan(out=m.cum[:, e, :], data0=m.ones[:, 0:NB], data1=m.tot[:, e, :],
                                          initial=0.0, op0=ALU.mult, op1=ALU.add))
            steps = m.steps.rearrange("p (o k) -> p o k", o=1).broadcast_to([P, NE1, NB])
            link(v.tensor_scalar(m.steps, m.iota[:, 0:NB], float(P), None, ALU.mult))
            t = m.tmp1.rearrange("p b e -> p (b e)").rearrange("p (e k) -> p e k", k=NB)
            link(v.tensor_tensor(t, m.cum[:, :, NB - 1:NB].broadcast_to([P, NE1, NB]), steps, ALU.is_gt))
            link(v.tensor_reduce(m.ntiles, t, AX.X, ALU.add))
            link(v.tensor_tensor_scan(out=m.ends, data0=m.ones[:, 0:NE1], data1=m.ntiles, initial=0.0,
                                      op0=ALU.mult, op1=ALU.add))
            link(v.tensor_tensor(m.starts, m.ends, m.ntiles, ALU.subtract))
            link(v.tensor_tensor(m.tmp2, m.iota[:, 0:TILES].rearrange("p (t o) -> p t o", o=1
                                                                      ).broadcast_to([P, TILES, NE1]),
                                 per_expert(m.ends, TILES), ALU.is_ge))
            link(v.tensor_reduce(m.ofTf, m.tmp2, AX.X, ALU.add))
            link(v.tensor_scalar(m.ofTf, m.ofTf, float(NE1 - 1), None, ALU.min))
            link(v.tensor_copy(m.ofT, m.ofTf))
            link(v.tensor_scalar(m.starts, m.starts, float(P), None, ALU.mult))
            link(v.tensor_tensor(m.cum, m.cum, m.tot, ALU.subtract))
            link(v.tensor_tensor(m.before, m.ps[:, 0, 0:NB * NE1].rearrange("p (b e) -> p b e", e=NE1),
                                 m.cum.rearrange("p e b -> p b e"), ALU.add))
            link(v.tensor_tensor(m.before, m.before, per_expert(m.starts, NB), ALU.add))
            link(v.tensor_tensor(m.before, m.before, m.pick, ALU.mult))
            link(v.tensor_reduce(m.posf, m.before, AX.X, ALU.add))
            v.tensor_copy(m.slot_of, m.posf).then_inc(placed, 1)

        @block.scalar
        def _(act):
            act.wait_ge(v_step, 2)
            act.activation(m.prob1, m.tmp1, ACT.Exp).then_inc(a_step, 1)

        @block.tensor
        def _(pe):
            pe.wait_ge(v_step, 11)
            pick = m.pick.rearrange("p b e -> p (b e)")
            pe.matmul(m.ps[:, 0, 0:NB * NE1], m.tri, pick, start=True, stop=True)
            pe.matmul(m.ps[:, 1, 0:NB * NE1], m.ones[:, :], pick, start=True, stop=True).then_inc(counted, 1)

        @block.gpsimd
        def _(g):
            g.memset(m.tri, 1.0).then_inc(p_step, 1)
            g.memset(m.padmask, 1.0).then_inc(p_step, 1)
            g.wait_ge(p_step, 2)
            g.affine_select(out=m.tri, in_=m.tri, compare_op=ALU.is_gt, fill=0.0, base=0, pattern=[[1, P]],
                            channel_multiplier=-1).then_inc(p_step, 1)
            g.affine_select(out=m.padmask, in_=m.padmask, compare_op=ALU.is_ge, fill=0.0, base=NTAIL - 1,
                            pattern=[[0, NE1]], channel_multiplier=-1).then_inc(p_step, 1)
            g.wait_ge(placed, 1)
            for b in range(NB):
                n = P if b < NB - 1 else NTAIL
                g.indirect_dma_start(io["slots_in"], bass.IndirectOffsetOnAxis(ap=m.slot_of[0:n, b:b + 1], axis=0),
                                     m.h[0:n, b, :], None).then_inc(sent, 16)
            g.wait_ge(sent, 16 * NB)

        @block.sync
        def _(sp):
            for e in range(NE1):
                sp.dma_start(m.Wd[:, e, :, :], io["Wd"][e].rearrange("(c p) d -> p c d", p=P)).then_inc(wd_in, 16)
            sp.dma_start(m.bd, io["bd"].rearrange("(o e) d -> o e d", o=1).broadcast_to([P, NE1, D])).then_inc(wd_in, 16)
            sp.wait_ge(wd_in, 16 * (NE1 + 1))


def experts(nc, ctx, m, io):
    def sem(name):
        return ctx.enter_context(nc.semaphore("ex_" + name))

    loaded = [sem("loaded0"), sem("loaded1")]
    stored = [sem("stored0"), sem("stored1")]
    turned, evacuated, task, gelued, product, read = (
        sem(s) for s in ("turned", "evacuated", "task", "gelued", "product", "read"))
    Q = TILES // 4
    with nc.Block() as block:
        @block.sync
        def _(sp):
            def rows(t, q):
                return t[bass.ds(q * 4 * P, 4 * P), :].rearrange("(i p) d -> p i d", p=P)
            for i in range(2):
                sp.dma_start(m.slots[i], rows(io["slots_in"], i)).then_inc(loaded[i], 16)
            for q in range(Q):
                i = q % 2
                sp.wait_ge(read, 4 * (q + 1))
                sp.dma_start(rows(io["slots_out"], q), m.results[i]).then_inc(stored[i], 16)
                if q + 2 < Q:
                    sp.wait_ge(turned, q + 1)
                    sp.dma_start(m.slots[i], rows(io["slots_in"], q + 2)).then_inc(loaded[i], 16)
            for i in range(2):
                sp.wait_ge(stored[i], 16 * Q // 2)

        @block.tensor
        def _(pe):
            landed, hts, free, hid, ofree = (Level(pe, "ex_" + s) for s in ("landed", "hts", "free", "hid", "ofree"))

            def quad(q, i, first):
                e = [pe.value_load(m.ofT[0:1, bass.ds(q * 4 + t, 1)], min_val=0, max_val=NE1 - 1) for t in range(4)]
                if i == 0:
                    landed.up(16)
                pe.wait_ge(loaded[i], landed.reg)
                for c in range(2):
                    for t in range(4):
                        mm = pe.transpose(m.ps[:, c, t * P:(t + 1) * P], m.slots[i][:, t, c * P:(c + 1) * P],
                                          m.ident[:, :])
                mm.then_inc(turned, 1)
                pe.wait_ge(evacuated, hts.up())
                for k in range(MH):
                    if not (first and k < 4):
                        pe.wait_ge(gelued, free.up())
                    for c in range(2):
                        mm = pe.matmul(m.ps[:, 2 + k % 4, :], m.W1[:, c, k * P:(k + 1) * P], m.hTQ[:, c, :],
                                       start=(c == 0), stop=(c == 1))
                    mm.then_inc(task, 1)
                pe.wait_ge(gelued, hid.up(MH))
                for t in range(4):
                    if not (first and t < 2):
                        pe.wait_ge(read, ofree.up())
                    for k in range(MH):
                        mm = pe.matmul(m.ps[:, 6 + t % 2, 0:D], m.HQ[i][:, k, t * P:(t + 1) * P],
                                       m.Wd[:, one(e[t]), k, :], start=(k == 0), stop=(k == MH - 1))
                    mm.then_inc(product, 1)
            quad(0, 0, True)
            quad(1, 1, False)
            with pe.Fori(1, Q // 2) as q2:
                for i in range(2):
                    quad(q2 * 2 + i, i, False)

        @block.scalar
        def _(act):
            ready, free = Level(act, "ex_ready"), Level(act, "ex_hfree")

            def quad(i, first):
                if not first:
                    act.wait_ge(product, free.up(4))
                for k in range(MH):
                    act.wait_ge(task, ready.up())
                    act.activation(m.HQ[i][:, k, :], m.ps[:, 2 + k % 4, :], ACT.Gelu, bias=m.bf1[:, k:k + 1]
                                   ).then_inc(gelued, 1)
            for i in range(2):
                quad(i, True)
            with act.Fori(1, Q // 2):
                for i in range(2):
                    quad(i, False)

        @block.vector
        def _(v):
            turn, prod, store = Level(v, "ex_turn"), Level(v, "ex_prod"), Level(v, "ex_store")

            def quad(q, i, first):
                v.wait_ge(turned, turn.up())
                for c in range(2):
                    ins = v.tensor_copy(m.hTQ[:, c, :], m.ps[:, c, :])
                ins.then_inc(evacuated, 1)
                if not first:
                    if i == 0:
                        store.up(16)
                    v.wait_ge(stored[i], store.reg)
                for t in range(4):
                    e = v.value_load(m.ofT[0:1, bass.ds(q * 4 + t, 1)], min_val=0, max_val=NE1 - 1)
                    v.wait_ge(product, prod.up())
                    v.tensor_tensor(m.results[i][:, t, :].rearrange("p (o d) -> p o d", o=1),
                                    m.ps[:, 6 + t % 2, 0:D].rearrange("p (o d) -> p o d", o=1),
                                    m.bd[:, one(e), :], ALU.add).then_inc(read, 1)
            for i in range(2):
                quad(i, i, True)
            with v.Fori(1, Q // 2) as q2:
                for i in range(2):
                    quad(q2 * 2 + i, i, False)


def finish(nc, ctx, m, io):
    def sem(name):
        return ctx.enter_context(nc.semaphore("fin_" + name))

    fetched = [sem(f"fetched{g}") for g in range(NG)]
    done, stored = sem("done"), sem("stored")

    def size(b):
        return P if b < NB - 1 else NTAIL
    with nc.Block() as block:
        @block.gpsimd
        def _(g):
            for b in range(NB):
                n = size(b)
                g.indirect_dma_start(m.h[0:n, b, :], None, io["slots_out"],
                                     bass.IndirectOffsetOnAxis(ap=m.slot_of[0:n, b:b + 1], axis=0)
                                     ).then_inc(fetched[b // GB], 16)

        @block.vector
        def _(v):
            for g in range(NG):
                v.wait_ge(fetched[g], 16 * GB)
                for b in range(g * GB, (g + 1) * GB):
                    n = size(b)
                    v.scalar_tensor_tensor(out=m.x[0:n, b, :], in0=m.h[0:n, b, :], scalar=m.best[0:n, b:b + 1],
                                           in1=m.x[0:n, b, :], op0=ALU.mult, op1=ALU.add).then_inc(done, 1)

        @block.sync
        def _(sp):
            for g in range(NG):
                sp.wait_ge(done, GB * (g + 1))
                lo, hi = g * GB, min((g + 1) * GB, NB - 1)
                sp.dma_start(io["out"][lo * P:hi * P, :].rearrange("(b p) d -> p b d", p=P), m.x[:, lo:hi, :]
                             ).then_inc(stored, 16)
            sp.dma_start(io["out"][(NB - 1) * P:N, :], m.x[0:NTAIL, NB - 1, :]).then_inc(stored, 16)
            sp.wait_ge(stored, 16 * (NG + 1))


def program(nc, io):
    with ExitStack() as ctx:
        m = allocate(nc, ctx)

        def bcast(t):
            n = t.shape[0]
            return t.rearrange("(o d) -> o d", o=1).broadcast_to([P, n])

        def phase(build, *args, **named):
            build(nc, ctx, m, io, *args, **named)
        phase(prepare)
        phase(layernorm, "n0_", use="G", full=False, table=io["g_table"])
        phase(messages0)
        phase(aggregate)
        phase(layernorm, "n1_", use="gates", loads=[
            (m.gW, io["gW"].rearrange("(c p) e -> p c e", p=P)), (m.gb, bcast(io["gb"])),
            (m.sW1, io["sW1"].rearrange("(c p) h -> p c h", p=P)), (m.sW2, io["sW2"].rearrange("(c p) h -> p c h", p=P)),
            (m.sW3, io["sW3"]), (m.eW2, io["eW2"].rearrange("e p h -> p e h")),
            (m.eW3, io["eW3q"].rearrange("q p d -> p q d")),
            (m.b1, io["b1T"]), (m.b2, io["b2T"]),
            (m.b3[0:NE0, :], io["eb3"]), (m.b3[NE0:NE0 + 1, :], io["sb3"].rearrange("(o d) -> o d", o=1)),
        ] + [(m.eW1[:, e, :, :], io["eW1"][e].rearrange("(c p) h -> p c h", p=P)) for e in range(NE0)])
        phase(top_two)
        phase(ffn0)
        phase(layernorm, "n2_", keep=True, table=io["h_table"])
        phase(layer1)
        phase(route)
        phase(experts)
        phase(finish)


def kernel(**inputs):
    import numpy as np
    import concourse.bacc as bacc
    from concourse.bass_utils import run_bass_kernel_spmd as run

    a = {k: np.asarray(v) for k, v in inputs.items()}

    def tiles(e):
        return e.reshape(ET, EP).T

    def columns(b):
        return b.reshape(-1, P).T
    host = {
        "x": a["x"], "dst_groups": a["dst"].reshape(NSG, SG * EP),
        "src": tiles(a["src"]), "dst": tiles(a["dst"]), "t8": tiles(a["edge_type_8"]),
        "t16": tiles(a["edge_type_16"]),
        "basis": a["L0_gnn_basis"].reshape(R8 * P, D), "w_comp": a["L0_gnn_w_comp"], "gnn_bias": a["L0_gnn_bias"],
        "sW1": a["L0_ffn_sW1"], "sW2": a["L0_ffn_sW2"], "sW3": a["L0_ffn_sW3"], "sb3": a["L0_ffn_sb3"],
        "eW1": a["L0_ffn_eW1"], "eW2": a["L0_ffn_eW2"], "eW3q": a["L0_ffn_eW3"].reshape(2, P, D), "eb3": a["L0_ffn_eb3"],
        "b1T": np.concatenate([columns(a["L0_ffn_sb1"]), columns(a["L0_ffn_eb1"])], 1),
        "b2T": np.concatenate([columns(a["L0_ffn_sb2"]), columns(a["L0_ffn_eb2"])], 1),
        "gW": a["L0_ffn_gW"], "gb": a["L0_ffn_gb"],
        "rel": a["L1_gnn_relvectors"], "w_ihT": a["L1_gnn_w_ih"].T, "w_hhT": a["L1_gnn_w_hh"].T,
        "b_ihT": columns(a["L1_gnn_b_ih"]), "b_hhT": columns(a["L1_gnn_b_hh"]),
        "W1": a["L1_ffn_W1"], "bf1T": columns(a["L1_ffn_b1"]), "Wg": a["L1_ffn_Wg"], "bg": a["L1_ffn_bg"],
        "Wd": a["L1_ffn_Wd"], "bd": a["L1_ffn_bd"],
    }
    host = {k: np.ascontiguousarray(v) for k, v in host.items()}
    nc = bacc.Bacc("TRN2", target_bir_lowering=False, num_devices=1)
    io = {k: nc.dram_tensor("in_" + k, v.shape, mybir.dt.from_np(v.dtype), kind="ExternalInput").ap()
          for k, v in host.items()}
    io["out"] = nc.dram_tensor("out_x", (N, D), F32, kind="ExternalOutput").ap()
    for name, shape in (("g_table", (NP, P)), ("h_table", (NP, D)), ("slots_in", (SLOTS, D)),
                        ("slots_out", (SLOTS, D))):
        io[name] = nc.dram_tensor(name, shape, F32).ap()
    program(nc, io)
    r = run(nc, [{"in_" + k: v for k, v in host.items()}], core_ids=[0])
    return r.results[0]["out_x"]
```

```python
from contextlib import ExitStack

import concourse.bass as bass
from concourse import mybir

F32 = mybir.dt.float32
I32 = mybir.dt.int32
BF16 = mybir.dt.bfloat16
ALU = mybir.AluOpType
ACT = mybir.ActivationFunctionType
AX = mybir.AxisListType

P = 128
N, D, E = 3125, 256, 50000
NB = -(-N // P)
NTAIL = N - (NB - 1) * P
NP = NB * P
GB = 5
NG = NB // GB
GN = GB * P
EP = 125
ET = E // EP
UNR = 16
NIT = ET // UNR
SG = 4
NSG = ET // SG
PG = UNR // SG
PART = UNR // 2
WIN = 16
GWIN = 48
ACCW0, ACCW1 = NP + WIN, NP + GWIN
REGION = 8 * ACCW0
WORK = 11360
NONE = 1.0e6
R8, R16, NBASE = 8, 16, 4
NE0, NE1 = 4, 8
HID = 1024
MH = HID // P
TILES = (N + NE1 * (P - 1)) // P
SLOTS = TILES * P
EPS = 1e-5
assert EP * ET == E and UNR * NIT == ET and NIT == NB and GB * NG == NB and TILES % 8 == 0


class Level:

    def __init__(self, eng, name, start=0):
        self.eng, self.reg = eng, eng.alloc_register(name)
        eng.reg_mov(self.reg, start)

    def up(self, n=1):
        self.eng.reg_add(self.reg, self.reg, n)
        return self.reg


def one(b):
    return bass.ds(b, 1)


def allocate(nc, ctx):
    def sb(name, shape, dt=F32):
        return ctx.enter_context(nc.sbuf_tensor(name, shape, dt))

    class M:
        pass

    m = M()
    m.x = sb("x", [P, NB, D])
    m.hT = sb("hT", [P, 2, NP])
    m.region = sb("region", [P, REGION])
    m.work = sb("work", [P, WORK])
    m.ident = sb("ident", [P, P])
    m.iota = sb("iota", [P, P])
    m.ones = sb("ones", [P, P])
    m.mv = sb("mv", [P, 2, 2])
    m.stats = sb("stats", [P, 2, 6])
    m.rstd = sb("rstd", [P, 2])
    m.half_neg = sb("half_neg", [P, 2])
    m.src = sb("src", [EP, ET], I32)
    m.src_now = sb("src_now", [EP, UNR], I32)
    m.dst = sb("dst", [EP, ET])
    m.type = sb("type", [EP, ET])
    m.base = sb("base", [P, ET + NSG])
    m.first_row = sb("first_row", [1, ET + NSG], I32)
    m.walk_row = sb("walk_row", [1, PART], I32)
    m.key = sb("key", [EP, ET])
    m.cmat = sb("cmat", [P, 64])
    m.wincol = sb("wincol", [EP, 1])
    m.rounds = sb("rounds", [1, 2], I32)
    m.ps = ctx.enter_context(nc.psum_tensor("ps", [P, 8, 512], F32))

    def carve(whole, start, *shape):
        n = 1
        for s in shape:
            n *= s
        v = whole[:, start:start + n]
        names = "abcd"[:len(shape)]
        if len(shape) > 1:
            v = v.rearrange("p (" + " ".join(names) + ") -> p " + " ".join(names), **dict(zip(names, shape)))
        return v, start + n

    reg, work = m.region[:, :], m.work[:, :]
    m.gbuf, at = carve(work, 0, NB, P)
    m.hn0, at = carve(work, at, 2, GB, D)
    m.tT0, at = carve(work, at, 2, GB, 2, P)
    m.mv0, at = carve(work, at, 2, GB, 2)
    m.stats0, at = carve(work, at, 2, GB, 6)
    m.rstd0, at = carve(work, at, 2, GB)
    assert at <= WORK
    m.acc0, _ = carve(reg, 0, R8, ACCW0)
    m.ring0, at = carve(work[0:EP], 0, UNR, P)
    m.hot0, at = carve(work[0:EP], at, 2 * SG, P)
    m.basis, at = carve(work, at, R8, D)
    m.sW1, at = carve(work, at, 2, 256)
    m.sW2, at = carve(work, at, 2, 128)
    m.sW3, at = carve(work, at, 256)
    m.eW1, at = carve(work, at, NE0, 2, 128)
    m.eW2, at = carve(work, at, NE0, 64)
    m.eW3, at = carve(work, at, 2, 256)
    m.gW, at = carve(work, at, 2, NE0)
    m.gb, at = carve(work, at, NE0)
    m.b1, at = carve(work, at, 6)
    m.b2, at = carve(work, at, 3)
    m.b3, at = carve(work, at, 256)
    m.bias0, at = carve(work, at, 256)
    m.sel, at = carve(work, at, 2, P)
    m.low, at = carve(work, at, NE0, NE0)
    m.sring, at = carve(work, at, R8 // 2, P)
    m.hn1, at = carve(work, at, D)
    m.hn2, at = carve(work, at, D)
    m.tT1, at = carve(work, at, 2, P)
    m.a1, at = carve(work, at, 6, P)
    m.a2, at = carve(work, at, 3, P)
    m.wT, at = carve(work, at, P)
    m.w5, at = carve(work, at, NE0 + 1)
    m.gate, at = carve(work, at, 3, NE0)
    m.comp, at = carve(work, at, NE0, 2, NE0)
    m.rank, at = carve(work, at, NE0)
    m.gcol, at = carve(work, at, 4)
    assert at <= WORK
    m.h, at = carve(work, 0, NB, D)
    small, at = work[:, at:at + 1500], at + 1500
    small2, at = work[:, at:at + 900], at + 900
    m.hn, at = carve(work, at, D)
    m.tT, at = carve(work, at, 2, P)
    assert at <= WORK
    hflat = work[:, 0:NB * D]
    m.acc1, at = carve(reg, 0, 3, ACCW1)
    m.ring1, at = carve(reg[0:EP], at, UNR, D)
    m.hot1, at = carve(reg[0:EP], at, UNR, GWIN)
    m.wih, at = carve(reg, at, 2, 768)
    m.whh, at = carve(reg, at, 2, 768)
    m.rel, at = carve(reg, at, D)
    m.bih, at = carve(reg, at, 6)
    m.bhh, at = carve(reg, at, 6)
    m.brz, third = carve(reg, at, 4)
    m.Wd, at = carve(reg, 0, NE1, MH, D)
    m.bd, at = carve(reg, at, NE1, D)
    assert third <= at
    m.W1, at = carve(reg, at, 2, HID)
    m.Wg, at = carve(reg, at, MH, NE1)
    m.bg, at = carve(reg, at, NE1)
    m.bf1, at = carve(reg, at, MH)
    m.rz, at2 = carve(reg, at, 2, 2, P)
    m.gt, at2 = carve(reg, at2, 2, P)
    m.gn, at2 = carve(reg, at2, 2, P)
    m.H0, at2 = carve(reg, at2, MH, P)
    m.zeros, at2 = carve(reg, at2, D)
    m.lt, at2 = carve(reg, at2, P)
    flat, at2 = carve(reg[0:EP], at2, UNR * R16 // 2)
    m.hot_type = flat.bitcast(BF16).rearrange("p (t w) -> p t w", w=R16)
    flat, at2 = carve(reg[0:EP], at2, UNR * GWIN // 2)
    m.hot1b = flat.bitcast(BF16).rearrange("p (t w) -> p t w", w=GWIN)
    assert at2 <= REGION and at + MH * 4 * P <= REGION
    m.HQ = [carve(reg, at, MH, 4 * P)[0], carve(m.hT[:, :, :].rearrange("p a n -> p (a n)"), 0, MH, 4 * P)[0]]
    m.hTQ = [carve(m.hT[:, :, :].rearrange("p a n -> p (a n)"), (MH + 2 * i) * 4 * P, 2, 4 * P)[0] for i in range(2)]
    m.slots = [carve(hflat, i * 4 * D, 4, D)[0] for i in range(2)]
    m.results = [carve(hflat, (2 + i) * 4 * D, 4, D)[0] for i in range(2)]
    m.logit1, at = carve(small, 0, NB, NE1)
    m.prob1, at = carve(small, at, NB, NE1)
    m.pick, at = carve(small, at, NB, NE1)
    m.before, at = carve(small, at, NB, NE1)
    m.cum, at = carve(small, at, NE1, NB)
    m.tmp1, at = carve(small, at, NB, NE1)
    assert at <= 1500
    small = small2
    m.tri, at = carve(small, 0, P)
    m.tmp2, at = carve(small, at, TILES, NE1)
    m.tot, at = carve(small, at, NE1, NB)
    m.best, at = carve(small, at, NB)
    m.col1, at = carve(small, at, NB)
    m.posf, at = carve(small, at, NB)
    m.slot_of, at = carve(small, at, NB)
    m.slot_of = m.slot_of.bitcast(I32)
    m.steps, at = carve(small, at, NB)
    m.ntiles, at = carve(small, at, NE1)
    m.ends, at = carve(small, at, NE1)
    m.starts, at = carve(small, at, NE1)
    m.padmask, at = carve(small, at, NE1)
    m.ofTf, at = carve(small, at, TILES)
    m.ofT, at = carve(small, at, TILES)
    m.ofT = m.ofT.bitcast(I32)
    assert at <= 900
    return m


def prepare(nc, ctx, m, io):
    def sem(name):
        return ctx.enter_context(nc.semaphore(name))

    in_x, in_src, in_edges, in_dstrow, in_comp = (sem("in_" + s) for s in ("x", "src", "edges", "dstrow", "comp"))
    pads, pool_step, v_step, bc_ready, fl_ready = (
        sem(s) for s in ("pads", "pool_step", "v_step", "bc_ready", "fl_ready"))
    hTflat = m.hT[:, :, :].rearrange("p a n -> p (a n)")
    stage = hTflat[0:EP, 4100:4100 + 2 * ET].rearrange("p (a t) -> p a t", a=2).bitcast(I32)
    rows = hTflat[0:NSG, 0:SG * EP].bitcast(I32)
    rows_f = hTflat[0:NSG, 500:500 + SG * EP].rearrange("p (k e) -> p k e", k=SG)
    lows = hTflat[0:NSG, 1024:1024 + SG + 1]
    diag = hTflat[0:NSG, 1100:1100 + (SG + 1) * NSG].rearrange("p (k g) -> p k g", k=SG + 1)
    over = hTflat[0:EP, 1700:1701]
    over_t = hTflat[0:EP, 1800:1800 + 2 * ET + NSG]
    limit = hTflat[0:EP, 2800:2800 + ET]
    flag = hTflat[0:1, 3300:3301]
    spare = hTflat[0:1, 3302:3302 + ET + NSG]
    flagr = hTflat[0:1, 3301:3302]
    m.comp_rep = hTflat[:, 4000:4004]
    with nc.Block() as block:
        @block.sync
        def _(sp):
            sp.dma_start(rows, io["dst_groups"]).then_inc(in_dstrow, 16)
            for k, name in enumerate(("dst", "t8")):
                sp.dma_start(stage[:, k, :], io[name]).then_inc(in_edges, 16)
            sp.dma_start(m.src[:, :], io["src"]).then_inc(in_src, 16)
            sp.wait_ge(in_x, 32)
            sp.wait_ge(in_src, 16)

        @block.scalar
        def _(act):
            act.wait_ge(in_edges, 32)
            act.dma_start(m.x[:, 0:NB - 1, :], io["x"][0:(NB - 1) * P, :].rearrange("(b p) d -> p b d", p=P)
                          ).then_inc(in_x, 16)
            act.wait_ge(pads, 1)
            act.dma_start(m.x[0:NTAIL, NB - 1, :], io["x"][(NB - 1) * P:N, :]).then_inc(in_x, 16)
            act.dma_start(m.comp_rep, io["w_comp"].rearrange("(o r) b -> o r b", o=1).broadcast_to(
                [P // R8, R8, NBASE])).then_inc(in_comp, 16)

        @block.gpsimd
        def _(g):
            g.memset(m.ident[:, :], 0.0).then_inc(pool_step, 1)
            g.memset(m.ones[:, :], 1.0).then_inc(pool_step, 1)
            g.memset(m.x[:, NB - 1, :], 0.0).then_inc(pads, 1)
            g.iota(m.iota[:, :], pattern=[[1, P]], base=0, channel_multiplier=0,
                   allow_small_or_imprecise_dtypes=True).then_inc(pool_step, 1)
            g.wait_ge(pool_step, 3)
            g.affine_select(out=m.ident[:, :], in_=m.ident[:, :], compare_op=ALU.not_equal, fill=1.0, base=0,
                            pattern=[[-1, P]], channel_multiplier=1).then_inc(pool_step, 1)
            g.iota(limit.rearrange("p (i t) -> p i t", t=UNR), pattern=[[P, NIT], [0, UNR]], base=-P,
                   channel_multiplier=0, allow_small_or_imprecise_dtypes=True).then_inc(pool_step, 1)

        @block.vector
        def _(v):
            v.memset(m.wincol[:, :], 0.0).then_inc(v_step, 1)
            v.wait_ge(in_dstrow, 16)
            v.tensor_copy(rows_f, rows.rearrange("p (k e) -> p k e", k=SG)).then_inc(v_step, 1)
            v.wait_ge(v_step, 2)
            v.tensor_reduce(lows[:, 0:SG], rows_f, AX.X, ALU.min).then_inc(v_step, 1)
            v.wait_ge(v_step, 3)
            v.tensor_reduce(lows[:, SG:SG + 1], lows[:, 0:SG], AX.X, ALU.min).then_inc(v_step, 1)
            v.wait_ge(v_step, 4)
            v.wait_ge(pool_step, 5)
            for k in range(SG + 1):
                v.tensor_scalar(diag[:, k, :], m.ident[0:NSG, 0:NSG], lows[:, k:k + 1], None, ALU.mult
                                ).then_inc(v_step, 1)
            v.wait_ge(in_edges, 16 * 2)
            v.tensor_copy(m.dst[:, :], stage[:, 0, :]).then_inc(v_step, 1)
            v.tensor_copy(m.type[:, :], stage[:, 1, :]).then_inc(v_step, 1)
            v.wait_ge(bc_ready, 1)
            v.tensor_copy(m.base[:, 0:ET].rearrange("p (g k) -> p k g", k=SG),
                          m.ps[:, 0, 0:ET].rearrange("p (k g) -> p k g", k=SG)).then_inc(v_step, 1)
            v.tensor_copy(m.base[:, ET:ET + NSG], m.ps[:, 0, ET:ET + NSG]).then_inc(v_step, 1)
            v.wait_ge(v_step, 13)
            v.tensor_tensor(over_t[:, 0:ET], m.dst[:, :], m.base[0:EP, 0:ET], ALU.subtract).then_inc(v_step, 1)
            v.tensor_tensor(over_t[:, ET:2 * ET].rearrange("p (g k) -> p g k", k=SG),
                            m.dst[:, :].rearrange("p (g k) -> p g k", k=SG),
                            m.base[0:EP, ET:ET + NSG].rearrange("p (g o) -> p g o", o=1).broadcast_to([EP, NSG, SG]),
                            ALU.subtract).then_inc(v_step, 1)
            v.tensor_tensor(limit, m.base[0:EP, 0:ET], limit, ALU.is_lt).then_inc(v_step, 1)
            v.wait_ge(v_step, 16)
            v.tensor_scalar(over_t[:, 0:ET], over_t[:, 0:ET], float(WIN), None, ALU.is_ge).then_inc(v_step, 1)
            v.tensor_scalar(over_t[:, ET:2 * ET], over_t[:, ET:2 * ET], float(GWIN), None, ALU.is_ge).then_inc(v_step, 1)
            v.wait_ge(v_step, 18)
            v.tensor_tensor(over_t[:, 0:ET], over_t[:, 0:ET], limit, ALU.max).then_inc(v_step, 1)
            v.wait_ge(v_step, 19)
            v.tensor_reduce(over, over_t[:, 0:2 * ET], AX.X, ALU.max).then_inc(v_step, 1)
            v.wait_ge(fl_ready, 1)
            v.tensor_reduce(flag, m.ps[0:1, 1, 0:EP], AX.X, ALU.max).then_inc(v_step, 1)
            v.wait_ge(v_step, 21)
            for layer, width in enumerate((WIN, GWIN)):
                v.tensor_scalar(m.rounds[:, layer:layer + 1], flag, float(-(-N // width)), None, ALU.mult
                                ).then_inc(v_step, 1)
            v.tensor_scalar(flagr, flag, -1.0, 1.0, ALU.mult, ALU.add).then_inc(v_step, 1)
            v.tensor_scalar(flag, flag, float(NP), None, ALU.mult).then_inc(v_step, 1)
            v.wait_ge(v_step, 25)
            v.tensor_scalar(spare, m.base[0:1, :], flagr, flag, ALU.mult, ALU.add).then_inc(v_step, 1)
            v.wait_ge(v_step, 26)
            v.tensor_copy(m.first_row[:, :], spare).then_inc(v_step, 1)
            v.wait_ge(in_comp, 16)

        @block.tensor
        def _(pe):
            pe.wait_ge(v_step, 9)
            for k in range(SG + 1):
                mm = pe.matmul(m.ps[:, 0, k * NSG:(k + 1) * NSG], m.ones[0:NSG, :], diag[:, k, :], start=True, stop=True)
            mm.then_inc(bc_ready, 1)
            pe.wait_ge(v_step, 20)
            pe.transpose(m.ps[0:1, 1, 0:EP], over, m.ident[0:EP, 0:EP]).then_inc(fl_ready, 1)


def factors(nc, ctx, m, io):
    def sem(name):
        return ctx.enter_context(nc.semaphore("g_" + name))

    stat, varied, rooted, normed, turned, evacuated, used, made, stored, cmat, cleared = (sem(s) for s in (
        "stat", "varied", "rooted", "normed", "turned", "evacuated", "used", "made", "stored", "cmat", "cleared"))
    cd = m.cmat[:, :]
    BANKS = (0, 1, 0, 1, 7)

    def groups(eng, step, finish):
        step(0, 0, True)
        step(1, 1, True)
        with eng.Fori(1, NG // 2) as k:
            step(k * 2, 0, False)
            step(k * 2 + 1, 1, False)
        step(NG - 1, 0, False)
        finish(0)
    with nc.Block() as block:
        @block.vector
        def _(v):
            v.tensor_copy(cd.rearrange("p (k b) -> p k b", b=NBASE),
                          m.comp_rep.rearrange("p (o b) -> p o b", o=1).broadcast_to([P, 16, NBASE])
                          ).then_inc(cmat, 1)
            measured, root, slot_free = Level(v, "g_measured", GB), Level(v, "g_root", 1), Level(v, "g_slot_free", 1)

            def statistics(g, s):
                for j in range(GB):
                    v.bn_stats(m.stats0[:, s, j, :], m.x[:, one(g * GB + j), :]).then_inc(stat, 1)
                v.wait_ge(stat, measured.reg)
                measured.up(GB)
                for j in range(GB):
                    v.bn_aggr(m.mv0[:, s, j, :], m.stats0[:, s, j, :]).then_inc(stat, 1)
                v.wait_ge(stat, measured.reg)
                measured.up(GB)
                v.tensor_scalar(m.mv0[:, s, :, 1], m.mv0[:, s, :, 1], EPS, None, ALU.add).then_inc(varied, 1)

            def normalise(g, s, first):
                v.wait_ge(rooted, root.reg)
                root.up()
                for j in range(GB):
                    if not first:
                        v.wait_ge(turned, slot_free.reg)
                        slot_free.up()
                    v.tensor_scalar(m.hn0[:, s, j, :], m.x[:, one(g * GB + j), :], m.mv0[:, s, j, 0:1],
                                    m.rstd0[:, s, j:j + 1], ALU.subtract, ALU.mult).then_inc(normed, 1)

            def step(g, s, first):
                if not (isinstance(g, int) and g == NG - 1):
                    statistics(g + 1, 1 - s)
                normalise(g, s, first)
            statistics(0, 0)
            groups(v, step, lambda s: None)

        @block.tensor
        def _(pe):
            pe.wait_ge(cmat, 3)
            in_hn, bank_free, in_tT, out_free = (Level(pe, "g_" + s, 1) for s in ("in_hn", "bank_free", "in_tT", "out_free"))

            def product(s, j, first):
                pe.wait_ge(evacuated, in_tT.reg)
                in_tT.up()
                if not first:
                    pe.wait_ge(made, out_free.reg)
                    out_free.up()
                for c in range(2):
                    q = pe.matmul(m.ps[:, 2 + j, c * 64:(c + 1) * 64], m.tT0[:, s, j, c, :], cd,
                                  start=True, stop=True)
                q.then_inc(used, 1)

            def step(g, s, first):
                first_group = isinstance(g, int) and g == 0
                for j in range(GB):
                    pe.wait_ge(normed, in_hn.reg)
                    in_hn.up()
                    if not (first_group and j < 2):
                        pe.wait_ge(evacuated, bank_free.reg)
                        bank_free.up()
                    for c in range(2):
                        t = pe.transpose(m.ps[:, BANKS[j], c * P:(c + 1) * P], m.hn0[:, s, j, c * P:(c + 1) * P],
                                         m.ident[:, :])
                    t.then_inc(turned, 1)
                    if not first_group:
                        product(1 - s, j, first)
            groups(pe, step, lambda s: [product(s, j, False) for j in range(GB)])

        @block.scalar
        def _(act):
            in_bank, slot_free, done = (Level(act, "g_" + s, 1) for s in ("in_bank", "aslot_free", "done"))

            def take(g, j):
                act.wait_ge(used, done.reg)
                done.up()
                act.activation(m.gbuf[:, one(g * GB + j), :], m.ps[:, 2 + j, 0:P].rearrange(
                    "p (o n) -> p o n", o=1), ACT.Copy).then_inc(made, 1)

            def step(g, s, first):
                for j in range(GB):
                    act.wait_ge(turned, in_bank.reg)
                    in_bank.up()
                    if not first:
                        act.wait_ge(used, slot_free.reg)
                        slot_free.up()
                    act.activation(m.tT0[:, s, j, :, :], m.ps[:, BANKS[j], 0:2 * P].rearrange(
                        "p (c n) -> p c n", c=2), ACT.Copy).then_inc(evacuated, 1)
                    if not (isinstance(g, int) and g == 0):
                        take(g - 1, j)
            groups(act, step, lambda s: [take(NG - 1, j) for j in range(GB)])

        @block.gpsimd
        def _(gp):
            gp.memset(m.half_neg[:, :], -0.5).then_inc(cleared, 1)
            gp.wait_ge(cmat, 1)
            gp.affine_select(out=cd, in_=cd, compare_op=ALU.is_ge, fill=0.0, base=0,
                             pattern=[[-R8, 16], [0, NBASE]], channel_multiplier=1).then_inc(cmat, 1)
            gp.wait_ge(cmat, 2)
            gp.affine_select(out=cd, in_=cd, compare_op=ALU.is_ge, fill=0.0, base=R8 - 1,
                             pattern=[[R8, 16], [0, NBASE]], channel_multiplier=-1).then_inc(cmat, 1)
            gp.wait_ge(cleared, 1)
            for g in range(NG):
                gp.wait_ge(varied, g + 1)
                gp.tensor_tensor(m.rstd0[:, g % 2, :], m.mv0[:, g % 2, :, 1], m.half_neg[:, 0:1].broadcast_to([P, GB]),
                                 ALU.pow).then_inc(rooted, 1)
                rows = slice(g * R8 // NG, (g + 1) * R8 // NG)
                gp.memset(m.acc0[:, rows, :], 0.0).then_inc(cleared, 1)

        @block.sync
        def _(sp):
            for g in range(NG):
                sp.wait_ge(made, GB * (g + 1))
                sp.dma_start(io["g_table"][g * GN:(g + 1) * GN, :].rearrange("(b p) q -> p b q", p=P),
                             m.gbuf[:, g * GB:(g + 1) * GB, :]).then_inc(stored, 16)
            sp.wait_ge(stored, 16 * NG)


class Sweep:

    def __init__(self, nc, ctx, m, io, layer):
        def sem(name):
            return ctx.enter_context(nc.semaphore(f"l{layer}_{name}"))

        self.nc, self.m, self.io, self.layer, self.tag = nc, m, io, layer, f"l{layer}_"
        self.ring, self.table = ((m.ring0, io["g_table"]), (m.ring1, io["h_table"]))[layer]
        self.width = (WIN, GWIN)[layer]
        self.adds = (SG, 2)[layer]
        self.key_step, self.hot, self.summed, self.added = (
            sem(s) for s in ("key_step", "hot", "summed", "added"))
        self.src_ready = [sem(f"src_ready{p}") for p in range(2)]
        self.edges_in = sem("edges_in") if layer else None
        self.valid = ((m.hot0, m.hot1)[layer]).rearrange("p t w -> p (t w)")[:, 0:ET]
        self.gathered = [sem(f"gathered{j}") for j in range(UNR)]

    def rounds(self, eng):
        return eng.value_load(self.m.rounds[:, self.layer:self.layer + 1], min_val=0, max_val=-(-N // WIN))

    def start_sync(self, sp):
        self.taken = Level(sp, self.tag + "taken", 16)
        for p in range(2):
            self.load_indices(sp, 0, p)

    def load_indices(self, sp, it, p):
        sp.dma_start(self.m.src_now[:, p * PART:(p + 1) * PART], self.m.src[:, bass.ds(it * UNR + p * PART, PART)]
                     ).then_inc(self.src_ready[p], 16)

    def indices(self, sp, it):
        for p in range(2):
            for j in range(p * PART, (p + 1) * PART):
                sp.wait_ge(self.gathered[j], self.taken.reg)
            self.load_indices(sp, it, p)
        self.taken.up(16)

    def start_gather(self, g):
        self.indexed = [Level(g, f"{self.tag}indexed{p}", 16) for p in range(2)]
        self.ring_free = Level(g, self.tag + "ring_free", PG // 2)

    def gather_start(self, g, p):
        g.wait_ge(self.src_ready[p], self.indexed[p].reg)
        self.indexed[p].up(16)
        g.wait_ge(self.summed, self.ring_free.reg)
        self.ring_free.up(PG // 2)

    def gather_rows(self, g, k):
        for j in range(k * SG, (k + 1) * SG):
            g.indirect_dma_start(self.ring[:, j, :], None, self.table,
                                 bass.IndirectOffsetOnAxis(ap=self.m.src_now[:, j:j + 1], axis=0)
                                 ).then_inc(self.gathered[j], 16)

    def gather(self, g, p):
        self.gather_start(g, p)
        for k in range(2 * p, 2 * p + 2):
            self.gather_rows(g, k)

    def start_sums(self, pe):
        pe.sem_inc(self.summed, PG)
        names = ("hots", "landed", "bank_free")
        self.hots, self.landed, self.bank_free = (Level(pe, self.tag + s, n) for s, n in zip(names, (0, 0, self.adds)))

    def sums(self, pe, k):
        m, tiles = self.m, range(k * SG, (k + 1) * SG)
        if k == 0:
            self.landed.up(16)
        pe.wait_ge(self.added, self.bank_free.reg)
        self.bank_free.up(self.adds)
        if k % 2 == 0 or self.layer == 0:
            pe.wait_ge(self.hot, self.hots.up((1, 3)[self.layer]))
        if self.layer == 0:
            for j in tiles:
                pe.wait_ge(self.gathered[j], self.landed.reg)
                mm = pe.matmul(m.ps[:, k % 2, (j % SG) * P:(j % SG + 1) * P], self.ring[:, j, :], m.hot0[:, j % (2 * SG), :],
                               start=True, stop=True)
        else:
            for c in range(2):
                for j in tiles:
                    if c == 0:
                        pe.wait_ge(self.gathered[j], self.landed.reg)
                    pe.matmul(m.ps[:, k % 2, c * GWIN:(c + 1) * GWIN], self.ring[:, j, c * P:(c + 1) * P],
                              m.hot1[:, j, :], start=(j % SG == 0), stop=(j % SG == SG - 1))
            for j in tiles:
                mm = pe.matmul(m.ps[0:R16, k % 2, 2 * GWIN:3 * GWIN], m.hot_type[:, j, :], m.hot1b[:, j, :],
                               start=(j % SG == 0), stop=(j % SG == SG - 1))
        mm.then_inc(self.summed, 1)

    def start_windows(self, v):
        m = self.m
        self.step, self.ready = Level(v, self.tag + "step", 1), Level(v, self.tag + "ready", PG + 1)
        self.own = Level(v, self.tag + "own", 2 * self.adds)
        v.memset(m.wincol[:, :], 0.0).then_inc(self.added, 2 * self.adds)
        v.wait_ge(self.added, 2 * self.adds)

    def keys(self, v, walk):
        m, width = self.m, self.width

        def link(ins):
            ins.then_inc(self.key_step, 1)
            v.wait_ge(self.key_step, self.step.reg)
            self.step.up()

        def by_group(t):
            return t.rearrange("p (g k) -> p g k", k=SG)
        key, valid, dst = m.key[:, :], self.valid, m.dst[:, :]
        if walk:
            link(v.tensor_scalar(key, dst, m.wincol[:, :], None, ALU.subtract))
            link(v.tensor_scalar(m.walk_row[:, :], m.base[0:1, 0:PART], 0.0, m.wincol[0:1, :], ALU.mult, ALU.add))
        elif self.layer == 0:
            link(v.tensor_tensor(key, dst, m.base[0:EP, 0:ET], ALU.subtract))
        else:
            link(v.tensor_tensor(by_group(key), by_group(dst), m.base[0:EP, ET:].rearrange(
                "p (g o) -> p g o", o=1).broadcast_to([EP, NSG, SG]), ALU.subtract))
        link(v.tensor_scalar(valid, key, 0.0, None, ALU.is_ge))
        link(v.scalar_tensor_tensor(out=valid, in0=key, scalar=float(width), in1=valid, op0=ALU.is_lt, op1=ALU.mult))
        if self.layer == 0:
            link(v.scalar_tensor_tensor(out=key, in0=m.type[:, :], scalar=float(WIN), in1=key,
                                        op0=ALU.mult, op1=ALU.add))
        link(v.scalar_tensor_tensor(out=key, in0=key, scalar=1.0, in1=valid, op0=ALU.add, op1=ALU.mult))
        link(v.tensor_scalar(key, key, -1.0, None, ALU.add))
        if walk:
            link(v.scalar_tensor_tensor(out=dst, in0=valid, scalar=NONE, in1=dst, op0=ALU.mult, op1=ALU.add))
            link(v.tensor_scalar(m.wincol[:, :], m.wincol[:, :], float(width), None, ALU.add))

    def one_hots(self, v, it, k):
        m, n = self.m, SG * (1 + self.layer)
        a = k * SG

        def column(t):
            return t[:, bass.ds(it * UNR + a, n)].rearrange("p (t o) -> p t o", o=1)

        def row(w):
            return m.iota[0:EP, 0:w].rearrange("p (o w) -> p o w", o=1).broadcast_to([EP, n, w])
        if self.layer == 0:
            slot = k % 2 * SG
            v.tensor_tensor(m.hot0[:, slot:slot + SG, :], row(P), column(m.key).broadcast_to([EP, n, P]), ALU.is_equal
                            ).then_inc(self.hot, 1)
        else:
            v.tensor_tensor(m.hot1[:, a:a + n, :], row(GWIN), column(m.key).broadcast_to([EP, n, GWIN]), ALU.is_equal
                            ).then_inc(self.hot, 1)
            v.tensor_tensor(m.hot_type[:, a:a + n, :], row(R16), column(m.type).broadcast_to([EP, n, R16]),
                            ALU.is_equal).then_inc(self.hot, 1)
            v.tensor_tensor(m.hot1b[:, a:a + n, :], row(GWIN), column(m.key).broadcast_to([EP, n, GWIN]), ALU.is_equal
                            ).then_inc(self.hot, 1)

    def starts(self, v, it, p, walk=False):
        n = PART if self.layer == 0 else PG // 2
        table = self.m.walk_row[0:1, 0:n] if walk else self.m.first_row[
            0:1, bass.ds(it * (2 * n) + (p * n + ET * self.layer), n)]
        return self.nc.values_load_multi_w_load_instructions(
            table, engines=[mybir.EngineType.DVE], min_val=0, max_val=NP,
            skip_runtime_bounds_check_because="a window starts at a node or at the padding")[1]

    def add(self, v, k, at, windows=range(SG)):
        m, bank = self.m, k % 2
        if 0 in windows:
            v.wait_ge(self.summed, self.ready.reg)
            self.ready.up()
        if self.layer == 0:
            for i in windows:
                v.wait_ge(self.added, self.own.reg)
                self.own.up()
                win = m.acc0[:, :, bass.ds(at[bank * SG + i], WIN)]
                v.tensor_tensor(win, win, m.ps[:, bank, i * P:(i + 1) * P].rearrange("p (k w) -> p k w", k=R8),
                                ALU.add).then_inc(self.added, 1)
        else:
            v.wait_ge(self.added, self.own.reg)
            self.own.up(2)
            win = m.acc1[:, 0:2, bass.ds(at[bank], GWIN)]
            v.tensor_tensor(win, win, m.ps[:, bank, 0:2 * GWIN].rearrange("p (k w) -> p k w", k=2), ALU.add
                            ).then_inc(self.added, 1)
            win = m.acc1[0:R16, 2, bass.ds(at[bank], GWIN)]
            v.tensor_tensor(win, win, m.ps[0:R16, bank, 2 * GWIN:3 * GWIN], ALU.add).then_inc(self.added, 1)

    def walk_sync(self, sp):
        rounds = self.rounds(sp)
        with sp.If(rounds > 0):
            with sp.Fori(0, rounds):
                with sp.Fori(1, NIT) as it:
                    self.indices(sp, it)
                self.indices(sp, 0)

    def walk_gather(self, g):
        rounds = self.rounds(g)
        with g.If(rounds > 0):
            with g.Fori(0, rounds):
                with g.Fori(0, NIT):
                    for p in range(2):
                        self.gather(g, p)

    def walk_sums(self, pe):
        rounds = self.rounds(pe)
        with pe.If(rounds > 0):
            with pe.Fori(0, rounds):
                with pe.Fori(0, NIT):
                    for k in range(PG):
                        self.sums(pe, k)

    def count_walk(self, eng, level):
        rounds = self.rounds(eng)
        with eng.If(rounds > 0):
            with eng.Fori(0, rounds):
                level.up(self.adds * PG * NIT)

    def walk_windows(self, v):
        rounds = self.rounds(v)
        with v.If(rounds > 0):
            with v.Fori(0, rounds):
                self.keys(v, walk=True)
                with v.Fori(0, NIT) as it:
                    for p in range(2):
                        for k in range(2 * p, 2 * p + 2):
                            if self.layer == 0 or k % 2 == 0:
                                self.one_hots(v, it, k)
                        at = self.starts(v, it, p, walk=True)
                        for k in range(2 * p, 2 * p + 2):
                            self.add(v, k, at)


def turns(eng, turn, last, tail=0):
    def stages(i):
        return [i < NIT] + [0 <= i - 1 - k < NB for k in range(1, last + 1)]
    for i in range(last + 2):
        turn(i, stages(i))
    with eng.Fori(last + 2, NIT - tail) as i:
        turn(i, [True] * (last + 1))
    for i in range(NIT - tail, NIT + last + 1):
        turn(i, stages(i))


def first(i, n):
    return isinstance(i, int) and i < n


def layer0(nc, ctx, m, io):
    def sem(name):
        return ctx.enter_context(nc.semaphore("f_" + name))

    (loaded, setup, copied, agg_half, x_agg, x_mix, st_step, varied, rooted, norm1, norm2, turned1, turned2, in_tT, in_hT, logit_task,
     l1_task, a1_done, l2_task, a2_done, g_step, exped, wt_task, wt_done, spread, weighted, l3_task, stored) = (
        sem(s) for s in ("loaded", "setup", "copied", "agg_half", "x_agg", "x_mix", "st_step", "varied", "rooted", "norm1", "norm2",
                         "turned1", "turned2", "in_tT", "in_hT", "logit_task", "l1_task", "a1_done", "l2_task",
                         "a2_done", "g_step", "exped", "wt_task", "wt_done", "spread", "weighted", "l3_task", "stored"))
    s = Sweep(nc, ctx, m, io, 0)
    AG, TR, L1A, L1B, L2, L3 = 2, 3, 4, 5, 6, 7
    GSTEPS = 14
    loads = [
        (m.basis, io["basis"].rearrange("(r p) d -> p r d", p=P)),
        (m.bias0[0:1, :], io["gnn_bias"].rearrange("(o d) -> o d", o=1)),
        (m.gW, io["gW"].rearrange("(c p) e -> p c e", p=P)),
        (m.gb, io["gb"].rearrange("(o d) -> o d", o=1).broadcast_to([P, NE0])),
        (m.sW1, io["sW1"].rearrange("(c p) h -> p c h", p=P)), (m.sW2, io["sW2"].rearrange("(c p) h -> p c h", p=P)),
        (m.sW3, io["sW3"]), (m.eW2, io["eW2"].rearrange("e p h -> p e h")),
        (m.eW3, io["eW3q"].rearrange("q p d -> p q d")), (m.b1, io["b1T"]), (m.b2, io["b2T"]),
        (m.b3[0:NE0, :], io["eb3"]), (m.b3[NE0:NE0 + 1, :], io["sb3"].rearrange("(o d) -> o d", o=1)),
    ] + [(m.eW1[:, e, :, :], io["eW1"][e].rearrange("(c p) h -> p c h", p=P)) for e in range(NE0)]

    def at(b):
        return bass.ds(b * P, P)

    def flat(t):
        return t.rearrange("p (o d) -> p o d", o=1)
    with nc.Block() as block:
        @block.sync
        def _(sp):
            s.start_sync(sp)
            for dst, src in loads:
                sp.dma_start(dst, src).then_inc(loaded, 16)
            s.walk_sync(sp)
            ready = Level(sp, "f_sready", 1)

            def turn(i, stages):
                sweep, out = stages[0], stages[-1]
                if out:
                    sp.wait_ge(norm2, ready.reg)
                    sp.dma_start(io["h_table"][at(i - 7), :], m.hn2).then_inc(stored, 16)
                    ready.up()
                if sweep and not (isinstance(i, int) and i == NIT - 1):
                    s.indices(sp, i + 1)
            turns(sp, turn, 6, tail=1)
            sp.wait_ge(stored, 16 * NB)

        @block.gpsimd
        def _(g):
            g.memset(m.sel[0:NE0, :, :], 1.0).then_inc(setup, 1)
            sel = m.sel[0:NE0, :, :].rearrange("e q c -> e (q c)")
            g.memset(m.low, 1.0).then_inc(setup, 1)
            g.memset(m.w5, 1.0).then_inc(setup, 1)
            g.memset(m.mv[:, :, :], 1.0).then_inc(setup, 1)
            g.wait_ge(setup, 4)
            g.affine_select(out=sel, in_=sel, compare_op=ALU.is_ge, fill=0.0, base=0, pattern=[[1, 2 * P]],
                            channel_multiplier=-64).then_inc(setup, 1)
            g.affine_select(out=m.low, in_=m.low, compare_op=ALU.is_gt, fill=0.0, base=0,
                            pattern=[[1, NE0], [-1, NE0]], channel_multiplier=0).then_inc(setup, 1)
            g.wait_ge(setup, 6)
            g.affine_select(out=sel, in_=sel, compare_op=ALU.is_ge, fill=0.0, base=63, pattern=[[-1, 2 * P]],
                            channel_multiplier=64).then_inc(setup, 1)
            s.start_gather(g)
            s.walk_gather(g)
            has_var = Level(g, "f_has_var", 1)

            def turn(i, stages):
                sweep = stages[0]
                for p in range(2):
                    if sweep:
                        s.gather_start(g, p)
                        s.gather_rows(g, 2 * p)
                    if p == 1 and (stages[2] or stages[5]):
                        g.wait_ge(varied, has_var.reg)
                        has_var.up()
                        g.tensor_tensor(m.rstd[:, :], m.mv[:, :, 1], m.half_neg[:, :], ALU.pow).then_inc(rooted, 1)
                    if sweep:
                        s.gather_rows(g, 2 * p + 1)
            turns(g, turn, 6)

        @block.tensor
        def _(pe):
            s.start_sums(pe)
            s.walk_sums(pe)
            pe.wait_ge(loaded, 16 * len(loads))
            pe.wait_ge(setup, 7)
            (gates, wt, half, agfree, n1, n2, t2free, tt, l2free, l1free, l3free, wgt, a1, lgfree) = (
                Level(pe, "f_" + n, k) for n, k in (
                    ("gates", GSTEPS), ("wt", 1), ("half", 1), ("agfree", 1), ("n1", 1), ("n2", 1),
                    ("t2free", 1), ("tt", 1), ("l2free", 1), ("l1free", 2), ("l3free", 1), ("wgt", 1), ("a1", 2), ("lgfree", 1)))

            def aggregate(half_of):
                pe.wait_ge(copied, half.reg)
                half.up()
                for r in range(R8 // 2):
                    mm = pe.matmul(m.ps[:, AG, 0:D], m.sring[:, r, :], m.basis[:, half_of * 4 + r, :],
                                   start=(half_of + r == 0), stop=False)
                if half_of:
                    mm = pe.matmul(m.ps[:, AG, 0:D], m.ones[0:1, :], m.bias0[0:1, :], start=False, stop=True)
                mm.then_inc(agg_half, 1)

            def turn(i, stages):
                sweep, agg, norm_1, ffn, mix, norm_2, out = stages
                if sweep:
                    s.sums(pe, 0)
                if mix:
                    pe.wait_ge(g_step, gates.reg)
                    gates.up(GSTEPS)
                    pe.transpose(m.ps[0:NE0 + 1, L1B, 2 * P:3 * P], m.w5, m.ident[:, :]).then_inc(wt_task, 1)
                if (ffn or out) and not first(i, 8):
                    pe.wait_ge(in_hT, t2free.reg)
                    t2free.up()
                if ffn:
                    pe.wait_ge(norm1, n1.reg)
                    n1.up()
                    for c in range(2):
                        t = pe.transpose(m.ps[:, TR, c * P:(c + 1) * P], m.hn1[:, c * P:(c + 1) * P], m.ident[:, :])
                    t.then_inc(turned1, 1)
                if agg:
                    if not first(i, 3):
                        pe.wait_ge(x_agg, agfree.reg)
                        agfree.up()
                    aggregate(0)
                if ffn:
                    pe.wait_ge(in_tT, tt.reg)
                    tt.up()
                if out:
                    pe.wait_ge(norm2, n2.reg)
                    n2.up()
                    for c in range(2):
                        t = pe.transpose(m.ps[:, TR, (2 + c) * P:(3 + c) * P], m.hn2[:, c * P:(c + 1) * P],
                                         m.ident[:, :])
                    t.then_inc(turned2, 1)
                if ffn:
                    if not first(i, 5):
                        pe.wait_ge(a2_done, l2free.reg)
                        l2free.up()
                    for c in range(2):
                        mm = pe.matmul(m.ps[:, L2, 3 * P:3 * P + NE0], m.tT1[:, c, :], m.gW[:, c, :],
                                       start=(c == 0), stop=(c == 1))
                    mm.then_inc(logit_task, 1)
                    if not first(i, 5):
                        pe.wait_ge(a1_done, l1free.reg)
                        l1free.up(2)
                if mix:
                    pe.wait_ge(wt_done, wt.reg)
                    wt.up()
                if ffn:
                    for k in range(6):
                        for c in range(2):
                            w = m.sW1[:, c, k * P:(k + 1) * P] if k < 2 else m.eW1[:, k - 2, c, :]
                            mm = pe.matmul(m.ps[:, L1A + k // 4, k % 4 * P:(k % 4 + 1) * P], w, m.tT1[:, c, :],
                                           start=(c == 0), stop=(c == 1))
                        if k in (3, 5):
                            mm.then_inc(l1_task, 1)
                if sweep:
                    s.sums(pe, 1)
                if mix:
                    if not first(i, 6):
                        pe.wait_ge(x_mix, l3free.reg)
                        l3free.up()
                    for q in range(2):
                        mm = pe.matmul(m.ps[:, L3, q * P:(q + 1) * P], m.sel[0:NE0, q, :], m.wT[0:NE0, :],
                                       start=True, stop=True)
                    mm.then_inc(spread, 1)
                if sweep:
                    s.sums(pe, 2)
                if agg:
                    aggregate(1)
                if mix:
                    pe.wait_ge(weighted, wgt.reg)
                    wgt.up()
                    o = m.ps[:, L3, 2 * P:2 * P + D]
                    pe.matmul(o, m.a2[:, 0, :], m.sW3, start=True, stop=False)
                    for q in range(2):
                        pe.matmul(o, m.a2[:, 1 + q, :], m.eW3[:, q, :], start=False, stop=False)
                    pe.matmul(o, m.wT[0:NE0 + 1, :], m.b3[0:NE0 + 1, :], start=False, stop=True).then_inc(l3_task, 1)
                if sweep:
                    s.sums(pe, 3)
                if ffn:
                    pe.wait_ge(a1_done, a1.reg)
                    a1.up(2)
                    pe.wait_ge(g_step, lgfree.reg)
                    lgfree.up(GSTEPS)
                    for c in range(2):
                        pe.matmul(m.ps[:, L2, 0:P], m.sW2[:, c, :], m.a1[:, c, :], start=(c == 0), stop=(c == 1))
                    for q in range(2):
                        for e in range(2):
                            x = 2 * q + e
                            mm = pe.matmul(m.ps[64 * e:64 * e + 64, L2, (1 + q) * P:(2 + q) * P], m.eW2[:, x, :],
                                           m.a1[:, 2 + x, :], start=True, stop=True)
                    mm.then_inc(l2_task, 1)
            turns(pe, turn, 6)

        @block.scalar
        def _(act):
            (wt, covered, sfree, t1, t2, ttfree, l1, a1free, lg, e2, l2, a2free, wtfree) = (
                Level(act, "f_a" + n, k) for n, k in (
                    ("wt", 1), ("covered", s.adds * (2 + 2 * PG)), ("sfree", 1), ("t1", 1), ("t2", 1), ("ttfree", 2),
                    ("l1", 1), ("a1free", 1), ("lg", 2), ("e2", 6), ("l2", 1), ("a2free", 1), ("wtfree", 1)))
            s.count_walk(act, covered)
            act.wait_ge(loaded, 16 * len(loads))

            def turn(i, stages):
                sweep, agg, norm_1, ffn, mix, norm_2, out = stages
                if agg:
                    if sweep or i == NIT:
                        act.wait_ge(s.added, covered.reg)
                        covered.up(s.adds * PG)
                    if not first(i, 3):
                        act.wait_ge(agg_half, sfree.reg)
                        sfree.up()
                    act.activation(m.sring, m.acc0[:, 0:R8 // 2, at(i - 2)], ACT.Copy).then_inc(copied, 1)
                if mix:
                    if not first(i, 6):
                        act.wait_ge(l3_task, wtfree.reg)
                        wtfree.up()
                    act.wait_ge(wt_task, wt.reg)
                    wt.up()
                    act.activation(m.wT[0:NE0 + 1, :], m.ps[0:NE0 + 1, L1B, 2 * P:3 * P], ACT.Copy).then_inc(wt_done, 1)
                if ffn:
                    if not first(i, 5):
                        act.wait_ge(l1_task, ttfree.reg)
                        ttfree.up(2)
                    act.wait_ge(turned1, t1.reg)
                    t1.up()
                    act.activation(m.tT1, m.ps[:, TR, 0:D].rearrange("p (c n) -> p c n", c=2), ACT.Copy
                                   ).then_inc(in_tT, 1)
                if agg:
                    act.wait_ge(agg_half, sfree.reg)
                    sfree.up()
                    act.activation(m.sring, m.acc0[:, R8 // 2:R8, at(i - 2)], ACT.Copy).then_inc(copied, 1)
                if out:
                    act.wait_ge(turned2, t2.reg)
                    t2.up()
                    act.activation(m.hT[:, :, at(i - 7)], m.ps[:, TR, D:2 * D].rearrange("p (c n) -> p c n", c=2),
                                   ACT.Copy).then_inc(in_hT, 1)
                if ffn:
                    act.wait_ge(g_step, lg.reg)
                    lg.up(GSTEPS)
                    act.activation(m.gate[:, 1, :], m.gate[:, 0, :], ACT.Exp, bias=m.gcol[:, 0:1], scale=-1.0
                                   ).then_inc(exped, 1)
                    if not first(i, 5):
                        act.wait_ge(l2_task, a1free.reg)
                        a1free.up()
                    for part, ks in enumerate((range(4), range(4, 6))):
                        act.wait_ge(l1_task, l1.reg)
                        l1.up()
                        for k in ks:
                            ins = act.activation(m.a1[:, k, :], m.ps[:, L1A + k // 4, k % 4 * P:(k % 4 + 1) * P], ACT.Relu,
                                                 bias=m.b1[:, k:k + 1])
                        ins.then_inc(a1_done, 1)
                if ffn:
                    act.wait_ge(g_step, e2.reg)
                    e2.up(GSTEPS)
                    act.activation(m.gate[:, 1, :], m.gate[:, 2, :], ACT.Exp, bias=m.gcol[:, 3:4]).then_inc(exped, 1)
                    if not first(i, 5):
                        act.wait_ge(l3_task, a2free.reg)
                        a2free.up()
                    act.wait_ge(l2_task, l2.reg)
                    l2.up()
                    for k in range(3):
                        ins = act.activation(m.a2[:, k, :], m.ps[:, L2, k * P:(k + 1) * P], ACT.Relu, bias=m.b2[:, k:k + 1])
                    ins.then_inc(a2_done, 1)
            turns(act, turn, 6)

        @block.vector
        def _(v):
            (root, n1free, n2free, st, lg, gs, e1, e2, wtfree, spr, a2in, ag, l3, xa_done, xm_done, sl) = (Level(v, "f_v" + n, k) for n, k in (
                ("root", 1), ("n1free", 1), ("n2free", 1), ("st", 16), ("lg", 1), ("gs", 0), ("e1", 1), ("e2", 2),
                ("wtfree", 1), ("spr", 1), ("a2in", 1), ("ag", 2), ("l3", 1), ("xa_done", 1), ("xm_done", 1),
                ("sl", 0)))
            s.start_windows(v)
            v.wait_ge(setup, 7)
            s.walk_windows(v)
            s.keys(v, walk=False)
            v.wait_ge(loaded, 16 * len(loads))
            neg, expo, prob = m.gate[:, 0, :], m.gate[:, 1, :], m.gate[:, 2, :]

            def turn(i, stages):
                sweep, agg, norm_1, ffn, mix, norm_2, out = stages
                more = sweep and not (isinstance(i, int) and i == NIT - 1)
                if sweep:
                    low, high = s.starts(v, i, 0), s.starts(v, i, 1)
                def window(k, *tiles):
                    if sweep:
                        s.add(v, k, (low, high)[k // 2], tiles)

                def gate_step(op, *args, wait=True, **named):
                    if ffn:
                        if wait:
                            v.wait_ge(g_step, gs.reg)
                        op(*args, **named).then_inc(g_step, 1)
                        gs.up()
                other = prob.rearrange("p (o f) -> p o f", o=1).broadcast_to([P, NE0, NE0])
                this = prob.rearrange("p (e o) -> p e o", o=1).broadcast_to([P, NE0, NE0])
                window(0, 0, 1, 2, 3)
                if sweep:
                    s.one_hots(v, i, 2)
                if ffn:
                    v.wait_ge(logit_task, lg.reg)
                    lg.up()
                gate_step(v.scalar_tensor_tensor, out=neg, in0=m.ps[:, L2, 3 * P:3 * P + NE0], scalar=-1.0, in1=m.gb,
                          op0=ALU.mult, op1=ALU.subtract, wait=False)
                window(1, 0)
                gate_step(v.tensor_reduce, m.gcol[:, 0:1], neg, AX.X, ALU.min)
                window(1, 1, 2)
                if ffn:
                    v.wait_ge(exped, e1.reg)
                    e1.up(2)
                gate_step(v.tensor_reduce, m.gcol[:, 1:2], expo, AX.X, ALU.add)
                window(1, 3)
                gate_step(v.reciprocal, m.gcol[:, 2:3], m.gcol[:, 1:2])
                if sweep:
                    s.one_hots(v, i, 3)
                gate_step(v.tensor_scalar, m.gcol[:, 3:4], m.gcol[:, 2:3], -1.0, None, ALU.mult)
                gate_step(v.tensor_scalar, prob, expo, m.gcol[:, 2:3], None, ALU.mult, wait=False)
                if mix:
                    v.wait_ge(a2_done, a2in.reg)
                    a2in.up()
                    v.wait_ge(spread, spr.reg)
                    spr.up()
                    v.tensor_tensor(m.a2[:, 1:3, :], m.a2[:, 1:3, :], m.ps[:, L3, 0:2 * P].rearrange(
                        "p (c n) -> p c n", c=2), ALU.mult).then_inc(weighted, 1)
                window(2, 0)
                gate_step(v.tensor_tensor, m.comp[:, :, 0, :], other, this, ALU.is_gt)
                gate_step(v.tensor_tensor, m.comp[:, :, 1, :], other, this, ALU.is_equal, wait=False)
                window(2, 1)
                gate_step(v.tensor_tensor, m.comp[:, :, 1, :], m.comp[:, :, 1, :], m.low, ALU.mult)
                window(2, 2)
                gate_step(v.tensor_reduce, m.rank, m.comp.rearrange("p e a f -> p e (a f)"), AX.X, ALU.add)
                window(2, 3)
                if ffn:
                    v.wait_ge(exped, e2.reg)
                    e2.up(2)
                gate_step(v.scalar_tensor_tensor, out=neg, in0=m.rank, scalar=2.0, in1=expo, op0=ALU.is_lt,
                          op1=ALU.mult)
                if more:
                    s.one_hots(v, i + 1, 0)
                if agg:
                    xa = m.x[:, one(i - 2), :]
                    v.wait_ge(agg_half, ag.reg)
                    ag.up(2)
                    v.scalar_tensor_tensor(out=xa, in0=flat(m.ps[:, AG, 0:D]), scalar=0.0, in1=xa, op0=ALU.max,
                                           op1=ALU.add).then_inc(x_agg, 1)
                window(3, 0)
                gate_step(v.tensor_reduce, m.gcol[:, 1:2], neg, AX.X, ALU.add)
                window(3, 1)
                gate_step(v.reciprocal, m.gcol[:, 2:3], m.gcol[:, 1:2])
                window(3, 2)
                if ffn and not first(i, 5):
                    v.wait_ge(wt_task, wtfree.reg)
                    wtfree.up()
                gate_step(v.tensor_scalar, m.w5[:, 0:NE0], neg, m.gcol[:, 2:3], None, ALU.mult)
                window(3, 3)
                if more:
                    s.one_hots(v, i + 1, 1)
                if mix:
                    xm = m.x[:, one(i - 5), :]
                    v.wait_ge(l3_task, l3.reg)
                    l3.up()
                    v.tensor_tensor(xm, xm, flat(m.ps[:, L3, 2 * P:2 * P + D]), ALU.add).then_inc(x_mix, 1)
                if norm_1 or norm_2:
                    v.wait_ge(rooted, root.reg)
                    root.up()
                if norm_1:
                    if not first(i, 4):
                        v.wait_ge(turned1, n1free.reg)
                        n1free.up()
                    v.tensor_scalar(flat(m.hn1), m.x[:, one(i - 3), :], m.mv[:, 0, 0:1], m.rstd[:, 0:1],
                                    ALU.subtract, ALU.mult).then_inc(norm1, 1)
                if norm_2:
                    if not first(i, 7):
                        v.wait_ge(turned2, n2free.reg)
                        n2free.up()
                        v.wait_ge(stored, st.reg)
                        st.up(16)
                    v.tensor_scalar(flat(m.hn2), m.x[:, one(i - 6), :], m.mv[:, 1, 0:1], m.rstd[:, 1:2],
                                    ALU.subtract, ALU.mult).then_inc(norm2, 1)
                if agg:
                    v.wait_ge(x_agg, xa_done.reg)
                    xa_done.up()
                    v.bn_stats(m.stats[:, 0, :], m.x[:, one(i - 2), :]).then_inc(st_step, 1)
                if mix:
                    v.wait_ge(x_mix, xm_done.reg)
                    xm_done.up()
                    v.bn_stats(m.stats[:, 1, :], m.x[:, one(i - 5), :]).then_inc(st_step, 1)
                if agg or mix:
                    sl.up(agg + mix)
                    v.wait_ge(st_step, sl.reg)
                    sl.up(agg + mix)
                    for k in range(2):
                        if (agg, mix)[k]:
                            v.bn_aggr(m.mv[:, k, :], m.stats[:, k, :]).then_inc(st_step, 1)
                    v.wait_ge(st_step, sl.reg)
                    v.tensor_scalar(m.mv[:, :, 1], m.mv[:, :, 1], EPS, None, ALU.add).then_inc(varied, 1)
            for k in range(2):
                s.one_hots(v, 0, k)
            turns(v, turn, 6, tail=1)


def layer1(nc, ctx, m, io):
    def sem(name):
        return ctx.enter_context(nc.semaphore("c_" + name))

    (loaded, setup, rel_task, red, rz_task, n_task, rz_read, gate_step, pre, tanhed, mix_step, x_turned, x_step, varied,
     rooted, normed, h_turned, evacuated, kept, hid_task, gelued, logit_task, logit_read, zeroed, brz_ready,
     lt_done, lb_task) = (sem(s) for s in (
         "loaded", "setup", "rel_task", "red", "rz_task", "n_task", "rz_read", "gate_step", "pre", "tanhed", "mix_step",
         "x_turned", "x_step", "varied", "rooted", "normed", "h_turned", "evacuated", "kept", "hid_task", "gelued",
         "logit_task", "logit_read", "zeroed", "brz_ready",
         "lt_done", "lb_task"))
    s = Sweep(nc, ctx, m, io, 1)
    RZ, NN, HIDA, REL, TURN = 2, 3, 4, 6, 7
    hn, tT = m.hn, m.tT
    stats, mv, rstd, half_neg = m.stats[:, 0, :], m.mv[:, 0, :], m.rstd[:, 0:1], m.half_neg[:, 0:1]
    loads = [(m.wih, io["w_ihT"].rearrange("(c p) g -> p c g", p=P)),
             (m.whh, io["w_hhT"].rearrange("(c p) g -> p c g", p=P)),
             (m.rel[0:R16, :], io["rel"]), (m.bih, io["b_ihT"]), (m.bhh, io["b_hhT"]),
             (m.W1, io["W1"].rearrange("(c p) h -> p c h", p=P)), (m.Wg, io["Wg"].rearrange("(c p) e -> p c e", p=P)),
             (m.bg, io["bg"].rearrange("(o d) -> o d", o=1).broadcast_to([P, NE1])), (m.bf1, io["bf1T"])]

    def at(b):
        return bass.ds(b * P, P)
    with nc.Block() as block:
        @block.sync
        def _(sp):
            sp.dma_start(m.key[:, :].bitcast(I32), io["dst"]).then_inc(s.edges_in, 16)
            sp.dma_start(s.valid.bitcast(I32), io["t16"]).then_inc(s.edges_in, 16)
            s.start_sync(sp)
            for dst, src in loads:
                sp.dma_start(dst, src).then_inc(loaded, 16)
            s.walk_sync(sp)
            with sp.Fori(1, NIT) as it:
                s.indices(sp, it)
            sp.wait_ge(setup, 2)
            sp.dma_start(io["slots_in"].rearrange("(p r) c -> p r c", p=P),
                         m.zeros.rearrange("p (o c) -> p o c", o=1).broadcast_to([P, TILES, D])).then_inc(zeroed, 16)
            sp.wait_ge(mix_step, 3 * NB)
            for e in range(NE1):
                sp.dma_start(m.Wd[:, e, :, :], io["Wd"][e].rearrange("(c p) d -> p c d", p=P)).then_inc(m.wd_in, 16)
            sp.dma_start(m.bd, io["bd"].rearrange("(o e) d -> o e d", o=1).broadcast_to([P, NE1, D])).then_inc(m.wd_in, 16)
            sp.wait_ge(zeroed, 16)

        @block.gpsimd
        def _(g):
            g.memset(m.zeros, 0.0).then_inc(setup, 1)
            s.start_gather(g)
            s.walk_gather(g)
            has_var = Level(g, "c_has_var", 1)

            def turn(i, stages):
                sweep, root = stages[0], stages[3]
                for p in range(2):
                    if sweep:
                        s.gather_start(g, p)
                        s.gather_rows(g, 2 * p)
                    if p == 1 and root:
                        g.wait_ge(varied, has_var.reg)
                        has_var.up()
                        g.tensor_tensor(rstd, mv[:, 1:2], half_neg, ALU.pow).then_inc(rooted, 1)
                    if sweep:
                        s.gather_rows(g, 2 * p + 1)
            turns(g, turn, 5)

        @block.tensor
        def _(pe):
            s.start_sums(pe)
            s.walk_sums(pe)
            pe.wait_ge(loaded, 16 * len(loads))
            (covered, lread, red_in, rz_free, n_free, mixed, xread, hready, tready, hfree, gdone, ltready) = (
                Level(pe, "c_" + n, k) for n, k in (
                    ("covered", 0), ("lread", 1), ("red_in", 3), ("rz_free", 1), ("n_free", 1), ("mixed", 3),
                    ("xread", 1), ("hready", 1), ("tready", 1), ("hfree", 1), ("gdone", 2), ("ltready", 1)))
            covered.up(s.adds * (2 + PG * 2))
            s.count_walk(pe, covered)

            def turn(i, stages):
                sweep, cell, back, norm, hid, logit = stages
                if hid:
                    pe.wait_ge(normed, hready.reg)
                    hready.up()
                    for c in range(2):
                        t = pe.transpose(m.ps[:, REL, c * P:(c + 1) * P], hn[:, c * P:(c + 1) * P], m.ident[:, :])
                    t.then_inc(h_turned, 1)
                if norm:
                    pe.wait_ge(x_step, xread.reg)
                    xread.up(3)
                if logit:
                    if not back and i > NIT + 3:
                        pe.wait_ge(logit_read, lread.reg)
                        lread.up()
                    pe.wait_ge(gelued, gdone.reg)
                    gdone.up(2)
                    for k in range(MH):
                        mm = pe.matmul(m.ps[0:NE1, TURN, 2 * P:3 * P], m.Wg[:, k, :], m.H0[:, k, :],
                                       start=(k == 0), stop=(k == MH - 1))
                    mm.then_inc(logit_task, 1)
                if sweep:
                    s.sums(pe, 0)
                if logit:
                    pe.wait_ge(lt_done, ltready.reg)
                    ltready.up()
                    pe.matmul(m.ps[:, TURN, 3 * P:3 * P + NE1], m.lt[0:NE1, :], m.ident[0:NE1, 0:NE1],
                              start=True, stop=True).then_inc(lb_task, 1)
                if hid:
                    pe.wait_ge(evacuated, tready.reg)
                    tready.up()
                if cell:
                    if sweep or i == NIT:
                        pe.wait_ge(s.added, covered.reg)
                        covered.up(s.adds * PG)
                    for c in range(2):
                        mm = pe.matmul(m.ps[:, REL, (2 + c) * P:(3 + c) * P], m.rel[0:R16, c * P:(c + 1) * P],
                                       m.acc1[0:R16, 2, at(i - 2)], start=True, stop=True)
                    mm.then_inc(rel_task, 1)
                if hid:
                    for half in range(2):
                        if not first(i, 6):
                            pe.wait_ge(gelued, hfree.reg)
                            hfree.up()
                        for k in range(4 * half, 4 * half + 4):
                            for c in range(2):
                                mm = pe.matmul(m.ps[:, HIDA + half, (k % 4) * P:(k % 4 + 1) * P],
                                               m.W1[:, c, k * P:(k + 1) * P], tT[:, c, :], start=(c == 0), stop=(c == 1))
                        mm.then_inc(hid_task, 1)
                if back:
                    pe.wait_ge(mix_step, mixed.reg)
                    mixed.up(3)
                    if logit:
                        pe.wait_ge(logit_read, lread.reg)
                        lread.up()
                    for c in range(2):
                        t = pe.transpose(m.ps[:, TURN, c * P:(c + 1) * P], m.gn[:, c, :], m.ident[:, :])
                    t.then_inc(x_turned, 1)
                if sweep:
                    s.sums(pe, 1)
                if sweep:
                    s.sums(pe, 2)
                if cell:
                    pe.wait_ge(red, red_in.reg)
                    red_in.up()
                    if not first(i, 3):
                        pe.wait_ge(rz_read, rz_free.reg)
                        rz_free.up()
                    for gate in range(2):
                        for c in range(2):
                            col = slice((2 * gate + c) * P, (2 * gate + c + 1) * P)
                            for f in range(2):
                                pe.matmul(m.ps[:, RZ, col], m.whh[:, f, col], m.hT[:, f, at(i - 2)],
                                          start=(f == 0), stop=False)
                            for f in range(2):
                                mm = pe.matmul(m.ps[:, RZ, col], m.wih[:, f, col], m.acc1[:, f, at(i - 2)],
                                               start=False, stop=(f == 1))
                    mm.then_inc(rz_task, 1)
                    if not first(i, 3):
                        pe.wait_ge(pre, n_free.reg)
                        n_free.up()
                    for part, (w, src) in enumerate(((m.whh, m.hT), (m.wih, m.acc1))):
                        for c in range(2):
                            col = slice((4 + c) * P, (5 + c) * P)
                            for f in range(2):
                                mm = pe.matmul(m.ps[:, NN, (2 * part + c) * P:(2 * part + c + 1) * P], w[:, f, col],
                                               src[:, f, at(i - 2)], start=(f == 0), stop=(f == 1))
                    mm.then_inc(n_task, 1)
                if sweep:
                    s.sums(pe, 3)
            turns(pe, turn, 5)

        @block.scalar
        def _(act):
            rz, ht, pr, hidden_in, hfree, gfree = (Level(act, "c_a" + n, k) for n, k in (
                ("rz", 1), ("ht", 1), ("pr", 1), ("hid", 1), ("hfree", 1), ("gfree", 3)))
            act.wait_ge(setup, 1)
            act.activation(m.acc1, m.zeros[:, 0:1].rearrange("p (o c) -> p o c", o=1).broadcast_to([P, 3, ACCW1]),
                           ACT.Copy).then_inc(setup, 1)
            act.wait_ge(brz_ready, 1)

            def turn(i, stages):
                sweep, cell, back, norm, hid, logit = stages
                if hid:
                    act.wait_ge(h_turned, ht.reg)
                    ht.up()
                    act.activation(tT, m.ps[:, REL, 0:D].rearrange("p (c n) -> p c n", c=2), ACT.Copy
                                   ).then_inc(evacuated, 1)
                if logit:
                    act.wait_ge(logit_task, hfree.reg)
                    hfree.up()
                    act.activation(m.lt[0:NE1, :], m.ps[0:NE1, TURN, 2 * P:3 * P], ACT.Copy).then_inc(lt_done, 1)
                if hid:
                    act.activation(m.h[:, one(i - 5), :], hn.rearrange("p (o d) -> p o d", o=1), ACT.Copy
                                   ).then_inc(kept, 1)
                if hid:
                    for half in range(2):
                        act.wait_ge(hid_task, hidden_in.reg)
                        hidden_in.up()
                        for k in range(4 * half, 4 * half + 4):
                            ins = act.activation(m.H0[:, k, :], m.ps[:, HIDA + half, (k % 4) * P:(k % 4 + 1) * P],
                                                 ACT.Gelu, bias=m.bf1[:, k:k + 1])
                        ins.then_inc(gelued, 1)
                if cell:
                    if not first(i, 3):
                        act.wait_ge(mix_step, gfree.reg)
                        gfree.up(3)
                    act.wait_ge(rz_task, rz.reg)
                    rz.up()
                    for gate in range(2):
                        for c in range(2):
                            k = 2 * gate + c
                            ins = act.activation(m.rz[:, gate, c, :], m.ps[:, RZ, k * P:(k + 1) * P], ACT.Tanh,
                                                 bias=m.brz[:, k:k + 1], scale=0.5)
                    ins.then_inc(rz_read, 1)
                if cell:
                    act.wait_ge(pre, pr.reg)
                    pr.up()
                    for c in range(2):
                        ins = act.activation(m.gn[:, c, :], m.gt[:, c, :], ACT.Tanh, bias=m.bih[:, 4 + c:5 + c])
                    ins.then_inc(tanhed, 1)
            turns(act, turn, 5)

        @block.vector
        def _(v):
            v.wait_ge(s.edges_in, 32)
            v.tensor_copy(m.dst[:, :], m.key[:, :].bitcast(I32)).then_inc(red, 1)
            v.tensor_copy(m.type[:, :], s.valid.bitcast(I32)).then_inc(red, 1)
            s.start_windows(v)
            v.wait_ge(red, 2)
            v.wait_ge(setup, 2)
            s.walk_windows(v)
            s.keys(v, walk=False)
            v.wait_ge(loaded, 16 * len(loads))
            v.tensor_tensor(m.brz, m.bih[:, 0:4], m.bhh[:, 0:4], ALU.add).then_inc(gate_step, 1)
            v.wait_ge(gate_step, 1)
            v.tensor_scalar(m.brz, m.brz, 0.5, None, ALU.mult).then_inc(brz_ready, 1)
            (xt, xs, lg, rl, rzr, nt, gs, th, ms, root, kp) = (Level(v, "c_v" + n, k) for n, k in (
                ("xt", 1), ("xs", 1), ("lg", 1), ("rl", 1), ("rzr", 1), ("nt", 1), ("gs", 2), ("th", 1),
                ("ms", 1), ("root", 1), ("kp", 1)))

            def turn(i, stages):
                sweep, cell, back, norm, hid, logit = stages
                more = sweep and not (isinstance(i, int) and i == NIT - 1)
                if sweep:
                    low, high = s.starts(v, i, 0), s.starts(v, i, 1)
                if sweep:
                    s.add(v, 0, low)
                if cell:
                    acc = m.acc1[:, 0:2, at(i - 2)]
                    v.wait_ge(rel_task, rl.reg)
                    rl.up()
                    v.tensor_tensor(acc, acc, m.ps[:, REL, D:2 * D].rearrange("p (c n) -> p c n", c=2), ALU.add
                                    ).then_inc(red, 1)
                if logit:
                    v.wait_ge(lb_task, lg.reg)
                    lg.up()
                    v.tensor_tensor(m.logit1[:, one(i - 6), :], m.ps[:, TURN, 3 * P:3 * P + NE1].rearrange(
                        "p (o e) -> p o e", o=1), m.bg.rearrange("p (o e) -> p o e", o=1), ALU.add
                        ).then_inc(logit_read, 1)
                if sweep:
                    s.add(v, 1, low)
                if more:
                    s.one_hots(v, i + 1, 0)
                if back:
                    xb = m.x[:, one(i - 3), :]
                    v.wait_ge(x_turned, xt.reg)
                    xt.up()
                    v.tensor_tensor(xb, xb, m.ps[:, TURN, 0:D].rearrange("p (o d) -> p o d", o=1), ALU.add
                                    ).then_inc(x_step, 1)
                if norm:
                    if not first(i, 5):
                        v.wait_ge(kept, kp.reg)
                        kp.up()
                    v.wait_ge(rooted, root.reg)
                    root.up()
                    v.tensor_scalar(hn.rearrange("p (o d) -> p o d", o=1), m.x[:, one(i - 4), :], mv[:, 0:1], rstd,
                                    ALU.subtract, ALU.mult).then_inc(normed, 1)
                if back:
                    v.wait_ge(x_step, xs.reg)
                    xs.up()
                    v.bn_stats(stats, xb.rearrange("p o d -> p (o d)")).then_inc(x_step, 1)
                    v.wait_ge(x_step, xs.reg)
                    xs.up()
                    v.bn_aggr(mv, stats).then_inc(x_step, 1)
                    v.wait_ge(x_step, xs.reg)
                    xs.up()
                    v.tensor_scalar(mv[:, 1:2], mv[:, 1:2], EPS, None, ALU.add).then_inc(varied, 1)
                if sweep:
                    s.add(v, 2, high)
                if cell:
                    v.wait_ge(rz_read, rzr.reg)
                    rzr.up()
                    v.tensor_scalar(m.rz, m.rz, 0.5, 0.5, ALU.mult, ALU.add).then_inc(gate_step, 1)
                    v.wait_ge(n_task, nt.reg)
                    nt.up()
                    for c in range(2):
                        v.wait_ge(gate_step, gs.reg)
                        gs.up()
                        v.scalar_tensor_tensor(out=m.gt[:, c, :], in0=m.ps[:, NN, c * P:(c + 1) * P],
                                               scalar=m.bhh[:, 4 + c:5 + c], in1=m.rz[:, 0, c, :], op0=ALU.add,
                                               op1=ALU.mult).then_inc(gate_step, 1)
                    v.wait_ge(gate_step, gs.reg)
                    gs.up()
                    v.tensor_tensor(m.gt, m.gt, m.ps[:, NN, 2 * P:4 * P].rearrange("p (c n) -> p c n", c=2), ALU.add
                                    ).then_inc(pre, 1)
                if sweep:
                    s.add(v, 3, high)
                if more:
                    s.one_hots(v, i + 1, 2)
                if cell:
                    v.wait_ge(tanhed, th.reg)
                    th.up()
                    v.tensor_tensor(m.gt, m.hT[:, :, at(i - 2)], m.gn, ALU.subtract).then_inc(mix_step, 1)
                    v.wait_ge(mix_step, ms.reg)
                    ms.up()
                    v.tensor_tensor(m.gt, m.gt, m.rz[:, 1, :, :], ALU.mult).then_inc(mix_step, 1)
                    v.wait_ge(mix_step, ms.reg)
                    ms.up()
                    v.tensor_tensor(m.gn, m.gn, m.gt, ALU.add).then_inc(mix_step, 1)
                    ms.up()
            for k in (0, 2):
                s.one_hots(v, 0, k)
            turns(v, turn, 5, tail=1)


def route(nc, ctx, m, io):
    def sem(name):
        return ctx.enter_context(nc.semaphore("rt_" + name))

    v_step, a_step, p_step, counted, placed, sent = (
        sem(s) for s in ("v_step", "a_step", "p_step", "counted", "placed", "sent"))

    def per_block(c, e=NE1):
        return c.rearrange("p (b o) -> p b o", o=1).broadcast_to([P, NB, e])

    def per_expert(r, n):
        return r.rearrange("p (o e) -> p o e", o=1).broadcast_to([P, n, NE1])
    with nc.Block() as block:
        @block.vector
        def _(v):
            count = [0]

            def link(ins):
                count[0] += 1
                ins.then_inc(v_step, 1)
                v.wait_ge(v_step, count[0])

            link(v.tensor_reduce(m.col1, m.logit1, AX.X, ALU.max))
            link(v.tensor_tensor(m.tmp1, m.logit1, per_block(m.col1), ALU.subtract))
            v.wait_ge(a_step, 1)
            link(v.tensor_reduce(m.col1, m.prob1, AX.X, ALU.add))
            link(v.reciprocal(m.col1, m.col1))
            link(v.tensor_tensor(m.prob1, m.prob1, per_block(m.col1), ALU.mult))
            link(v.tensor_reduce(m.best, m.prob1, AX.X, ALU.max))
            link(v.tensor_tensor(m.tmp1, m.prob1, per_block(m.best), ALU.is_lt))
            link(v.scalar_tensor_tensor(out=m.tmp1, in0=m.tmp1, scalar=float(4 * NE1),
                                        in1=per_expert(m.iota[:, 0:NE1], NB), op0=ALU.mult, op1=ALU.add))
            link(v.tensor_reduce(m.col1, m.tmp1, AX.X, ALU.min))
            link(v.tensor_tensor(m.pick, per_expert(m.iota[:, 0:NE1], NB), per_block(m.col1), ALU.is_equal))
            v.wait_ge(p_step, 4)
            last = m.pick[:, NB - 1, :]
            link(v.tensor_tensor(last, last, m.padmask, ALU.mult))
            v.wait_ge(counted, 1)
            link(v.tensor_copy(m.tot, m.ps[:, 1, 0:NB * NE1].rearrange("p (b e) -> p e b", e=NE1)))
            for e in range(NE1):
                link(v.tensor_tensor_scan(out=m.cum[:, e, :], data0=m.ones[:, 0:NB], data1=m.tot[:, e, :],
                                          initial=0.0, op0=ALU.mult, op1=ALU.add))
            steps = m.steps.rearrange("p (o k) -> p o k", o=1).broadcast_to([P, NE1, NB])
            link(v.tensor_scalar(m.steps, m.iota[:, 0:NB], float(P), None, ALU.mult))
            t = m.tmp1.rearrange("p b e -> p (b e)").rearrange("p (e k) -> p e k", k=NB)
            link(v.tensor_tensor(t, m.cum[:, :, NB - 1:NB].broadcast_to([P, NE1, NB]), steps, ALU.is_gt))
            link(v.tensor_reduce(m.ntiles, t, AX.X, ALU.add))
            link(v.tensor_tensor_scan(out=m.ends, data0=m.ones[:, 0:NE1], data1=m.ntiles, initial=0.0,
                                      op0=ALU.mult, op1=ALU.add))
            link(v.tensor_tensor(m.starts, m.ends, m.ntiles, ALU.subtract))
            link(v.tensor_tensor(m.tmp2, m.iota[:, 0:TILES].rearrange("p (t o) -> p t o", o=1
                                                                      ).broadcast_to([P, TILES, NE1]),
                                 per_expert(m.ends, TILES), ALU.is_ge))
            link(v.tensor_reduce(m.ofTf, m.tmp2, AX.X, ALU.add))
            link(v.tensor_scalar(m.ofTf, m.ofTf, float(NE1 - 1), None, ALU.min))
            link(v.tensor_copy(m.ofT, m.ofTf))
            link(v.tensor_scalar(m.starts, m.starts, float(P), None, ALU.mult))
            link(v.tensor_tensor(m.cum, m.cum, m.tot, ALU.subtract))
            link(v.tensor_tensor(m.before, m.ps[:, 0, 0:NB * NE1].rearrange("p (b e) -> p b e", e=NE1),
                                 m.cum.rearrange("p e b -> p b e"), ALU.add))
            link(v.tensor_tensor(m.before, m.before, per_expert(m.starts, NB), ALU.add))
            link(v.tensor_tensor(m.before, m.before, m.pick, ALU.mult))
            link(v.tensor_reduce(m.posf, m.before, AX.X, ALU.add))
            v.tensor_copy(m.slot_of, m.posf).then_inc(placed, 1)

        @block.scalar
        def _(act):
            act.wait_ge(v_step, 2)
            act.activation(m.prob1, m.tmp1, ACT.Exp).then_inc(a_step, 1)

        @block.tensor
        def _(pe):
            pe.wait_ge(v_step, 11)
            pick = m.pick.rearrange("p b e -> p (b e)")
            pe.matmul(m.ps[:, 0, 0:NB * NE1], m.tri, pick, start=True, stop=True)
            pe.matmul(m.ps[:, 1, 0:NB * NE1], m.ones[:, :], pick, start=True, stop=True).then_inc(counted, 1)

        @block.gpsimd
        def _(g):
            g.memset(m.tri, 1.0).then_inc(p_step, 1)
            g.memset(m.padmask, 1.0).then_inc(p_step, 1)
            g.wait_ge(p_step, 2)
            g.affine_select(out=m.tri, in_=m.tri, compare_op=ALU.is_gt, fill=0.0, base=0, pattern=[[1, P]],
                            channel_multiplier=-1).then_inc(p_step, 1)
            g.affine_select(out=m.padmask, in_=m.padmask, compare_op=ALU.is_ge, fill=0.0, base=NTAIL - 1,
                            pattern=[[0, NE1]], channel_multiplier=-1).then_inc(p_step, 1)
            g.wait_ge(placed, 1)
            for b in range(NB):
                n = P if b < NB - 1 else NTAIL
                g.indirect_dma_start(io["slots_in"], bass.IndirectOffsetOnAxis(ap=m.slot_of[0:n, b:b + 1], axis=0),
                                     m.h[0:n, b, :], None).then_inc(sent, 16)
            g.wait_ge(sent, 16 * NB)


def experts(nc, ctx, m, io):
    def sem(name):
        return ctx.enter_context(nc.semaphore("ex_" + name))

    loaded = [sem("loaded0"), sem("loaded1")]
    stored = [sem("stored0"), sem("stored1")]
    turned, evacuated, task, gelued, product, read = (
        sem(s) for s in ("turned", "evacuated", "task", "gelued", "product", "read"))
    Q = TILES // 4
    with nc.Block() as block:
        @block.sync
        def _(sp):
            def rows(t, q):
                return t[bass.ds(q * 4 * P, 4 * P), :].rearrange("(i p) d -> p i d", p=P)
            for i in range(2):
                sp.dma_start(m.slots[i], rows(io["slots_in"], i)).then_inc(loaded[i], 16)
            for q in range(Q):
                i = q % 2
                sp.wait_ge(read, 4 * (q + 1))
                sp.dma_start(rows(io["slots_out"], q), m.results[i]).then_inc(stored[i], 16)
                if q + 2 < Q:
                    sp.wait_ge(turned, q + 1)
                    sp.dma_start(m.slots[i], rows(io["slots_in"], q + 2)).then_inc(loaded[i], 16)
            for i in range(2):
                sp.wait_ge(stored[i], 16 * Q // 2)

        @block.tensor
        def _(pe):
            pe.wait_ge(m.wd_in, 16 * (NE1 + 1))
            landed, hts, free, hid, ofree = (Level(pe, "ex_" + s) for s in ("landed", "hts", "free", "hid", "ofree"))

            def turn(i):
                if i == 0:
                    landed.up(16)
                pe.wait_ge(loaded[i], landed.reg)
                for c in range(2):
                    for t in range(4):
                        mm = pe.transpose(m.ps[:, c, t * P:(t + 1) * P], m.slots[i][:, t, c * P:(c + 1) * P],
                                          m.ident[:, :])
                mm.then_inc(turned, 1)

            def quad(q, i, first=False, last=False):
                e = [pe.value_load(m.ofT[0:1, bass.ds(q * 4 + t, 1)], min_val=0, max_val=NE1 - 1) for t in range(4)]
                pe.wait_ge(evacuated, hts.up())
                for k in range(MH):
                    if not (first and k < 4):
                        pe.wait_ge(gelued, free.up())
                    for c in range(2):
                        mm = pe.matmul(m.ps[:, 2 + k % 4, :], m.W1[:, c, k * P:(k + 1) * P], m.hTQ[i][:, c, :],
                                       start=(c == 0), stop=(c == 1))
                    mm.then_inc(task, 1)
                if not last:
                    turn(1 - i)
                pe.wait_ge(gelued, hid.up(MH))
                for t in range(4):
                    if not (first and t < 2):
                        pe.wait_ge(read, ofree.up())
                    for k in range(MH):
                        mm = pe.matmul(m.ps[:, 6 + t % 2, 0:D], m.HQ[i][:, k, t * P:(t + 1) * P],
                                       m.Wd[:, one(e[t]), k, :], start=(k == 0), stop=(k == MH - 1))
                    mm.then_inc(product, 1)
            turn(0)
            quad(0, 0, first=True)
            quad(1, 1)
            with pe.Fori(1, Q // 2 - 1) as q2:
                for i in range(2):
                    quad(q2 * 2 + i, i)
            quad(Q - 2, 0)
            quad(Q - 1, 1, last=True)

        @block.scalar
        def _(act):
            ready, free = Level(act, "ex_ready"), Level(act, "ex_hfree")

            def quad(i, first):
                if not first:
                    act.wait_ge(product, free.up(4))
                for k in range(MH):
                    act.wait_ge(task, ready.up())
                    act.activation(m.HQ[i][:, k, :], m.ps[:, 2 + k % 4, :], ACT.Gelu, bias=m.bf1[:, k:k + 1]
                                   ).then_inc(gelued, 1)
            for i in range(2):
                quad(i, True)
            with act.Fori(1, Q // 2):
                for i in range(2):
                    quad(i, False)

        @block.vector
        def _(v):
            v.wait_ge(m.wd_in, 16 * (NE1 + 1))
            turn, prod, store = Level(v, "ex_turn"), Level(v, "ex_prod"), Level(v, "ex_store")

            def evacuate(i):
                v.wait_ge(turned, turn.up())
                for c in range(2):
                    ins = v.tensor_copy(m.hTQ[i][:, c, :], m.ps[:, c, :])
                ins.then_inc(evacuated, 1)

            def quad(q, i, first=False, last=False):
                if not last:
                    evacuate(1 - i)
                for t in range(4):
                    e = v.value_load(m.ofT[0:1, bass.ds(q * 4 + t, 1)], min_val=0, max_val=NE1 - 1)
                    if t == 0 and not first:
                        if i == 0:
                            store.up(16)
                        v.wait_ge(stored[i], store.reg)
                    v.wait_ge(product, prod.up())
                    v.tensor_tensor(m.results[i][:, t, :].rearrange("p (o d) -> p o d", o=1),
                                    m.ps[:, 6 + t % 2, 0:D].rearrange("p (o d) -> p o d", o=1),
                                    m.bd[:, one(e), :], ALU.add).then_inc(read, 1)
            evacuate(0)
            quad(0, 0, first=True)
            quad(1, 1, first=True)
            with v.Fori(1, Q // 2 - 1) as q2:
                for i in range(2):
                    quad(q2 * 2 + i, i)
            quad(Q - 2, 0)
            quad(Q - 1, 1, last=True)


def finish(nc, ctx, m, io):
    def sem(name):
        return ctx.enter_context(nc.semaphore("fin_" + name))

    chunks = [(g * GB, (g + 1) * GB) for g in range(NG - 1)] + [((NG - 1) * GB, NB - 3), (NB - 3, NB - 1), (NB - 1, NB)]
    fetched = [sem(f"fetched{k}") for k in range(len(chunks))]
    done, stored = sem("done"), sem("stored")

    def size(b):
        return P if b < NB - 1 else NTAIL
    with nc.Block() as block:
        @block.gpsimd
        def _(g):
            for k, (lo, hi) in enumerate(chunks):
                for b in range(lo, hi):
                    n = size(b)
                    g.indirect_dma_start(m.h[0:n, b, :], None, io["slots_out"],
                                         bass.IndirectOffsetOnAxis(ap=m.slot_of[0:n, b:b + 1], axis=0)
                                         ).then_inc(fetched[k], 16)

        @block.vector
        def _(v):
            for k, (lo, hi) in enumerate(chunks):
                v.wait_ge(fetched[k], 16 * (hi - lo))
                for b in range(lo, hi):
                    n = size(b)
                    v.scalar_tensor_tensor(out=m.x[0:n, b, :], in0=m.h[0:n, b, :], scalar=m.best[0:n, b:b + 1],
                                           in1=m.x[0:n, b, :], op0=ALU.mult, op1=ALU.add).then_inc(done, 1)

        @block.sync
        def _(sp):
            for lo, hi in chunks[:-1]:
                sp.wait_ge(done, hi)
                sp.dma_start(io["out"][lo * P:hi * P, :].rearrange("(b p) d -> p b d", p=P), m.x[:, lo:hi, :]
                             ).then_inc(stored, 16)
            sp.wait_ge(done, NB)
            sp.dma_start(io["out"][(NB - 1) * P:N, :], m.x[0:NTAIL, NB - 1, :]).then_inc(stored, 16)
            sp.wait_ge(stored, 16 * len(chunks))


def program(nc, io):
    with ExitStack() as ctx:
        m = allocate(nc, ctx)
        m.wd_in = ctx.enter_context(nc.semaphore("wd_in"))
        for stage in (prepare, factors, layer0, layer1, route, experts, finish):
            stage(nc, ctx, m, io)


def kernel(**inputs):
    import numpy as np
    import concourse.bacc as bacc
    from concourse.bass_utils import run_bass_kernel_spmd as run

    a = {k: np.asarray(v) for k, v in inputs.items()}

    def tiles(e):
        return e.reshape(ET, EP).T

    def columns(b):
        return b.reshape(-1, P).T
    host = {
        "x": a["x"], "dst_groups": a["dst"].reshape(NSG, SG * EP),
        "src": tiles(a["src"]), "dst": tiles(a["dst"]), "t8": tiles(a["edge_type_8"]),
        "t16": tiles(a["edge_type_16"]),
        "basis": a["L0_gnn_basis"].reshape(R8 * P, D), "w_comp": a["L0_gnn_w_comp"], "gnn_bias": a["L0_gnn_bias"],
        "sW1": a["L0_ffn_sW1"], "sW2": a["L0_ffn_sW2"], "sW3": a["L0_ffn_sW3"], "sb3": a["L0_ffn_sb3"],
        "eW1": a["L0_ffn_eW1"], "eW2": a["L0_ffn_eW2"], "eW3q": a["L0_ffn_eW3"].reshape(2, P, D), "eb3": a["L0_ffn_eb3"],
        "b1T": np.concatenate([columns(a["L0_ffn_sb1"]), columns(a["L0_ffn_eb1"])], 1),
        "b2T": np.concatenate([columns(a["L0_ffn_sb2"]), columns(a["L0_ffn_eb2"])], 1),
        "gW": a["L0_ffn_gW"], "gb": a["L0_ffn_gb"],
        "rel": a["L1_gnn_relvectors"], "w_ihT": a["L1_gnn_w_ih"].T, "w_hhT": a["L1_gnn_w_hh"].T,
        "b_ihT": columns(a["L1_gnn_b_ih"]), "b_hhT": columns(a["L1_gnn_b_hh"]),
        "W1": a["L1_ffn_W1"], "bf1T": columns(a["L1_ffn_b1"]), "Wg": a["L1_ffn_Wg"], "bg": a["L1_ffn_bg"],
        "Wd": a["L1_ffn_Wd"], "bd": a["L1_ffn_bd"],
    }
    host = {k: np.ascontiguousarray(v) for k, v in host.items()}
    nc = bacc.Bacc("TRN2", target_bir_lowering=False, num_devices=1)
    io = {k: nc.dram_tensor("in_" + k, v.shape, mybir.dt.from_np(v.dtype), kind="ExternalInput").ap()
          for k, v in host.items()}
    io["out"] = nc.dram_tensor("out_x", (N, D), F32, kind="ExternalOutput").ap()
    for name, shape in (("g_table", (NP, P)), ("h_table", (NP, D)), ("slots_in", (SLOTS, D)),
                        ("slots_out", (SLOTS, D))):
        io[name] = nc.dram_tensor(name, shape, F32).ap()
    program(nc, io)
    r = run(nc, [{"in_" + k: v for k, v in host.items()}], core_ids=[0])
    return r.results[0]["out_x"]
```
